# Optimizing a Trainium2 kernel written in Bass

```python
import numpy as np
import jax
import jax.numpy as jnp

def _softmax(x, axis=-1):
    return jax.nn.softmax(x, axis=axis)

def _gelu(x):
    return jax.nn.gelu(x, approximate=True)

def _silu(x):
    return jax.nn.silu(x)

def _sigmoid(x):
    return jax.nn.sigmoid(x)

def _layernorm(x, axis=-1, eps=1e-05):
    m = jnp.mean(x, axis=axis, keepdims=True)
    v = jnp.var(x, axis=axis, keepdims=True)
    return (x - m) / jnp.sqrt(v + eps)

def _scatter_add(tgt, idx, src, axis=0):
    return tgt.at[idx].add(src)

def _segment_sum(src, seg, n):
    return jax.ops.segment_sum(src, seg, n)
kernel_name = 'mk_adaln_ffn_d2_seqx_r4_dbcf5b'

def setup_inputs(seed: int=0):
    np.random.seed(seed)
    _w = jnp.asarray

    def _rec_inputs():
        import jax
        import jax.numpy as jnp
        _rk = jax.random.key(seed)
        x = -7.109e-05 + 0.9999 * jax.random.normal(jax.random.fold_in(_rk, 1), (8, 512, 256), jnp.float32)
        _lenS = 512 - jax.random.randint(jax.random.fold_in(_rk, 7), (8,), 0, max(1, 512 // 4) + 1, jnp.int32)
        _lenS2 = 512 - jax.random.randint(jax.random.fold_in(_rk, 8), (8,), 0, max(1, 512 // 4) + 1, jnp.int32)
        itok_B_0_8 = jax.random.randint(jax.random.fold_in(_rk, 11), (8,), 0, 9, jnp.int32)
        condB_tauraws = -5.74692 + 0.777674 * jax.random.normal(jax.random.fold_in(_rk, 12), (8,), jnp.float32)
        cond_256 = -0.000235209 + 0.019331 * jax.random.normal(jax.random.fold_in(_rk, 13), (8, 64), jnp.float32)
        condB_bn2 = jnp.zeros((8,), jnp.float32)
        cond_1024 = -4.10585e-05 + 0.0199478 * jax.random.normal(jax.random.fold_in(_rk, 15), (8, 256), jnp.float32)
        return (x, itok_B_0_8, condB_tauraws, cond_256, condB_bn2, cond_1024)
    x, itok_B_0_8, condB_tauraws, cond_256, condB_bn2, cond_1024 = _rec_inputs()

    def _L0_cond_setup():
        import jax, jax.numpy as jnp
        import numpy as np
        LN_EPS = 1e-05
        key = jax.random.key(seed)
        ks = jax.random.split(key, 8)
        B, S, H, A, L = (32, 512, 256, 64, 10)
        return {'hidden_states': jax.random.normal(ks[0], (B, S, H), dtype=jnp.float32), 'language_ids': jax.random.randint(ks[1], (B,), 0, L, dtype=jnp.int64), 'W1': jax.random.normal(ks[2], (L, H, A), dtype=jnp.float32) * (1.0 / np.sqrt(H)), 'b1': jnp.zeros((L, A), dtype=jnp.float32), 'W2': jax.random.normal(ks[3], (L, A, H), dtype=jnp.float32) * (1.0 / np.sqrt(A)), 'b2': jnp.zeros((L, H), dtype=jnp.float32), 'gamma': jnp.ones((L, H), dtype=jnp.float32), 'beta': jnp.zeros((L, H), dtype=jnp.float32)}
    _L0_cond_all = _L0_cond_setup()
    _L0_cond_in = {k: v for k, v in _L0_cond_all.items() if k in ('W1', 'b1', 'W2', 'b2', 'gamma', 'beta')}
    del _L0_cond_all

    def _L0_ffn_setup():
        import jax, jax.numpy as jnp
        import numpy as np
        B, S, H, E, K, F = (4, 512, 256, 8, 128, 1024)
        key = jax.random.key(seed)
        k0, k1, k2, k3 = jax.random.split(key, 4)
        sc = lambda d: 1.0 / np.sqrt(d).astype(np.float32)
        return {'x': jax.random.normal(k0, (B, S, H), jnp.float32), 'Wg': jax.random.normal(k1, (E, H), jnp.float32) * sc(H), 'W1': jax.random.normal(k2, (E, H, F), jnp.float32) * sc(H), 'b1': jnp.zeros((E, F), jnp.float32), 'W2': jax.random.normal(k3, (E, F, H), jnp.float32) * sc(F), 'b2': jnp.zeros((E, H), jnp.float32)}
    _L0_ffn_all = _L0_ffn_setup()
    _L0_ffn_in = {k: v for k, v in _L0_ffn_all.items() if k in ('Wg', 'W1', 'b1', 'W2', 'b2')}
    del _L0_ffn_all

    def _L1_cond_setup():
        import jax, jax.numpy as jnp
        import numpy as np
        import math
        B, T, E, D = (4, 512, 256, 4)

        def _tau_init(t):
            a = 0.1 ** (1.0 / max(t - 1, 1))
            tt = -math.log(max(a, 1e-10))
            return math.log(math.exp(tt) - 1 + 1e-10)

        def causal_ema(b, tau_raw):
            alpha = jnp.exp(-jax.nn.softplus(tau_raw)).astype(b.dtype)

            def step(h, bt):
                h = alpha * h + bt
                return (h, h)
            h0 = jnp.zeros((b.shape[0], b.shape[2]), b.dtype)
            _, hs = jax.lax.scan(step, h0, jnp.swapaxes(b, 0, 1))
            return jnp.swapaxes(hs, 0, 1)
        key = jax.random.key(seed)
        ks = jax.random.split(key, 10)
        s = 0.02
        return {'x': jax.random.normal(ks[0], (B, T, E), jnp.float32), 'tau_ctx': jnp.float32(_tau_init(max(T // 2, 4))), 'tau_raws': jnp.array([_tau_init(max(T // 2 ** i, 2)) for i in range(D)], jnp.float32), 'Wg': jax.random.normal(ks[1], (E, 2 * E), jnp.float32) * s, 'bg': jnp.full((E,), -0.5, jnp.float32), 'Wn1': jax.random.normal(ks[2], (E // 4, E), jnp.float32) * s, 'bn1': jnp.zeros((E // 4,), jnp.float32), 'Wn2': jax.random.normal(ks[3], (D, E // 4), jnp.float32) * s, 'bn2': jnp.zeros((D,), jnp.float32), 'blend': jax.random.normal(ks[4], (D, E), jnp.float32) * s, 'Wsoma': jax.random.normal(ks[5], (E, E), jnp.float32) * s, 'bsoma': jnp.zeros((E,), jnp.float32), 'Wtemp': jax.random.normal(ks[6], (E, E), jnp.float32) * s, 'btemp': jnp.zeros((E,), jnp.float32), 'Wout': jax.random.normal(ks[7], (E, E), jnp.float32) * s, 'gamma': jnp.ones((E,), jnp.float32), 'beta': jnp.zeros((E,), jnp.float32)}
    _L1_cond_all = _L1_cond_setup()
    _L1_cond_in = {k: v for k, v in _L1_cond_all.items() if k in ('tau_ctx', 'Wg', 'bg', 'Wn1', 'bn1', 'Wsoma', 'bsoma', 'Wtemp', 'btemp', 'Wout', 'gamma', 'beta')}
    del _L1_cond_all

    def _L1_ffn_setup():
        import jax, jax.numpy as jnp
        import numpy as np
        B, S, D = (1, 512, 256)
        E, K, F = (64, 8, 192)
        SF = 192
        C = 128
        ROUTED_SCALE = 1.0

        def _moe_forward(x, router_w, w_gate, w_up, w_down, ws_gate_up, ws_down):
            T = x.shape[0]
            logits = x.astype(jnp.float32) @ router_w.T
            probs = jax.nn.softmax(logits, axis=-1)
            topk_w, topk_ids = jax.lax.top_k(probs, K)
            topk_w = topk_w / jnp.sum(topk_w, axis=-1, keepdims=True)
            topk_w = topk_w.astype(x.dtype)
            N = T * K
            flat_e = topk_ids.reshape(-1)
            flat_w = topk_w.reshape(-1)
            tok = jnp.arange(N) // K
            onehot = flat_e[:, None] == jnp.arange(E)[None, :]
            pos = jnp.cumsum(onehot, axis=0)[jnp.arange(N), flat_e] - 1
            valid = pos < C
            idx = jnp.where(valid, flat_e * C + pos, E * C)
            x_buf = jnp.zeros((E * C + 1, x.shape[1]), x.dtype).at[idx].set(x[tok])
            xb = x_buf[:E * C].reshape(E, C, -1)
            g = jnp.einsum('ecd,edf->ecf', xb, w_gate)
            u = jnp.einsum('ecd,edf->ecf', xb, w_up)
            h = jax.nn.silu(g) * u
            y = jnp.einsum('ecf,efd->ecd', h, w_down).reshape(E * C, -1)
            safe = jnp.where(valid, idx, 0)
            contrib = y[safe] * (flat_w * valid.astype(flat_w.dtype))[:, None]
            routed = jax.ops.segment_sum(contrib, tok, num_segments=T)
            routed = routed * ROUTED_SCALE
            gu = x @ ws_gate_up
            sg, su = (gu[:, :SF], gu[:, SF:])
            shared = jax.nn.silu(sg) * su @ ws_down
            return routed + shared
        key = jax.random.key(seed)
        ks = jax.random.split(key, 7)
        w = 0.02
        return {'hidden_states': jax.random.normal(ks[0], (B, S, D), jnp.float32), 'router_w': jax.random.normal(ks[1], (E, D), jnp.float32) * w, 'w_gate': jax.random.normal(ks[2], (E, D, F), jnp.float32) * w, 'w_up': jax.random.normal(ks[3], (E, D, F), jnp.float32) * w, 'w_down': jax.random.normal(ks[4], (E, F, D), jnp.float32) * w, 'ws_gate_up': jax.random.normal(ks[5], (D, 2 * SF), jnp.float32) * w, 'ws_down': jax.random.normal(ks[6], (SF, D), jnp.float32) * w}
    _L1_ffn_all = _L1_ffn_setup()
    _L1_ffn_in = {k: v for k, v in _L1_ffn_all.items() if k in ('router_w', 'w_gate', 'w_up', 'w_down', 'ws_gate_up', 'ws_down')}
    del _L1_ffn_all
    return {'x': x, 'itok_B_0_8': itok_B_0_8, 'condB_tauraws': condB_tauraws, 'cond_256': cond_256, 'condB_bn2': condB_bn2, 'cond_1024': cond_1024, 'L0_cond_W1': _L0_cond_in['W1'], 'L0_cond_b1': _L0_cond_in['b1'], 'L0_cond_W2': _L0_cond_in['W2'], 'L0_cond_b2': _L0_cond_in['b2'], 'L0_cond_gamma': _L0_cond_in['gamma'], 'L0_cond_beta': _L0_cond_in['beta'], 'L0_ffn_Wg': _L0_ffn_in['Wg'], 'L0_ffn_W1': _L0_ffn_in['W1'], 'L0_ffn_b1': _L0_ffn_in['b1'], 'L0_ffn_W2': _L0_ffn_in['W2'], 'L0_ffn_b2': _L0_ffn_in['b2'], 'L1_cond_tau_ctx': _L1_cond_in['tau_ctx'], 'L1_cond_Wg': _L1_cond_in['Wg'], 'L1_cond_bg': _L1_cond_in['bg'], 'L1_cond_Wn1': _L1_cond_in['Wn1'], 'L1_cond_bn1': _L1_cond_in['bn1'], 'L1_cond_Wsoma': _L1_cond_in['Wsoma'], 'L1_cond_bsoma': _L1_cond_in['bsoma'], 'L1_cond_Wtemp': _L1_cond_in['Wtemp'], 'L1_cond_btemp': _L1_cond_in['btemp'], 'L1_cond_Wout': _L1_cond_in['Wout'], 'L1_cond_gamma': _L1_cond_in['gamma'], 'L1_cond_beta': _L1_cond_in['beta'], 'L1_ffn_router_w': _L1_ffn_in['router_w'], 'L1_ffn_w_gate': _L1_ffn_in['w_gate'], 'L1_ffn_w_up': _L1_ffn_in['w_up'], 'L1_ffn_w_down': _L1_ffn_in['w_down'], 'L1_ffn_ws_gate_up': _L1_ffn_in['ws_gate_up'], 'L1_ffn_ws_down': _L1_ffn_in['ws_down']}

def reference(x, itok_B_0_8, condB_tauraws, cond_256, condB_bn2, cond_1024, L0_cond_W1, L0_cond_b1, L0_cond_W2, L0_cond_b2, L0_cond_gamma, L0_cond_beta, L0_ffn_Wg, L0_ffn_W1, L0_ffn_b1, L0_ffn_W2, L0_ffn_b2, L1_cond_tau_ctx, L1_cond_Wg, L1_cond_bg, L1_cond_Wn1, L1_cond_bn1, L1_cond_Wsoma, L1_cond_bsoma, L1_cond_Wtemp, L1_cond_btemp, L1_cond_Wout, L1_cond_gamma, L1_cond_beta, L1_ffn_router_w, L1_ffn_w_gate, L1_ffn_w_up, L1_ffn_w_down, L1_ffn_ws_gate_up, L1_ffn_ws_down):
    import jax
    import jax.numpy as jnp

    def _L0_cond_ref(hidden_states, language_ids, W1, b1, W2, b2, gamma, beta):
        import jax, jax.numpy as jnp
        import numpy as np
        LN_EPS = 1e-05
        w1 = W1[language_ids]
        w2 = W2[language_ids]
        h = jnp.einsum('bsh,bha->bsa', hidden_states, w1) + b1[language_ids][:, None, :]
        h = jax.nn.relu(h)
        adapted = jnp.einsum('bsa,bah->bsh', h, w2) + b2[language_ids][:, None, :]
        x = hidden_states + adapted
        mean = jnp.mean(x, axis=-1, keepdims=True)
        var = jnp.mean(jnp.square(x - mean), axis=-1, keepdims=True)
        normed = (x - mean) * jax.lax.rsqrt(var + LN_EPS)
        return normed * gamma[language_ids][:, None, :] + beta[language_ids][:, None, :]

    def _L0_ffn_ref(x, Wg, W1, b1, W2, b2):
        import jax, jax.numpy as jnp
        import numpy as np
        B, S, H, E, K, F = (4, 512, 256, 8, 128, 1024)
        b, s, h = x.shape
        logits = jnp.einsum('bsh,eh->bse', x, Wg)
        Sm = jnp.swapaxes(jax.nn.softmax(logits, axis=-1), 1, 2)
        G, I = jax.lax.top_k(Sm, K)
        ex = jnp.take_along_axis(x[:, None, :, :], I[..., None], axis=2)
        h1 = jax.nn.gelu(jnp.einsum('bekh,ehf->bekf', ex, W1) + b1[None, :, None, :])
        out = jnp.einsum('bekf,efh->bekh', h1, W2) + b2[None, :, None, :]
        out = G[..., None] * out
        new_x = jnp.zeros_like(x).at[jnp.arange(b)[:, None, None], I].add(out)
        return new_x

    def _L1_cond_ref(x, tau_ctx, tau_raws, Wg, bg, Wn1, bn1, Wn2, bn2, blend, Wsoma, bsoma, Wtemp, btemp, Wout, gamma, beta):
        import jax, jax.numpy as jnp
        import numpy as np
        import math
        B, T, E, D = (4, 512, 256, 4)

        def _tau_init(t):
            a = 0.1 ** (1.0 / max(t - 1, 1))
            tt = -math.log(max(a, 1e-10))
            return math.log(math.exp(tt) - 1 + 1e-10)

        def causal_ema(b, tau_raw):
            alpha = jnp.exp(-jax.nn.softplus(tau_raw)).astype(b.dtype)

            def step(h, bt):
                h = alpha * h + bt
                return (h, h)
            h0 = jnp.zeros((b.shape[0], b.shape[2]), b.dtype)
            _, hs = jax.lax.scan(step, h0, jnp.swapaxes(b, 0, 1))
            return jnp.swapaxes(hs, 0, 1)
        ctx = causal_ema(x, tau_ctx)
        gate_in = jnp.concatenate([x, ctx], axis=-1)
        wg = jax.nn.sigmoid(jnp.einsum('btc,ec->bte', gate_in, Wg) + bg)
        gated = x * wg
        h1 = jax.nn.gelu(jnp.einsum('btc,hc->bth', x, Wn1) + bn1, approximate=False)
        mod = 0.5 + jax.nn.sigmoid(jnp.einsum('bth,dh->btd', h1, Wn2) + bn2)
        traces = jax.vmap(lambda tau, m: causal_ema(gated * m[..., None], tau))(tau_raws, jnp.moveaxis(mod, -1, 0))
        blend_w = jax.nn.softmax(blend, axis=0)
        temporal = jnp.einsum('dbtc,dc->btc', traces, blend_w)
        gate = jax.nn.sigmoid(jnp.einsum('btc,ec->bte', temporal, Wtemp) + btemp)
        soma = jax.nn.gelu(jnp.einsum('btc,ec->bte', x, Wsoma) + bsoma, approximate=False)
        out = jnp.einsum('btc,ec->bte', soma * gate, Wout)
        mu = out.mean(-1, keepdims=True)
        var = out.var(-1, keepdims=True)
        return (out - mu) / jnp.sqrt(var + 1e-05) * gamma + beta

    def _L1_ffn_ref(hidden_states, router_w, w_gate, w_up, w_down, ws_gate_up, ws_down):
        import jax, jax.numpy as jnp
        import numpy as np
        B, S, D = (1, 512, 256)
        E, K, F = (64, 8, 192)
        SF = 192
        C = 128
        ROUTED_SCALE = 1.0

        def _moe_forward(x, router_w, w_gate, w_up, w_down, ws_gate_up, ws_down):
            T = x.shape[0]
            logits = x.astype(jnp.float32) @ router_w.T
            probs = jax.nn.softmax(logits, axis=-1)
            topk_w, topk_ids = jax.lax.top_k(probs, K)
            topk_w = topk_w / jnp.sum(topk_w, axis=-1, keepdims=True)
            topk_w = topk_w.astype(x.dtype)
            N = T * K
            flat_e = topk_ids.reshape(-1)
            flat_w = topk_w.reshape(-1)
            tok = jnp.arange(N) // K
            onehot = flat_e[:, None] == jnp.arange(E)[None, :]
            pos = jnp.cumsum(onehot, axis=0)[jnp.arange(N), flat_e] - 1
            valid = pos < C
            idx = jnp.where(valid, flat_e * C + pos, E * C)
            x_buf = jnp.zeros((E * C + 1, x.shape[1]), x.dtype).at[idx].set(x[tok])
            xb = x_buf[:E * C].reshape(E, C, -1)
            g = jnp.einsum('ecd,edf->ecf', xb, w_gate)
            u = jnp.einsum('ecd,edf->ecf', xb, w_up)
            h = jax.nn.silu(g) * u
            y = jnp.einsum('ecf,efd->ecd', h, w_down).reshape(E * C, -1)
            safe = jnp.where(valid, idx, 0)
            contrib = y[safe] * (flat_w * valid.astype(flat_w.dtype))[:, None]
            routed = jax.ops.segment_sum(contrib, tok, num_segments=T)
            routed = routed * ROUTED_SCALE
            gu = x @ ws_gate_up
            sg, su = (gu[:, :SF], gu[:, SF:])
            shared = jax.nn.silu(sg) * su @ ws_down
            return routed + shared
        b, s, d = hidden_states.shape
        x = hidden_states.reshape(-1, d)
        out = _moe_forward(x, router_w, w_gate, w_up, w_down, ws_gate_up, ws_down)
        return out.reshape(b, s, d)
    x = x + _L0_ffn_ref(_L0_cond_ref(x, itok_B_0_8, L0_cond_W1, L0_cond_b1, L0_cond_W2, L0_cond_b2, L0_cond_gamma, L0_cond_beta), L0_ffn_Wg, L0_ffn_W1, L0_ffn_b1, L0_ffn_W2, L0_ffn_b2)
    x = x + _L1_ffn_ref(_L1_cond_ref(x, L1_cond_tau_ctx, condB_tauraws, L1_cond_Wg, L1_cond_bg, L1_cond_Wn1, L1_cond_bn1, cond_256, condB_bn2, cond_1024, L1_cond_Wsoma, L1_cond_bsoma, L1_cond_Wtemp, L1_cond_btemp, L1_cond_Wout, L1_cond_gamma, L1_cond_beta), L1_ffn_router_w, L1_ffn_w_gate, L1_ffn_w_up, L1_ffn_w_down, L1_ffn_ws_gate_up, L1_ffn_ws_down)
    return x

_drawn_inputs = setup_inputs


def setup_inputs(seed=0):
    import zlib

    import numpy as np

    out = dict(_drawn_inputs(seed))
    spreads = {'condB_bn2': (0.0, 0.8),
     'L0_cond_b1': (0.0, 0.1),
     'L0_cond_b2': (0.0, 0.1),
     'L0_cond_gamma': (1.0, 0.2),
     'L0_cond_beta': (0.0, 0.1),
     'L0_ffn_b1': (0.0, 0.1),
     'L0_ffn_b2': (0.0, 0.1),
     'L1_cond_bg': (-0.5, 0.6),
     'L1_cond_bn1': (0.0, 0.8),
     'L1_cond_bsoma': (0.0, 0.8),
     'L1_cond_btemp': (0.0, 0.8),
     'L1_cond_gamma': (1.0, 0.6),
     'L1_cond_beta': (0.0, 0.8)}
    factors = {'condB_tauraws': 8.0,
     'cond_256': 8.0,
     'cond_1024': 8.0,
     'L1_cond_Wg': 7.384,
     'L1_cond_Wn1': 8.0,
     'L1_cond_Wsoma': 3.654,
     'L1_cond_Wtemp': 4.944,
     'L1_cond_Wout': 3.641,
     'L1_ffn_router_w': 8.0,
     'L1_ffn_w_gate': 8.0,
     'L1_ffn_w_up': 8.0,
     'L1_ffn_w_down': 8.0,
     'L1_ffn_ws_gate_up': 3.667,
     'L1_ffn_ws_down': 3.675}
    for name, (base, spread) in spreads.items():
        noise = np.random.default_rng([zlib.crc32(name.encode()), seed]).standard_normal(out[name].shape)
        drawn = base * np.exp(spread * noise) if base else spread * noise
        out[name] = jnp.asarray(drawn.astype(out[name].dtype))
    for name, factor in factors.items():
        out[name] = (out[name] * factor).astype(out[name].dtype)
    return out
```

```python
from contextlib import ExitStack

import concourse.bass as bass
from concourse import mybir

F32 = mybir.dt.float32
BF16 = mybir.dt.bfloat16
I32 = mybir.dt.int32
U32 = mybir.dt.uint32
ALU = mybir.AluOpType
ACT = mybir.ActivationFunctionType
AX = mybir.AxisListType

P = 128
B, S, H = 8, 512, 256
TOK = B * S
CT = H // P
TT = S // P
LANGS, AD = 10, 64
E0, K0, FF0 = 8, 128, 1024
FT0 = FF0 // P
D = 8
HN = H // 4
E1, TOPK, CAP, FF1 = 64, 8, 128, 192
NT = TOK // P
ZW = H + E1
EPS = 1e-5
CREDIT = 12


def level(m, per=1):
    return (m + 1 + CREDIT) * per


def wait_moved(eng, sem, m, per):
    if not isinstance(m, int) or m >= 0:
        eng.wait_ge(sem, (m + 1) * per)


def settle(eng, tally):
    eng.sem_inc(tally, 1)


def build(nc, t):
    ctx = ExitStack()
    credited = []

    def sb(name, shape, dt=F32):
        return ctx.enter_context(nc.sbuf_tensor(name, shape, dt))

    def sem(name, per=1):
        s = ctx.enter_context(nc.semaphore(name))
        if per:
            credited.append((s, per))
        return s

    out = t["out"]
    x_rows = t["x"].rearrange("b s h -> (b s) h")
    n0_rows = nc.dram_tensor("n0_rows", (TOK, H), F32, kind="Internal").ap()
    x1_rows = nc.dram_tensor("x1_rows", (TOK, H), F32, kind="Internal").ap()
    odd_rows = nc.dram_tensor("odd_rows", (TOK + P, H), F32, kind="Internal").ap()
    z_rows = nc.dram_tensor("z_rows", (TOK + P, ZW), F32, kind="Internal").ap()

    with ctx:
        ident = sb("ident", [P, P])
        iota_f = sb("iota_f", [P, P])
        iota_p = sb("iota_p", [P, 1])
        dummy_row = sb("dummy_row", [P, 1])
        tri = sb("tri", [P, P], BF16)
        before = sb("before", [NT, NT], BF16)
        mhalf = sb("mhalf", [P, TT])
        rowbase = sb("rowbase", [P, 1], I32)
        rowbase_f = sb("rowbase_f", [P, 1])
        zeros = sb("zeros", [P, TOK // 4 * H // P])
        wg0 = sb("wg0", [P, CT, E0])
        gam0 = sb("gam0", [P, B, CT])
        bet0 = sb("bet0", [P, B, CT])
        b1_0 = sb("b1_0", [P, E0, FT0])
        wg1 = sb("wg1", [P, 2 * CT, H])
        wsoma = sb("wsoma", [P, CT, H])
        wtemp = sb("wtemp", [P, CT, H])
        wout = sb("wout", [P, CT, H])
        wn1 = sb("wn1", [P, CT, HN])
        wn2 = sb("wn2", [HN, D])
        wn2_rep = sb("wn2_rep", [HN, D, P])
        router = sb("router", [P, CT, E1])
        ws_gu = sb("ws_gu", [P, CT, 2 * FF1])
        ws_da = sb("ws_da", [P, H])
        ws_db = sb("ws_db", [FF1 - P, H])
        bg_h = sb("bg_h", [P, CT])
        btemp_h = sb("btemp_h", [P, CT])
        bsoma = sb("bsoma", [P, CT])
        bn1 = sb("bn1", [HN, 1])
        bn2_h = sb("bn2_h", [P, D])
        gam1 = sb("gam1", [P, CT])
        bet1 = sb("bet1", [P, CT])
        tau = sb("tau", [P, D + 1])
        alpha = sb("alpha", [P, D + 1])
        blend = sb("blend", [P, CT, D])
        blend_m = sb("blend_m", [P, CT])
        blend_s = sb("blend_s", [P, CT])
        mask_all = sb("mask_all", [P, E1, NT], BF16)
        Rx = sb("Rx", [NT, 4, P + 3], BF16)

        layer0 = ExitStack()
        outer, ctx_of = ctx, [layer0]

        def sb(name, shape, dt=F32):
            return ctx_of[0].enter_context(nc.sbuf_tensor(name, shape, dt))

        xt = [sb(f"xt{p}", [P, TT, H]) for p in range(2)]
        w1c = [sb(f"w1c{p}", [P, CT, AD]) for p in range(2)]
        w2c = [sb(f"w2c{p}", [AD + 1, H]) for p in range(2)]
        b1c = [sb(f"b1c{p}", [AD, 1]) for p in range(2)]
        xT = sb("xT", [P, CT, S])
        hT = sb("hT", [AD + 1, S])
        y = [sb(f"y{p}", [P, TT, H]) for p in range(2)]
        stat = sb("stat", [P, TT, 6])
        mv = [sb(f"mv{p}", [P, TT, 2]) for p in range(2)]
        veps = sb("veps", [P, TT])
        rstd = [sb(f"rstd{p}", [P, TT]) for p in range(2)]
        nrm = [sb(f"nrm{p}", [P, TT, H]) for p in range(2)]
        yT = sb("yT", [P, CT, S])
        lg0 = sb("lg0", [P, B, TT, E0])
        red0 = sb("red0", [P, B * TT])
        prob = sb("prob", [P, TT, B * E0])
        ranks = sb("ranks", [B * E0, S])
        gval = sb("gval", [B * E0, K0])
        gidx = sb("gidx", [B * E0, K0], U32)
        gidx_f = sb("gidx_f", [B * E0, K0])
        idxT = sb("idxT", [P, B, E0], I32)
        gateT = sb("gateT", [P, B, E0])
        w1r = [sb(f"w1r{p}", [P, CT, FF0]) for p in range(2)]
        w2r = [sb(f"w2r{p}", [P, FT0, H]) for p in range(2)]
        b2r = [sb(f"b2r{p}", [P, H]) for p in range(2)]
        take = [sb(f"take{p}", [P, 4], I32) for p in range(2)]
        put = [sb(f"put{p}", [P, 4], I32) for p in range(2)]
        xg0 = [sb(f"xg0_{p}", [P, 4, H]) for p in range(2)]
        exT = [sb(f"exT{p}", [P, CT, S]) for p in range(2)]
        h1 = sb("h1", [P, FT0, S])
        ob = [sb(f"ob{p}", [P, 4, H]) for p in range(2)]
        layer0.close()
        ctx_of[0] = outer
        x1t = [sb(f"x1t{p}", [P, TT, H]) for p in range(2)]
        x1T = sb("x1T", [P, CT, S])
        ctxT = sb("ctxT", [P, CT, S])
        wgt = sb("wgt", [P, CT, S])
        gated2 = [sb(f"gated2_{p}", [P, CT, S]) for p in range(2)]
        h1T = [sb(f"h1T{p}", [HN, S]) for p in range(2)]
        soma = [sb(f"soma{p}", [P, CT, S]) for p in range(2)]
        md = [sb(f"md{p}", [P, S]) for p in range(2)]
        drive = [sb(f"drive{p}", [P, CT, S]) for p in range(2)]
        trace = [sb(f"trace{p}", [P, CT, S]) for p in range(2)]
        acc = [sb(f"acc{p}", [P, CT, S]) for p in range(2)]
        gt = sb("gt", [P, CT, S])
        prodT = sb("prodT", [P, CT, S])
        stat1 = sb("stat1", [P, TT, 6])
        mv1 = sb("mv_b", [P, TT, 2])
        veps1 = sb("veps1", [P, TT])
        rstd1 = sb("rstd_b", [P, TT])
        zrow = sb("zrow", [P, TT, ZW])
        zT = sb("zT", [P, CT, S])
        top8 = sb("top8", [P, TT, 8])
        rep = sb("rep", [P, TT, E1])
        neg = sb("neg", [P, TT, E1])
        mask = sb("mask", [P, TT, E1])
        ex = sb("ex", [P, TT, E1])
        wsum = sb("wsum", [P, TT])
        sgA = sb("sgA", [P, S])
        sgB = sb("sgB", [FF1 - P, S])
        hsA = sb("hsA", [P, S])
        hsB = sb("hsB", [FF1 - P, S])
        xr = sb("xr", [P, TT, H])
        ost = sb("ost", [P, TT, H])
        mstat = sb("mstat", [P, 4, NT], BF16)
        Bf = sb("Bf", [NT, 4])
        Bn = sb("Bn", [NT, 4])
        ge = sb("ge", [NT, 4, P], BF16)
        lt = sb("lt", [NT, 4, P], BF16)
        sel = sb("sel", [NT, 4, P], BF16)
        meta = sb("meta", [P, 4, 3])
        cb = sb("cb", [P, 4])
        cmp = sb("cmp", [P, 4, P])
        pos = sb("pos", [P, 4])
        slot_f = sb("slot_f", [P, 4])
        slot_g = sb("slot_g", [P, 4])
        slots = sb("slots", [P, E1], I32)
        gi = [sb(f"gi{i}", [P, 1], I32) for i in range(4)]
        xg1 = [sb(f"xg1_{i}", [P, ZW]) for i in range(4)]
        xgT = [sb(f"xgT{p}", [P, CT, P]) for p in range(2)]
        wgr = [sb(f"wgr{i}", [P, CT, FF1]) for i in range(4)]
        wur = [sb(f"wur{i}", [P, CT, FF1]) for i in range(4)]
        wda = [sb(f"wda{i}", [P, H]) for i in range(4)]
        wdb = [sb(f"wdb{i}", [FF1 - P, H]) for i in range(4)]
        sg1 = [sb(f"sg1_{p}", [P, 2, P]) for p in range(2)]
        he = [sb(f"he{p}", [P, 2, P]) for p in range(2)]
        ys = [sb(f"ys{i}", [P, H]) for i in range(4)]
        pi = [sb(f"pi{i}", [P, 1], I32) for i in range(4)]
        share = [sb(f"share{i}", [P, 1]) for i in range(4)]

        bank = ctx.enter_context(nc.psum_tensor("bank", [P, 8, 512], F32))

        def two(n):
            return bank[:, n:n + 2, :]

        def rows4(n):
            return bank[:, n:n + 2, :].rearrange("p k (j c) -> p (k j) c", c=H)

        FR = FF1 - P
        RB = FR

        loaded0 = sem("loaded0", 0)
        loaded1 = sem("loaded1", 0)
        x1_set = sem("x1_set", 0)
        z_dummy = sem("z_dummy", 0)
        zeros_set = sem("zeros_set", 0)
        consts = sem("consts", 0)
        tally = sem("tally", 0)
        prep1 = sem("prep1", 0)
        prep1a = sem("prep1a", 0)
        N_CONST0 = 2

        a_in = [sem(f"a_in{p}", 16 * 7) for p in range(2)]
        a_stored = [sem(f"a_stored{p}", 16) for p in range(2)]
        a_xTm, a_xT, a_hm, a_h, a_ad, a_y, a_mv, a_rstd, a_nrm, a_nT, a_yT, a_lgm, a_lg = (
            sem("a_" + n) for n in ("xTm", "xT", "hm", "h", "ad", "y", "mv", "rstd", "nrm", "nT", "yT", "lgm", "lg"))

        k_sub, k_exp, k_prob, k_pT, k_sel, k_idx, k_tab = (
            sem("k_" + n, 0) for n in ("sub", "exp", "prob", "pT", "sel", "idx", "tab"))

        b_w = [sem(f"b_w{p}", 48) for p in range(2)]
        b_got = [sem(f"b_got{p}", 0) for p in range(2)]
        b_put = [sem(f"b_put{p}", 0) for p in range(2)]
        b_take, b_place, e_gi, e_pi = sem("b_take"), sem("b_place"), sem("e_gi"), sem("e_pi")
        b_T, b_exT, b_hm, b_h, b_o, b_oa, b_out = (
            sem("b_" + n) for n in ("T", "exT", "hm", "h", "o", "oa", "out"))

        c_in = [sem(f"c_in{p}", 16) for p in range(2)]
        c_xr, c_zst, c_ost = sem("c_xr", 16), sem("c_zst", 16), sem("c_ost", 16)
        (c_Tm, c_x1T, c_ctx, c_wgm, c_wgt, c_gat, c_h1m, c_h1, c_som, c_so, c_mm, c_md, c_u, c_acc,
         c_tem, c_gt, c_pr, c_om, c_mv, c_rs, c_no, c_zm, c_zT, c_lgm, c_neg, c_ex, c_top, c_zr,
         c_bm, c_bt, c_hsB, c_am, c_at, c_hsA, c_dm, c_fin) = (
            sem("c_" + n) for n in (
                "Tm", "x1T", "ctx", "wgm", "wgt", "gat", "h1m", "h1", "som", "so", "mm", "md", "u", "acc",
                "tem", "gt", "pr", "om", "mv", "rs", "no", "zm", "zT", "lgm", "neg", "ex", "top", "zr",
                "bm", "bt", "hsB", "am", "at", "hsA", "dm", "fin"))

        e_w = [sem(f"e_w{i}", 64) for i in range(4)]
        e_got = [sem(f"e_got{i}", 0) for i in range(4)]
        e_put = [sem(f"e_put{p}", 0) for p in range(2)]
        e_sum = sem("e_sum", 0)
        (e_ms, e_R, e_Rc, e_B, e_S, e_G, e_slot, e_T, e_xT, e_gu, e_sg, e_h, e_d, e_ys) = (
            sem("e_" + n) for n in ("ms", "R", "Rc", "B", "S", "G", "slot", "T", "xT", "gu", "sg", "h", "d", "ys"))

        block = ctx.enter_context(nc.Block())

        def prev(h, p):
            return (h, 0) if p else (h - 1, 1)

        def nxt(h, p):
            return (h + 1, 0) if p else (h, 1)

        def staggered(eng, front, both, back):
            front(0, 0)
            with eng.Fori(0, B // 2 - 1) as i:
                both(i, 1)
                both(i + 1, 0)
            both(B // 2 - 1, 1)
            back(B // 2 - 1, 1)

        def experts(eng, group):
            n = E1 // 4
            group(0, True, True, False)
            with eng.Fori(1, n - 2) as k:
                group(k, True, False, False)
            group(n - 2, False, False, False)
            group(n - 1, False, False, True)

        def ffn(eng, group):
            group(0, False)
            with eng.Fori(1, E0 // 2 - 1) as g:
                group(g, False)
            group(E0 // 2 - 1, True)

        def conditioning(eng, front_only, step):
            front_only()
            step(0, 0, True, True, False)
            with eng.Fori(0, B // 2 - 1) as i:
                step(i, 1, True, True, True)
                step(i + 1, 0, True, True, True)
            step(B // 2 - 1, 1, False, True, True)
            step(B // 2, 0, False, False, True)

        @block.sync
        def _(sp):
            def a_load(h, p):
                b = 2 * h + p
                sp.wait_ge(a_y, level(b - 2))
                settle(sp, tally)
                lang = sp.value_load(t["ids"][0:1, bass.ds(b, 1)], min_val=0, max_val=LANGS - 1)
                sp.dma_start(xt[p][:, :, :], x_rows[bass.ds(b * S, S), :].rearrange("(t p) c -> p t c", p=P)).then_inc(a_in[p], 16)
                sp.dma_start(w1c[p][:, :, :], t["aW1"].rearrange("l (c p) a -> l p c a", p=P)[bass.ds(lang, 1), :, :, :].rearrange("l p c a -> (l p) c a")).then_inc(a_in[p], 16)
                sp.dma_start(w2c[p][0:AD, :], t["aW2"][bass.ds(lang, 1), :, :].rearrange("l a c -> (l a) c")).then_inc(a_in[p], 16)
                sp.dma_start(w2c[p][AD:AD + 1, :], t["ab2"][bass.ds(lang, 1), :]).then_inc(a_in[p], 16)
                sp.dma_start(b1c[p][:, :], t["ab1"][bass.ds(lang, 1), :].rearrange("l a -> a l")).then_inc(a_in[p], 16)
                sp.dma_start(gam0[:, bass.ds(b, 1), :].rearrange("p b c -> p (b c)"), t["agam"][bass.ds(lang, 1), :, :].rearrange("l p c -> (l p) c")).then_inc(a_in[p], 16)
                sp.dma_start(bet0[:, bass.ds(b, 1), :].rearrange("p b c -> p (b c)"), t["abet"][bass.ds(lang, 1), :, :].rearrange("l p c -> (l p) c")).then_inc(a_in[p], 16)

            def a_store(h, p):
                b = 2 * h + p
                sp.wait_ge(a_nrm, level(b))
                sp.dma_start(n0_rows[bass.ds(b * S, S), :].rearrange("(t p) c -> p t c", p=P), nrm[p][:, :, :]).then_inc(a_stored[p], 16)

            def a_both(h, p):
                a_load(h, p)
                a_store(*prev(h, p))

            staggered(sp, a_load, a_both, a_store)

            def b_load(g, last):
                for q in range(2):
                    e = 2 * g + q
                    sp.wait_ge(b_oa, level(2 * (e - 2) + 1))
                    sp.dma_start(w1r[q][:, :, :], t["fW1"].rearrange("e (c p) f -> e p c f", p=P)[bass.ds(e, 1), :, :, :].rearrange("e p c f -> (e p) c f")).then_inc(b_w[q], 16)
                    sp.dma_start(w2r[q][:, :, :], t["fW2"].rearrange("e (f p) c -> e p f c", p=P)[bass.ds(e, 1), :, :, :].rearrange("e p f c -> (e p) f c")).then_inc(b_w[q], 16)
                    sp.dma_start(b2r[q][:, :], t["fb2"][bass.ds(e, 1), :].to_broadcast([P, H])).then_inc(b_w[q], 16)

            ffn(sp, b_load)

            for p in range(2):
                wait_moved(sp, b_put[p], E0 - 1, 64)

            def c_load(h, p):
                b = 2 * h + p
                sp.wait_ge(c_Tm, level(b - 2))
                sp.dma_start(x1t[p][:, :, :], x1_rows[bass.ds(b * S, S), :].rearrange("(t p) c -> p t c", p=P)).then_inc(c_in[p], 16)

            def c_front():
                c_load(0, 0)
                c_load(0, 1)

            def c_step(h, p, front, middle, tail):
                b = 2 * h + p
                if front and not (isinstance(h, int) and h == B // 2 - 1):
                    c_load(h + 1, p)
                if tail:
                    q = b - 1
                    sp.wait_ge(c_fin, level(q - 1))
                    sp.dma_start(xr[:, :, :], x1_rows[bass.ds(q * S, S), :].rearrange("(t p) c -> p t c", p=P)).then_inc(c_xr, 16)
                    sp.wait_ge(c_zr, level(q))
                    sp.dma_start(z_rows[bass.ds(q * S, S), :].rearrange("(t p) c -> p t c", p=P), zrow[:, :, :]).then_inc(c_zst, 16)
                    sp.wait_ge(c_fin, level(q))
                    sp.dma_start(out[bass.ds(q * S, S), :].rearrange("(t p) c -> p t c", p=P), ost[:, :, :]).then_inc(c_ost, 16)

            c_front()
            c_step(0, 0, True, True, False)
            with sp.Fori(0, B // 2 - 2) as i:
                c_step(i, 1, True, True, True)
                c_step(i + 1, 0, True, True, True)
            c_step(B // 2 - 2, 1, True, True, True)
            c_step(B // 2 - 1, 0, False, True, True)
            c_step(B // 2 - 1, 1, False, True, True)
            c_step(B // 2, 0, False, False, True)

            def e_load(k):
                for i in range(4):
                    e = 4 * k + i
                    sp.wait_ge(e_d, level(e - 4))
                    sp.dma_start(wgr[i][:, :, :], t["mwg"].rearrange("e (c p) f -> e p c f", p=P)[bass.ds(e, 1), :, :, :].rearrange("e p c f -> (e p) c f")).then_inc(e_w[i], 16)
                    sp.dma_start(wur[i][:, :, :], t["mwu"].rearrange("e (c p) f -> e p c f", p=P)[bass.ds(e, 1), :, :, :].rearrange("e p c f -> (e p) c f")).then_inc(e_w[i], 16)
                    sp.dma_start(wda[i][:, :], t["mwd"][bass.ds(e, 1), 0:P, :].rearrange("e f c -> (e f) c")).then_inc(e_w[i], 16)
                    sp.dma_start(wdb[i][:, :], t["mwd"][bass.ds(e, 1), P:FF1, :].rearrange("e f c -> (e f) c")).then_inc(e_w[i], 16)

            with sp.Fori(0, E1 // 4) as k:
                e_load(k)
            sp.wait_ge(e_sum, 16)

        @block.gpsimd
        def _(pool):
            G = nc.gpsimd
            for s, per in credited:
                pool.sem_inc(s, CREDIT * per)
            G.memset(zeros[:, :], 0.0).then_inc(zeros_set, 1)
            pool.drain()
            G.memset(ident[:, :], 0.0)
            pool.drain()
            G.memset(tri[:, :], 1.0)
            pool.drain()
            G.memset(before[:, :], 1.0)
            pool.drain()
            G.memset(mhalf[:, :], -0.5)
            pool.drain()
            G.memset(hT[AD:AD + 1, :], 1.0)
            pool.drain()
            G.iota(iota_f[:, :], [[1, P]], base=0, channel_multiplier=0, allow_small_or_imprecise_dtypes=True)
            pool.drain()
            G.iota(iota_p[:, :], [[0, 1]], base=0, channel_multiplier=1, allow_small_or_imprecise_dtypes=True)
            pool.drain()
            G.iota(dummy_row[:, :], [[0, 1]], base=TOK, channel_multiplier=1, allow_small_or_imprecise_dtypes=True)
            pool.drain()
            G.iota(rowbase[:, :], [[0, 1]], base=0, channel_multiplier=S // E0)
            pool.drain()
            G.memset(Rx[:, :, P + 2], 1.0)
            pool.drain()
            G.iota(Rx[:, :, P + 1], [[0, 4]], base=0, channel_multiplier=P, allow_small_or_imprecise_dtypes=True)
            pool.drain()
            G.affine_select(out=ident[:, :], in_=ident[:, :], compare_op=ALU.not_equal, fill=1.0, base=0,
                            pattern=[[-1, P]], channel_multiplier=1)
            pool.drain()
            G.affine_select(out=tri[:, :], in_=tri[:, :], compare_op=ALU.is_ge, fill=0.0, base=0,
                            pattern=[[1, P]], channel_multiplier=-1)
            pool.drain()
            G.affine_select(out=before[:, :], in_=before[:, :], compare_op=ALU.is_ge, fill=0.0, base=-1,
                            pattern=[[1, NT]], channel_multiplier=-1)
            pool.drain().then_inc(consts, 1)

            def a_pow(h, p):
                b = 2 * h + p
                pool.wait_ge(a_mv, level(b))
                pool.wait_ge(a_nrm, level(b - 2))
                settle(pool, tally)
                G.tensor_scalar(veps[:, :], mv[p][:, :, 1], EPS, None, ALU.add)
                pool.drain()
                G.tensor_tensor(rstd[p][:, :], veps[:, :], mhalf[:, :], ALU.pow).then_inc(a_rstd, 1)
                pool.drain()

            with pool.Fori(0, B // 2) as i:
                a_pow(i, 0)
                a_pow(i, 1)

            pool.wait_ge(k_tab, 1)
            pool.wait_ge(x1_set, 16)
            for p in range(2):
                pool.wait_ge(a_stored[p], level(B // 2 - 1, 16))

            def b_gather(g, r):
                p, e, s = r & 1, 2 * g + (r >> 1), 4 * g + r
                pool.wait_ge(b_T, level(s - 2))
                settle(pool, tally)
                G.tensor_copy(take[p][:, :], idxT[:, 4 * p:4 * p + 4, bass.ds(e, 1)].rearrange("p b e -> p (b e)")).then_inc(b_take, 1)
                pool.wait_ge(b_take, level(s))
                settle(pool, tally)
                for j in range(4):
                    G.indirect_dma_start(xg0[p][:, j, :], None, n0_rows[:, :],
                                         bass.IndirectOffsetOnAxis(ap=take[p][:, j:j + 1], axis=0)).then_inc(b_got[p], 16)

            def b_scatter(g, r):
                p, e, s = r & 1, 2 * g + (r >> 1), 4 * g + r
                pool.wait_ge(b_out, level(s))
                wait_moved(pool, b_put[p], e - 1, 64)
                settle(pool, tally)
                G.tensor_copy(put[p][:, :], idxT[:, 4 * p:4 * p + 4, bass.ds(e, 1)].rearrange("p b e -> p (b e)")).then_inc(b_place, 1)
                pool.wait_ge(b_place, level(s))
                settle(pool, tally)
                for j in range(4):
                    G.indirect_dma_start(x1_rows[:, :], bass.IndirectOffsetOnAxis(ap=put[p][:, j:j + 1], axis=0),
                                         ob[p][:, j, :], None, compute_op=ALU.add).then_inc(b_put[p], 16)

            def b_group(g, last):
                for r in range(4):
                    if r < 2:
                        b_gather(g, r + 2)
                    elif not last:
                        b_gather(g + 1, r - 2)
                    b_scatter(g, r)

            b_gather(0, 0)
            b_gather(0, 1)
            ffn(pool, b_group)

            with pool.Fori(0, B) as q:
                pool.wait_ge(c_mv, level(q))
                pool.wait_ge(c_no, level(q - 1))
                settle(pool, tally)
                G.tensor_scalar(veps1[:, :], mv1[:, :, 1], 4 * EPS, None, ALU.add)
                pool.drain()
                G.tensor_tensor(rstd1[:, :], veps1[:, :], mhalf[:, :], ALU.pow).then_inc(c_rs, 1)
                pool.drain()

            pool.wait_ge(z_dummy, 16 * 6)
            pool.wait_ge(c_zst, level(B - 1, 16))
            pool.wait_ge(c_ost, level(B - 1, 16))

            def e_gather(k, i):
                e = 4 * k + i
                pool.wait_ge(e_slot, level(k))
                pool.wait_ge(e_xT, level(e - 4))
                settle(pool, tally)
                G.tensor_copy(gi[i][:, :], slots[:, bass.ds(e, 1)]).then_inc(e_gi, 1)
                pool.wait_ge(e_gi, level(e))
                settle(pool, tally)
                G.indirect_dma_start(xg1[i][:, :], None, z_rows[:, :],
                                     bass.IndirectOffsetOnAxis(ap=gi[i][:, :], axis=0)).then_inc(e_got[i], 16)

            def e_scatter(k, i):
                e = 4 * k + i
                pool.wait_ge(e_ys, level(e))
                wait_moved(pool, e_put[i % 2], 2 * k + i // 2 - 1, 16)
                G.tensor_copy(pi[i][:, :], slots[:, bass.ds(e, 1)]).then_inc(e_pi, 1)
                pool.wait_ge(e_pi, level(e))
                settle(pool, tally)
                G.indirect_dma_start((out, odd_rows)[i % 2][:, :], bass.IndirectOffsetOnAxis(ap=pi[i][:, :], axis=0),
                                     ys[i][:, :], None, compute_op=ALU.add).then_inc(e_put[i % 2], 16)

            def e_group(k, prepare, first, last):
                for i in range(4):
                    if i < 1:
                        e_gather(k, i + 3)
                    elif not last:
                        e_gather(k + 1, i - 1)
                    if i > 1:
                        e_scatter(k, i - 2)
                    elif not first:
                        e_scatter(k - 1, i + 2)

            for i in range(3):
                e_gather(0, i)
            experts(pool, e_group)
            e_scatter(E1 // 4 - 1, 2)
            e_scatter(E1 // 4 - 1, 3)
            for p in range(2):
                wait_moved(pool, e_put[p], E1 // 2 - 1, 16)
            pool.dma_start(out[0:TOK, :].rearrange("(a r) c -> a (r c)", a=P),
                           odd_rows[0:TOK, :].rearrange("(a r) c -> a (r c)", a=P),
                           accum_op=ALU.add, max_dma_last_dim=8192).then_inc(e_sum, 16)

        @block.scalar
        def _(act):
            A = nc.scalar
            act.dma_start(wg0[:, :, :], t["fWgT"].rearrange("(c p) e -> p c e", p=P)).then_inc(loaded0, 16)
            act.dma_start(b1_0[:, :, :], t["fb1"]).then_inc(loaded0, 16)
            act.dma_start(x1_rows.rearrange("(a r) c -> a (r c)", a=P), x_rows.rearrange("(a r) c -> a (r c)", a=P)).then_inc(x1_set, 16)
            act.wait_ge(zeros_set, 1)
            act.dma_start(z_rows[TOK:TOK + P, :], zeros[:, 0:ZW]).then_inc(z_dummy, 16)
            for n in range(4):
                rows = odd_rows[n * TOK // 4:(n + 1) * TOK // 4, :]
                act.dma_start(rows.rearrange("(a r) c -> a (r c)", a=P), zeros[:, :]).then_inc(z_dummy, 16)
            act.dma_start(odd_rows[TOK:TOK + P, :], zeros[:, 0:H]).then_inc(z_dummy, 16)
            n = 0
            for dst, src in (
                    (wg1[:, :, :], t["cWgT"].rearrange("(c p) e -> p c e", p=P)),
                    (wsoma[:, :, :], t["cWsomaT"].rearrange("(c p) e -> p c e", p=P)),
                    (wtemp[:, :, :], t["cWtempT"].rearrange("(c p) e -> p c e", p=P)),
                    (wout[:, :, :], t["cWoutT"].rearrange("(c p) e -> p c e", p=P)),
                    (wn1[:, :, :], t["cWn1T"].rearrange("(c p) e -> p c e", p=P)),
                    (wn2[:, :], t["cWn2T"]),
                    (router[:, :, :], t["routerT"].rearrange("(c p) e -> p c e", p=P)),
                    (ws_gu[:, :, :], t["wsgu"].rearrange("(c p) e -> p c e", p=P)),
                    (ws_da[:, :], t["wsd"][0:P, :]),
                    (ws_db[:, :], t["wsd"][P:FF1, :]),
                    (bg_h[:, :], t["cbg"]),
                    (btemp_h[:, :], t["cbtemp"]),
                    (bsoma[:, :], t["cbsoma"]),
                    (bn1[:, :], t["cbn1"].rearrange("(a o) -> a o", o=1)),
                    (bn2_h[:, :], t["cbn2"].rearrange("(o d) -> o d", o=1).to_broadcast([P, D])),
                    (gam1[:, :], t["cgam"]),
                    (bet1[:, :], t["cbet"]),
                    (tau[:, 0:D], t["tau"].rearrange("(o d) -> o d", o=1).to_broadcast([P, D])),
                    (tau[:, D:D + 1], t["tau_ctx"].rearrange("(o d) -> o d", o=1).to_broadcast([P, 1])),
                    (blend[:, :, :], t["blendT"].rearrange("(c p) d -> p c d", p=P))):
                act.dma_start(dst, src).then_inc(loaded1, 16)
                n += 1
            assert n == N_LOADED1

            act.wait_ge(prep1a, 1)
            A.activation(alpha[:, :], tau[:, :], ACT.Exp)
            A.activation(blend[:, :, :], blend[:, :, :], ACT.Exp)
            act.drain().then_inc(prep1, 1)

            def a_front(h, p):
                b = 2 * h + p
                act.wait_ge(a_xTm, level(b))
                act.wait_ge(a_hm, level(b - 1))
                A.activation(xT[:, :, :], two(0), ACT.Copy).then_inc(a_xT, 1)
                act.wait_ge(a_hm, level(b))
                act.wait_ge(a_ad, level(b - 1))
                A.activation(hT[0:AD, :], bank[0:AD, 2, :], ACT.Relu, bias=b1c[p][:, :]).then_inc(a_h, 1)

            def a_back(h, p):
                b = 2 * h + p
                act.wait_ge(a_nT, level(b))
                act.wait_ge(a_lgm, level(b - 1))
                settle(act, tally)
                for c in range(CT):
                    o = A.activation(yT[:, c, :], bank[:, 5 + c, :], ACT.Identity,
                                     bias=bet0[:, bass.ds(b, 1), c], scale=gam0[:, bass.ds(b, 1), c])
                o.then_inc(a_yT, 1)

            def a_both(h, p):
                a_front(h, p)
                a_back(*prev(h, p))

            staggered(act, a_front, a_both, a_back)

            act.wait_ge(k_sub, 1)
            A.activation(lg0[:, :, :, :], lg0[:, :, :, :], ACT.Exp).then_inc(k_exp, 1)

            def b_group(g, last):
                for r in range(4):
                    s, e = 4 * g + r, 2 * g + (r >> 1)
                    act.wait_ge(b_o, level(s - 1))
                    for f in range(FT0):
                        act.wait_ge(b_hm, level(8 * s + f))
                        settle(act, tally)
                        A.activation(h1[:, f, :], bank[:, 2 + f % 4, :], ACT.Gelu_apprx_tanh,
                                     bias=b1_0[:, bass.ds(e, 1), f]).then_inc(b_h, 1)

            ffn(act, b_group)

            def mod(h, p, d):
                b = 2 * h + p
                act.wait_ge(c_mm, level(D * b + d))
                act.wait_ge(c_u, level(D * b + d - 2))
                A.activation(md[d % 2][:, :], bank[:, 6 + d % 2, :], ACT.Tanh, bias=bn2_h[:, d:d + 1],
                             scale=0.5).then_inc(c_md, 1)

            def x1T_out(n):
                act.wait_ge(c_Tm, level(n))
                act.wait_ge(c_som, level(n - 1))
                act.wait_ge(c_gat, level(n - 1))
                A.activation(x1T[:, :, :], two(0), ACT.Copy).then_inc(c_x1T, 1)

            def wg_out(n, pn):
                act.wait_ge(c_wgm, level(n))
                act.wait_ge(c_gat, level(n - 1))
                for c in range(CT):
                    o = A.activation(wgt[:, c, :], bank[:, 2 + c, :], ACT.Tanh, bias=bg_h[:, c:c + 1], scale=0.5)
                o.then_inc(c_wgt, 1)
                act.wait_ge(c_h1m, level(n))
                act.wait_ge(c_mm, level(D * (n - 1) - 1))
                A.activation(h1T[pn][:, :], bank[0:HN, 4, :], ACT.Gelu, bias=bn1[:, :]).then_inc(c_h1, 1)

            def soma_out(n, pn):
                act.wait_ge(c_som, level(n))
                act.wait_ge(c_pr, level(n - 2))
                for c in range(CT):
                    o = A.activation(soma[pn][:, c, :], bank[:, 2 + c, :], ACT.Gelu, bias=bsoma[:, c:c + 1])
                o.then_inc(c_so, 1)

            def gate_out(q):
                act.wait_ge(c_tem, level(q))
                act.wait_ge(c_pr, level(q - 1))
                for c in range(CT):
                    o = A.activation(gt[:, c, :], bank[:, 4 + c, :], ACT.Tanh, bias=btemp_h[:, c:c + 1], scale=0.5)
                o.then_inc(c_gt, 1)

            def z_out(q):
                act.wait_ge(c_zm, level(q))
                act.wait_ge(c_am, level(q - 1))
                for c in range(CT):
                    o = A.activation(zT[:, c, :], bank[:, c, :], ACT.Identity, bias=bet1[:, c:c + 1],
                                     scale=gam1[:, c:c + 1])
                o.then_inc(c_zT, 1)
                act.wait_ge(c_bm, level(q))
                A.activation(sgB[:, :], bank[0:FR, 2, :], ACT.Tanh, scale=0.5).then_inc(c_bt, 1)

            def exponentials(q):
                act.wait_ge(c_neg, level(q))
                act.wait_ge(c_zr, level(q - 1))
                A.activation(ex[:, :, :], neg[:, :, :], ACT.Exp).then_inc(c_ex, 1)

            def shared_out(q):
                act.wait_ge(c_am, level(q))
                A.activation(sgA[:, :], bank[:, 2, :], ACT.Tanh, scale=0.5).then_inc(c_at, 1)

            def step(h, p, front, middle, tail):
                b = 2 * h + p
                for d in range(D):
                    if middle:
                        mod(h, p, d)
                    if d == 0 and front:
                        x1T_out(b + 1)
                    if d == 1 and front:
                        wg_out(b + 1, 1 - p)
                    if d == 2 and tail:
                        gate_out(b - 1)
                    if d == 3 and front:
                        soma_out(b + 1, 1 - p)
                    if d == 5 and tail:
                        z_out(b - 1)
                    if d == 6 and tail:
                        shared_out(b - 1)
                        exponentials(b - 1)

            def front_only():
                x1T_out(0)
                wg_out(0, 0)
                soma_out(0, 0)

            conditioning(act, front_only, step)

            def silu(k, i):
                e = 4 * k + i
                act.wait_ge(e_gu, level(e))
                act.wait_ge(e_h, level(e - 2))
                A.activation(sg1[i % 2][:, 0, :], bank[:, 4 + i % 2, 0:P], ACT.Silu)
                A.activation(sg1[i % 2][0:FR, 1, :], bank[0:FR, 4 + i % 2, P:2 * P], ACT.Silu).then_inc(e_sg, 1)

            def weigh(k, i):
                e = 4 * k + i
                act.wait_ge(e_d, level(e))
                wait_moved(act, e_put[i % 2], 2 * k + i // 2 - 2, 16)
                A.activation(ys[i][:, :], bank[:, 6 + i % 2, 0:H], ACT.Copy, scale=share[i][:, :]).then_inc(e_ys, 1)

            def e_group(k, prepare, first, last):
                for i in range(4):
                    silu(k, i)
                    if i:
                        weigh(k, i - 1)
                    elif not first:
                        weigh(k - 1, 3)

            experts(act, e_group)
            weigh(E1 // 4 - 1, 3)

        @block.vector
        def _(dve):
            V = nc.vector
            dve.wait_ge(consts, 1)
            dve.wait_ge(loaded1, 16 * N_LOADED1)
            V.tensor_scalar(rowbase[:, :], rowbase[:, :], -S, None, ALU.bitwise_and)
            V.tensor_scalar(bg_h[:, :], bg_h[:, :], 0.5, None, ALU.mult)
            V.tensor_scalar(btemp_h[:, :], btemp_h[:, :], 0.5, None, ALU.mult)
            V.tensor_scalar(bn2_h[:, :], bn2_h[:, :], 0.5, None, ALU.mult)
            V.tensor_copy(wn2_rep[:, :, :], wn2[:, :].unsqueeze(2).to_broadcast([HN, D, P]))
            V.tensor_reduce(blend_m[:, :], blend[:, :, :], AX.X, ALU.max)
            dve.drain()
            V.tensor_copy(rowbase_f[:, :], rowbase[:, :])
            V.tensor_tensor(blend[:, :, :], blend[:, :, :], blend_m[:, :].unsqueeze(2).to_broadcast([P, CT, D]), ALU.subtract)
            dve.drain().then_inc(prep1a, 1)
            dve.wait_ge(prep1, 1)
            V.tensor_scalar(alpha[:, :], alpha[:, :], 1.0, None, ALU.add)
            V.tensor_reduce(blend_s[:, :], blend[:, :, :], AX.X, ALU.add)
            dve.drain()
            V.reciprocal(alpha[:, :], alpha[:, :])
            V.reciprocal(blend_s[:, :], blend_s[:, :])
            dve.drain()
            V.tensor_scalar(blend_s[:, :], blend_s[:, :], 0.25, None, ALU.mult)
            dve.drain()
            V.tensor_tensor(blend[:, :, :], blend[:, :, :], blend_s[:, :].unsqueeze(2).to_broadcast([P, CT, D]), ALU.mult)
            dve.drain().then_inc(prep1a, 1)

            def a_front(h, p):
                b = 2 * h + p
                dve.wait_ge(a_ad, level(b))
                V.tensor_tensor(y[p][:, :, :], rows4(3), xt[p][:, :, :], ALU.add).then_inc(a_y, 1)
                dve.drain()
                for j in range(TT):
                    V.bn_stats(stat[:, j, :], y[p][:, j, :])
                dve.drain()
                for j in range(TT):
                    o = V.bn_aggr(mv[p][:, j, :], stat[:, j, :])
                dve.drain().then_inc(a_mv, 1)

            def a_norm(h, p):
                b = 2 * h + p
                dve.wait_ge(a_rstd, level(b))
                dve.wait_ge(a_stored[p], level(h - 1, 16))
                dve.wait_ge(a_nT, level(b - 2))
                for j in range(TT):
                    o = V.tensor_scalar(nrm[p][:, j, :], y[p][:, j, :], mv[p][:, j, 0:1], rstd[p][:, j:j + 1],
                                        ALU.subtract, ALU.mult)
                o.then_inc(a_nrm, 1)

            def a_logits(h, p):
                b = 2 * h + p
                dve.wait_ge(a_lgm, level(b))
                V.tensor_copy(lg0[:, bass.ds(b, 1), :, :].rearrange("p b t e -> p (b t e)"), bank[:, 7, 0:TT * E0]).then_inc(a_lg, 1)

            def a_both(h, p):
                a_norm(*prev(h, p))
                a_front(h, p)
                a_logits(*prev(h, p))

            def a_back(h, p):
                a_norm(h, p)
                a_logits(h, p)

            staggered(dve, a_front, a_both, a_back)

            lgf = lg0[:, :, :, :].rearrange("p b t e -> p (b t) e")
            rd = red0[:, :].unsqueeze(2).to_broadcast([P, B * TT, E0])
            dve.drain()
            V.tensor_reduce(red0[:, :], lgf, AX.X, ALU.max)
            dve.drain()
            V.tensor_tensor(lgf, lgf, rd, ALU.subtract)
            dve.drain().then_inc(k_sub, 1)
            dve.wait_ge(k_exp, 1)
            V.tensor_reduce(red0[:, :], lgf, AX.X, ALU.add)
            dve.drain()
            V.reciprocal(red0[:, :], red0[:, :])
            dve.drain()
            for j in range(TT):
                V.tensor_tensor(prob[:, j, :].rearrange("p (b e) -> p b e", e=E0), lg0[:, :, j, :],
                                red0[:, :].rearrange("p (b t) -> p b t", t=TT)[:, :, j].unsqueeze(2).to_broadcast([P, B, E0]),
                                ALU.mult)
            dve.drain().then_inc(k_prob, 1)
            dve.wait_ge(k_pT, 1)
            V.tensor_copy(ranks[:, :], bank[0:B * E0, 0, :])
            dve.drain()
            with dve.Fori(0, 1) as _one:
                pass
            for r in range(K0 // 8):
                V.max(gval[:, 8 * r:8 * r + 8], ranks[:, :])
                dve.drain()
                V.max_index(gidx[:, 8 * r:8 * r + 8], gval[:, 8 * r:8 * r + 8], ranks[:, :])
                dve.drain()
                V.match_replace(ranks[:, :], gval[:, 8 * r:8 * r + 8], ranks[:, :], -1.0)
                dve.drain()
            V.tensor_copy(gidx_f[:, :], gidx[:, :])
            dve.drain()
            V.tensor_scalar(gidx_f[:, :], gidx_f[:, :], rowbase_f[0:B * E0, :], None, ALU.add)
            dve.drain().then_inc(k_sel, 1)
            dve.wait_ge(k_idx, 1)
            V.tensor_copy(idxT[:, :, :].rearrange("p b e -> p (b e)"), bank[:, 1, 0:B * E0])
            V.tensor_copy(gateT[:, :, :].rearrange("p b e -> p (b e)"), bank[:, 1, B * E0:2 * B * E0])
            dve.drain().then_inc(k_tab, 1)

            def b_exT_out(s, p):
                dve.wait_ge(b_T, level(s))
                dve.wait_ge(b_hm, level(8 * (s - 2) + 7 + 0))
                for j in range(4):
                    for c in range(CT):
                        b = 4 * p + j
                        o = V.tensor_scalar(exT[p][:, c, j * P:(j + 1) * P], bank[:, c, j * P:(j + 1) * P],
                                            gam0[:, b, c:c + 1], bet0[:, b, c:c + 1], ALU.mult, ALU.add)
                o.then_inc(b_exT, 1)

            def b_o_out(g, r):
                p, q, e, s = r & 1, r >> 1, 2 * g + (r >> 1), 4 * g + r
                dve.wait_ge(b_o, level(s))
                wait_moved(dve, b_put[p], e - 1, 64)
                V.tensor_tensor(ob[p][:, :, :], rows4(6), b2r[q][:, :].unsqueeze(1).to_broadcast([P, 4, H]),
                                ALU.add).then_inc(b_oa, 1)
                dve.drain()
                V.tensor_tensor(ob[p][:, :, :], ob[p][:, :, :],
                                gateT[:, 4 * p:4 * p + 4, bass.ds(e, 1)].to_broadcast([P, 4, H]),
                                ALU.mult).then_inc(b_out, 1)

            def b_group(g, last):
                for r in range(4):
                    if not (last and r == 3):
                        b_exT_out(4 * g + r + 1, (r + 1) & 1)
                    b_o_out(g, r)

            b_exT_out(0, 0)
            ffn(dve, b_group)

            def bank_step(h, p, d):
                b = 2 * h + p
                if d < D:
                    dve.wait_ge(c_md, level(D * b + d))
                    V.scalar_tensor_tensor(drive[d % 2][:, :, :], md[d % 2][:, :].unsqueeze(1).to_broadcast([P, CT, S]),
                                           2.0, gated2[p][:, :, :], ALU.add, ALU.mult).then_inc(c_u, 1)
                if 1 <= d <= D:
                    q = d - 1
                    for c in range(CT):
                        V.tensor_tensor_scan(trace[q % 2][:, c, :], alpha[:, q:q + 1].to_broadcast([P, S]),
                                             drive[q % 2][:, c, :], 0.0, ALU.mult, ALU.add)
                if d >= 2:
                    q = d - 2
                    if q == 0:
                        dve.wait_ge(c_tem, level(b - 2))
                    for c in range(CT):
                        if q == 0:
                            o = V.tensor_scalar(acc[p][:, c, :], trace[0][:, c, :], blend[:, c, 0:1], None, ALU.mult)
                        else:
                            o = V.scalar_tensor_tensor(acc[p][:, c, :], trace[q % 2][:, c, :], blend[:, c, q:q + 1],
                                                       acc[p][:, c, :], ALU.mult, ALU.add)
                    if q == D - 1:
                        o.then_inc(c_acc, 1)
                dve.drain()

            def ctx_scan(n):
                dve.wait_ge(c_x1T, level(n))
                dve.wait_ge(c_wgm, level(n - 1))
                for c in range(CT):
                    o = V.tensor_tensor_scan(ctxT[:, c, :], alpha[:, D:D + 1].to_broadcast([P, S]), x1T[:, c, :],
                                             0.0, ALU.mult, ALU.add)
                o.then_inc(c_ctx, 1)

            def gate_in(n, pn):
                dve.wait_ge(c_wgt, level(n))
                V.scalar_tensor_tensor(gated2[pn][:, :, :], wgt[:, :, :], 1.0, x1T[:, :, :], ALU.add,
                                       ALU.mult).then_inc(c_gat, 1)

            def gate_soma(q, pq):
                dve.wait_ge(c_gt, level(q))
                dve.wait_ge(c_so, level(q))
                dve.wait_ge(c_om, level(q - 1))
                V.scalar_tensor_tensor(prodT[:, :, :], gt[:, :, :], 1.0, soma[pq][:, :, :], ALU.add,
                                       ALU.mult).then_inc(c_pr, 1)

            def stats(q):
                dve.wait_ge(c_om, level(q))
                for j in range(TT):
                    V.bn_stats(stat1[:, j, :], rows4(0)[:, j, :])
                dve.drain()
                for j in range(TT):
                    V.bn_aggr(mv1[:, j, :], stat1[:, j, :])
                dve.drain().then_inc(c_mv, 1)

            def normalise(q):
                dve.wait_ge(c_rs, level(q))
                dve.wait_ge(c_zst, level(q - 1, 16))
                dve.wait_ge(c_zm, level(q - 1))
                for j in range(TT):
                    o = V.tensor_scalar(zrow[:, j, 0:H], rows4(0)[:, j, :], mv1[:, j, 0:1], rstd1[:, j:j + 1],
                                        ALU.subtract, ALU.mult)
                o.then_inc(c_no, 1)

            lgp = bank[:, 5, 0:TT * E1].rearrange("p (t e) -> p t e", e=E1)

            def pick(q):
                dve.wait_ge(c_lgm, level(q))
                settle(dve, tally)
                for j in range(TT):
                    V.max(top8[:, j, :], lgp[:, j, :])
                dve.drain()
                dve.wait_ge(c_ex, level(q - 1))
                V.tensor_tensor(neg[:, :, :], lgp, top8[:, :, 0:1].to_broadcast([P, TT, E1]), ALU.subtract).then_inc(c_neg, 1)
                for j in range(TT):
                    V.match_replace(rep[:, j, :], top8[:, j, :], lgp[:, j, :], -3.0e38)
                dve.drain()
                V.tensor_tensor(mask[:, :, :], rep[:, :, :], lgp, ALU.not_equal).then_inc(c_top, 1)
                dve.drain()
                V.tensor_copy(mask_all[:, :, bass.ds(q * TT, TT)].rearrange("p e t -> p t e"), mask[:, :, :])

            def shared_b(q):
                dve.wait_ge(c_bt, level(q))
                dve.wait_ge(c_dm, level(q - 1))
                V.scalar_tensor_tensor(hsB[:, :], sgB[:, :], 1.0, bank[0:FR, 2, :], ALU.add, ALU.mult)
                dve.drain()
                V.tensor_tensor(hsB[:, :], hsB[:, :], bank[0:FR, 3, :], ALU.mult).then_inc(c_hsB, 1)

            def shared_a(q):
                dve.wait_ge(c_at, level(q))
                V.scalar_tensor_tensor(hsA[:, :], sgA[:, :], 1.0, bank[:, 2, :], ALU.add, ALU.mult)
                dve.drain()
                V.tensor_tensor(hsA[:, :], hsA[:, :], bank[:, 3, :], ALU.mult).then_inc(c_hsA, 1)

            def route_weights(q):
                dve.wait_ge(c_ex, level(q))
                V.tensor_tensor(mask[:, :, :], mask[:, :, :], ex[:, :, :], ALU.mult)
                dve.drain()
                V.tensor_reduce(wsum[:, :], mask[:, :, :], AX.X, ALU.add)
                dve.drain()
                V.reciprocal(wsum[:, :], wsum[:, :])
                dve.drain()
                V.tensor_tensor(zrow[:, :, H:ZW], mask[:, :, :], wsum[:, :].unsqueeze(2).to_broadcast([P, TT, E1]),
                                ALU.mult).then_inc(c_zr, 1)

            def finish(q):
                dve.wait_ge(c_dm, level(q))
                dve.wait_ge(c_xr, level(q, 16))
                dve.wait_ge(c_ost, level(q - 1, 16))
                V.scalar_tensor_tensor(ost[:, :, :], rows4(0), 0.5, xr[:, :, :], ALU.mult, ALU.add).then_inc(c_fin, 1)

            def step(h, p, front, middle, tail):
                b = 2 * h + p
                for d in range(D):
                    if middle:
                        bank_step(h, p, d)
                    else:
                        dve.drain()
                    if d == 0 and front:
                        ctx_scan(b + 1)
                    if d == 1 and front:
                        gate_in(b + 1, 1 - p)
                    if d == 2 and tail:
                        gate_soma(b - 1, 1 - p)
                    if d == 3 and tail:
                        stats(b - 1)
                    if d == 4 and tail:
                        normalise(b - 1)
                    if d == 5 and tail:
                        pick(b - 1)
                        shared_b(b - 1)
                    if d == 6 and tail:
                        shared_a(b - 1)
                        route_weights(b - 1)
                    if d == 7 and tail:
                        finish(b - 1)
                if middle:
                    bank_step(h, p, D)
                    bank_step(h, p, D + 1)

            def front_only():
                ctx_scan(0)
                gate_in(0, 0)
                dve.drain()

            conditioning(dve, front_only, step)

            dve.drain()

            def prep(k, part):
                if part == 0:
                    dve.wait_ge(e_R, level(k - 1))
                    V.tensor_copy(mstat[:, :, :], mask_all[:, bass.ds(4 * k, 4), :]).then_inc(e_ms, 1)
                elif part == 1:
                    dve.wait_ge(e_R, level(k))
                    dve.wait_ge(e_G, level(k - 1))
                    V.tensor_copy(Rx[:, :, 0:P], bank[0:NT, 1, :].rearrange("p (i s) -> p i s", i=4)).then_inc(e_Rc, 1)
                elif part == 2:
                    dve.wait_ge(e_B, level(k))
                    V.tensor_copy(Bf[:, :], bank[0:NT, 2, 508:512])
                    dve.drain()
                    V.tensor_tensor(Bn[:, :], Bf[:, :], Rx[:, :, P - 1], ALU.add)
                    V.tensor_copy(Rx[:, :, P], Bf[:, :])
                    dve.drain()
                    slot_no = iota_f[0:NT, :].unsqueeze(1).to_broadcast([NT, 4, P])
                    V.tensor_tensor(ge[:, :, :], slot_no, Bf[:, :].unsqueeze(2).to_broadcast([NT, 4, P]), ALU.is_ge)
                    V.tensor_tensor(lt[:, :, :], slot_no, Bn[:, :].unsqueeze(2).to_broadcast([NT, 4, P]), ALU.is_lt)
                    dve.drain()
                    V.tensor_tensor(sel[:, :, :], ge[:, :, :], lt[:, :, :], ALU.mult).then_inc(e_S, 1)
                else:
                    grp = rows4(1)
                    dve.wait_ge(e_G, level(k))
                    V.tensor_copy(meta[:, :, :], grp[:, :, P:P + 3])
                    dve.drain()
                    V.tensor_scalar(cb[:, :], meta[:, :, 0], -1.0, iota_p[:, :], ALU.mult, ALU.add)
                    dve.drain()
                    V.tensor_tensor(cmp[:, :, 0:P - 1], grp[:, :, 0:P - 1], cb[:, :].unsqueeze(2).to_broadcast([P, 4, P - 1]), ALU.is_le)
                    dve.drain()
                    V.tensor_reduce(pos[:, :], cmp[:, :, 0:P - 1], AX.X, ALU.add)
                    dve.drain()
                    V.scalar_tensor_tensor(slot_f[:, :], pos[:, :], dummy_row[:, :], meta[:, :, 1], ALU.subtract, ALU.add)
                    dve.drain()
                    V.tensor_tensor(slot_g[:, :], slot_f[:, :], meta[:, :, 2], ALU.mult)
                    dve.drain()
                    V.tensor_scalar(slots[:, bass.ds(4 * k, 4)], slot_g[:, :], dummy_row[:, :], None, ALU.add).then_inc(e_slot, 1)

            def xgT_out(k, i):
                e = 4 * k + i
                dve.wait_ge(e_T, level(e))
                dve.wait_ge(e_gu, level(e - 2))
                dve.wait_ge(e_ys, level(e - 4))
                V.tensor_copy(share[i][:, :], xg1[i][:, bass.ds(H + e, 1)])
                for c in range(CT):
                    o = V.tensor_scalar(xgT[i % 2][:, c, :], bank[:, 3 * (i % 2), c * P:(c + 1) * P],
                                        gam1[:, c:c + 1], bet1[:, c:c + 1], ALU.mult, ALU.add)
                o.then_inc(e_xT, 1)

            def hidden(k, i):
                e = 4 * k + i
                dve.wait_ge(e_sg, level(e))
                dve.wait_ge(e_d, level(e - 2))
                V.tensor_tensor(he[i % 2][:, 0, :], sg1[i % 2][:, 0, :], bank[:, 4 + i % 2, 2 * P:3 * P], ALU.mult)
                V.tensor_tensor(he[i % 2][0:FR, 1, :], sg1[i % 2][0:FR, 1, :], bank[0:FR, 4 + i % 2, 3 * P:4 * P],
                                ALU.mult).then_inc(e_h, 1)

            def e_group(k, prepare, first, last):
                for i in range(4):
                    if prepare and i == 0:
                        prep(k + 2, 0)
                    if i < 3:
                        xgT_out(k, i + 1)
                    elif not last:
                        xgT_out(k + 1, 0)
                    hidden(k, i)
                    if prepare and i < 3:
                        prep(k + 2, i + 1)

            for k in range(2):
                for part in range(4):
                    prep(k, part)
            xgT_out(0, 0)
            experts(dve, e_group)

        @block.tensor
        def _(pe):
            T = nc.tensor
            pe.wait_ge(consts, 1)
            pe.wait_ge(loaded0, 16 * N_CONST0)

            def a_front(h, p, mid=None):
                b = 2 * h + p
                pe.wait_ge(a_in[p], level(h, 16 * 7))
                pe.wait_ge(a_xT, level(b - 1))
                for c in range(CT):
                    for j in range(TT):
                        o = T.transpose(bank[:, c, j * P:(j + 1) * P], xt[p][:, j, c * P:(c + 1) * P], ident[:, :])
                o.then_inc(a_xTm, 1)
                pe.wait_ge(a_xT, level(b))
                pe.wait_ge(a_h, level(b - 1))
                for c in range(CT):
                    o = T.matmul(bank[0:AD, 2, :], w1c[p][:, c, :], xT[:, c, :], start=(c == 0), stop=(c == CT - 1))
                o.then_inc(a_hm, 1)
                if mid:
                    mid()
                pe.wait_ge(a_h, level(b))
                pe.wait_ge(a_y, level(b - 1))
                for j in range(TT):
                    o = T.matmul(rows4(3)[:, j, :], hT[:, j * P:(j + 1) * P], w2c[p][:, :], start=True, stop=True)
                o.then_inc(a_ad, 1)

            def a_backT(h, p):
                b = 2 * h + p
                pe.wait_ge(a_nrm, level(b))
                pe.wait_ge(a_yT, level(b - 1))
                for c in range(CT):
                    for j in range(TT):
                        o = T.transpose(bank[:, 5 + c, j * P:(j + 1) * P], nrm[p][:, j, c * P:(c + 1) * P], ident[:, :])
                o.then_inc(a_nT, 1)

            def a_logits(h, p):
                b = 2 * h + p
                pe.wait_ge(a_yT, level(b))
                pe.wait_ge(a_lg, level(b - 1))
                for j in range(TT):
                    for c in range(CT):
                        o = T.matmul(bank[:, 7, j * E0:(j + 1) * E0], yT[:, c, j * P:(j + 1) * P], wg0[:, c, :],
                                     start=(c == 0), stop=(c == CT - 1))
                o.then_inc(a_lgm, 1)

            def a_both(h, p):
                a_front(h, p, lambda: a_backT(*prev(h, p)))
                a_logits(*prev(h, p))

            def a_back(h, p):
                a_backT(h, p)
                a_logits(h, p)

            staggered(pe, a_front, a_both, a_back)

            pe.wait_ge(k_prob, 1)
            for j in range(TT):
                o = T.transpose(bank[0:B * E0, 0, j * P:(j + 1) * P], prob[:, j, :], ident[:, :])
            o.then_inc(k_pT, 1)
            pe.wait_ge(k_sel, 1)
            T.transpose(bank[:, 1, 0:B * E0], gidx_f[:, :], ident[0:B * E0, 0:B * E0])
            T.transpose(bank[:, 1, B * E0:2 * B * E0], gval[:, :], ident[0:B * E0, 0:B * E0]).then_inc(k_idx, 1)
            pe.wait_ge(k_tab, 1)

            def b_T_in(s, p, m):
                wait_moved(pe, b_got[p], m, 64)
                pe.wait_ge(b_exT, level(s - 1))
                for j in range(4):
                    for c in range(CT):
                        o = T.transpose(bank[:, c, j * P:(j + 1) * P], xg0[p][:, j, c * P:(c + 1) * P], ident[:, :])
                o.then_inc(b_T, 1)

            def b_group(g, last):
                for r in range(4):
                    p, q, s = r & 1, r >> 1, 4 * g + r
                    if p == 0:
                        pe.wait_ge(b_w[q], level(g, 48))
                    pe.wait_ge(b_exT, level(s))
                    for f in range(FT0):
                        pe.wait_ge(b_h, level(8 * s + f - 4))
                        for c in range(CT):
                            o = T.matmul(bank[:, 2 + f % 4, :], w1r[q][:, c, f * P:(f + 1) * P], exT[p][:, c, :],
                                         start=(c == 0), stop=(c == CT - 1))
                        o.then_inc(b_hm, 1)
                    if not (last and r == 3):
                        b_T_in(s + 1, 1 - p, 2 * g + (r + 1) // 2)
                    pe.wait_ge(b_h, level(8 * s + 7))
                    pe.wait_ge(b_oa, level(s - 1))
                    for j in range(4):
                        for f in range(FT0):
                            o = T.matmul(rows4(6)[:, j, :], h1[:, f, j * P:(j + 1) * P], w2r[q][:, f, :],
                                         start=(f == 0), stop=(f == FT0 - 1))
                    o.then_inc(b_o, 1)

            b_T_in(0, 0, 0)
            ffn(pe, b_group)

            pe.wait_ge(prep1a, 2)

            def mod(h, p, d):
                b = 2 * h + p
                if d == 0:
                    pe.wait_ge(c_h1, level(b))
                pe.wait_ge(c_md, level(D * b + d - 2))
                T.matmul(bank[:, 6 + d % 2, :], wn2_rep[:, d, :], h1T[p][:, :], start=True, stop=True).then_inc(c_mm, 1)

            def project(o_banks, w, src):
                for n in range(CT):
                    k = len(src)
                    for c in range(k):
                        o = T.matmul(bank[:, o_banks + n, :], w[:, c, n * P:(n + 1) * P], src[c], start=(c == 0),
                                     stop=(c == k - 1))
                return o

            def x1T_in(n, hn, pn):
                pe.wait_ge(c_in[pn], level(hn, 16))
                pe.wait_ge(c_fin, level(n - 3))
                for c in range(CT):
                    for j in range(TT):
                        o = T.transpose(bank[:, c, j * P:(j + 1) * P], x1t[pn][:, j, c * P:(c + 1) * P], ident[:, :])
                o.then_inc(c_Tm, 1)

            def wg_in(n):
                pe.wait_ge(c_x1T, level(n))
                pe.wait_ge(c_ctx, level(n))
                pe.wait_ge(c_hsA, level(n - 3))
                project(2, wg1, [x1T[:, 0, :], x1T[:, 1, :], ctxT[:, 0, :], ctxT[:, 1, :]]).then_inc(c_wgm, 1)
                pe.wait_ge(c_top, level(n - 3))
                for c in range(CT):
                    o = T.matmul(bank[0:HN, 4, :], wn1[:, c, :], x1T[:, c, :], start=(c == 0), stop=(c == CT - 1))
                o.then_inc(c_h1m, 1)

            def soma_in(n):
                pe.wait_ge(c_wgt, level(n))
                project(2, wsoma, [x1T[:, 0, :], x1T[:, 1, :]]).then_inc(c_som, 1)

            def temp_in(q, pq, front):
                pe.wait_ge(c_acc, level(q))
                if front:
                    pe.wait_ge(c_h1, level(q + 2))
                pe.wait_ge(c_top, level(q - 1))
                project(4, wtemp, [acc[pq][:, 0, :], acc[pq][:, 1, :]]).then_inc(c_tem, 1)

            def out_in(q, front):
                pe.wait_ge(c_pr, level(q))
                if front:
                    pe.wait_ge(c_x1T, level(q + 2))
                pe.wait_ge(c_fin, level(q - 1))
                for j in range(TT):
                    for c in range(CT):
                        o = T.matmul(rows4(0)[:, j, :], prodT[:, c, j * P:(j + 1) * P], wout[:, c, :],
                                     start=(c == 0), stop=(c == CT - 1))
                o.then_inc(c_om, 1)

            def z_in(q, front):
                pe.wait_ge(c_no, level(q))
                for c in range(CT):
                    for j in range(TT):
                        o = T.transpose(bank[:, c, j * P:(j + 1) * P], zrow[:, j, c * P:(c + 1) * P], ident[:, :])
                o.then_inc(c_zm, 1)
                pe.wait_ge(c_zT, level(q))
                pe.wait_ge(c_gt, level(q))
                for j in range(TT):
                    for c in range(CT):
                        o = T.matmul(bank[:, 5, j * E1:(j + 1) * E1], zT[:, c, j * P:(j + 1) * P], router[:, c, :],
                                     start=(c == 0), stop=(c == CT - 1))
                o.then_inc(c_lgm, 1)
                if front:
                    pe.wait_ge(c_so, level(q + 2))
                pe.wait_ge(c_hsA, level(q - 1))
                for n, lo in ((0, P), (1, FF1 + P)):
                    for c in range(CT):
                        o = T.matmul(bank[0:FR, 2 + n, :], ws_gu[:, c, lo:lo + FR], zT[:, c, :], start=(c == 0),
                                     stop=(c == CT - 1))
                o.then_inc(c_bm, 1)

            def shared_in(q):
                pe.wait_ge(c_hsB, level(q))
                for n, lo in ((0, 0), (1, FF1)):
                    for c in range(CT):
                        o = T.matmul(bank[:, 2 + n, :], ws_gu[:, c, lo:lo + P], zT[:, c, :], start=(c == 0),
                                     stop=(c == CT - 1))
                o.then_inc(c_am, 1)

            def down_in(q):
                pe.wait_ge(c_hsA, level(q))
                for j in range(TT):
                    T.matmul(rows4(0)[:, j, :], hsA[:, j * P:(j + 1) * P], ws_da[:, :], start=True, stop=False)
                    o = T.matmul(rows4(0)[:, j, :], hsB[:, j * P:(j + 1) * P], ws_db[:, :], start=False, stop=True)
                o.then_inc(c_dm, 1)

            def step(h, p, front, middle, tail):
                b = 2 * h + p
                for d in range(D):
                    if middle:
                        mod(h, p, d)
                    if d == 0 and front:
                        x1T_in(b + 1, *nxt(h, p))
                    if d == 1 and front:
                        wg_in(b + 1)
                    if d == 2 and tail:
                        temp_in(b - 1, 1 - p, front)
                    if d == 3:
                        if tail:
                            out_in(b - 1, front)
                        if front:
                            soma_in(b + 1)
                    if d == 5 and tail:
                        z_in(b - 1, front)
                    if d == 6 and tail:
                        shared_in(b - 1)
                    if d == 7 and tail:
                        down_in(b - 1)

            def front_only():
                x1T_in(0, 0, 0)
                wg_in(0)
                soma_in(0)

            conditioning(pe, front_only, step)

            pe.wait_ge(c_fin, level(B - 1))

            def prep(k, part):
                if part == 0:
                    pe.wait_ge(e_ms, level(k))
                    pe.wait_ge(e_slot, level(k - 1))
                    for i in range(4):
                        o = T.matmul(bank[0:NT, 1, i * P:(i + 1) * P], mstat[:, i, :], tri[:, :], start=True, stop=True)
                    o.then_inc(e_R, 1)
                elif part == 1:
                    pe.wait_ge(e_Rc, level(k))
                    settle(pe, tally)
                    T.matmul(bank[0:NT, 2, 508:512], before[:, :], Rx[:, :, P - 1], start=True, stop=True).then_inc(e_B, 1)
                else:
                    pe.wait_ge(e_S, level(k))
                    for i in range(4):
                        o = T.matmul(rows4(1)[:, i, 0:P + 3], sel[:, i, :], Rx[:, i, :], start=True, stop=True)
                    o.then_inc(e_G, 1)

            def rows_in(k, i):
                e = 4 * k + i
                wait_moved(pe, e_got[i], k, 16)
                pe.wait_ge(e_xT, level(e - 2))
                for c in range(CT):
                    o = T.transpose(bank[:, 3 * (i % 2), c * P:(c + 1) * P], xg1[i][:, c * P:(c + 1) * P], ident[:, :])
                o.then_inc(e_T, 1)

            def gate_up(k, i):
                e = 4 * k + i
                pe.wait_ge(e_w[i], level(k, 64))
                pe.wait_ge(e_xT, level(e))
                pe.wait_ge(e_h, level(e - 2))
                dst = bank[:, 4 + i % 2, :]
                for n, (w, lo, m) in enumerate(((wgr, 0, P), (wgr, P, FR), (wur, 0, P), (wur, P, FR))):
                    for c in range(CT):
                        o = T.matmul(dst[0:m, n * P:(n + 1) * P], w[i][:, c, lo:lo + m], xgT[i % 2][:, c, :],
                                     start=(c == 0), stop=(c == CT - 1))
                o.then_inc(e_gu, 1)

            def down(k, i):
                e = 4 * k + i
                pe.wait_ge(e_h, level(e))
                pe.wait_ge(e_ys, level(e - 2))
                T.matmul(bank[:, 6 + i % 2, 0:H], he[i % 2][:, 0, :], wda[i][:, :], start=True, stop=False)
                T.matmul(bank[:, 6 + i % 2, 0:H], he[i % 2][0:FR, 1, :], wdb[i][:, :], start=False,
                         stop=True).then_inc(e_d, 1)

            def e_group(k, prepare, first, last):
                for i in range(4):
                    gate_up(k, i)
                    if i < 3:
                        rows_in(k, i + 1)
                    elif not last:
                        rows_in(k + 1, 0)
                    if prepare and i < 3:
                        prep(k + 2, i)
                    if i:
                        down(k, i - 1)
                    elif not first:
                        down(k - 1, 3)

            for k in range(2):
                for part in range(3):
                    prep(k, part)
            rows_in(0, 0)
            experts(pe, e_group)
            down(E1 // 4 - 1, 3)


N_LOADED1 = 20

LAYOUT = [
    ("x", "x", ""), ("ids", "itok_B_0_8", ""), ("tau", "condB_tauraws", ""),
    ("cWn2T", "cond_256", "transposed"), ("cbn2", "condB_bn2", ""), ("blendT", "cond_1024", "transposed"),
    ("aW1", "L0_cond_W1", ""), ("ab1", "L0_cond_b1", ""), ("aW2", "L0_cond_W2", ""),
    ("ab2", "L0_cond_b2", ""), ("agam", "L0_cond_gamma", "columns"), ("abet", "L0_cond_beta", "columns"),
    ("fWgT", "L0_ffn_Wg", "transposed"), ("fW1", "L0_ffn_W1", ""), ("fb1", "L0_ffn_b1", "partition first"),
    ("fW2", "L0_ffn_W2", ""), ("fb2", "L0_ffn_b2", ""), ("tau_ctx", "L1_cond_tau_ctx", ""),
    ("cWgT", "L1_cond_Wg", "transposed"), ("cbg", "L1_cond_bg", "columns"), ("cWn1T", "L1_cond_Wn1", "transposed"),
    ("cbn1", "L1_cond_bn1", ""), ("cWsomaT", "L1_cond_Wsoma", "transposed"), ("cbsoma", "L1_cond_bsoma", "columns"),
    ("cWtempT", "L1_cond_Wtemp", "transposed"), ("cbtemp", "L1_cond_btemp", "columns"), ("cWoutT", "L1_cond_Wout", "transposed"),
    ("cgam", "L1_cond_gamma", "columns"), ("cbet", "L1_cond_beta", "columns"), ("routerT", "L1_ffn_router_w", "transposed"),
    ("mwg", "L1_ffn_w_gate", ""), ("mwu", "L1_ffn_w_up", ""), ("mwd", "L1_ffn_w_down", ""),
    ("wsgu", "L1_ffn_ws_gate_up", ""), ("wsd", "L1_ffn_ws_down", ""),
]


def kernel(**inputs):
    import numpy as np
    import concourse.bacc as bacc
    from concourse.bass_utils import run_bass_kernel_spmd

    nc = bacc.Bacc("TRN2", target_bir_lowering=False, num_devices=1)
    arrays, t = {}, {}
    for short, name, layout in LAYOUT:
        a = np.asarray(inputs[name])
        if layout == "transposed":
            a = a.T
        elif layout == "columns":
            a = a.reshape(*a.shape[:-1], -1, P).swapaxes(-1, -2)
        elif layout == "partition first":
            a = a.reshape(a.shape[0], -1, P).transpose(2, 0, 1)
        a = np.ascontiguousarray(a)
        a = a.reshape((1,)) if a.ndim == 0 else a
        a = a.reshape((1, -1)) if short == "ids" else a
        arrays[f"in_{short}"] = a
        t[short] = nc.dram_tensor(f"in_{short}", a.shape, mybir.dt.from_np(a.dtype), kind="ExternalInput").ap()
    t["out"] = nc.dram_tensor("out_0", (TOK + P, H), F32, kind="ExternalOutput").ap()
    build(nc, t)
    r = run_bass_kernel_spmd(nc, [arrays], core_ids=[0])
    return np.asarray(r.results[0]["out_0"])[:TOK].reshape(B, S, H)
```

```python
from contextlib import ExitStack

import concourse.bass as bass
from concourse import mybir

F32 = mybir.dt.float32
F32R = mybir.dt.float32r
BF16 = mybir.dt.bfloat16
I32 = mybir.dt.int32
U32 = mybir.dt.uint32
ALU = mybir.AluOpType
ACT = mybir.ActivationFunctionType
AX = mybir.AxisListType

P = 128
B, S, H = 8, 512, 256
TOK = B * S
CT = H // P
TT = S // P
LANGS, AD = 10, 64
E0, K0, FF0 = 8, 128, 1024
FT0 = FF0 // P
D = 8
MR = 2 * 32 + D
HN = H // 4
E1, TOPK, CAP, FF1 = 64, 8, 128, 192
NT = TOK // P
ZW = H + E1
EPS = 1e-5
CREDIT = 12


def level(m, per=1):
    return (m + 1 + CREDIT) * per


def wait_moved(eng, sem, m, per):
    if not isinstance(m, int) or m >= 0:
        eng.wait_ge(sem, (m + 1) * per)


def settle(eng, tally):
    eng.sem_inc(tally, 1)


def build(nc, t):
    ctx = ExitStack()
    credited = []

    def sb(name, shape, dt=F32):
        return ctx.enter_context(nc.sbuf_tensor(name, shape, dt))

    def sem(name, per=1):
        s = ctx.enter_context(nc.semaphore(name))
        if per:
            credited.append((s, per))
        return s

    out = t["out"]
    x_rows = t["x"].rearrange("b s h -> (b s) h")
    n0_rows = nc.dram_tensor("n0_rows", (TOK, H), F32, kind="Internal").ap()
    x1_rows = nc.dram_tensor("x1_rows", (TOK, H), F32, kind="Internal").ap()
    odd_rows = nc.dram_tensor("odd_rows", (TOK + P, H), F32, kind="Internal").ap()
    z_rows = nc.dram_tensor("z_rows", (TOK + P, ZW), F32, kind="Internal").ap()

    with ctx:
        ident = sb("ident", [P, P])
        iota_f = sb("iota_f", [P, P])
        iota_p = sb("iota_p", [P, 1])
        dummy_row = sb("dummy_row", [P, 1])
        tri = sb("tri", [P, P], BF16)
        before = sb("before", [NT, NT], BF16)
        mhalf = sb("mhalf", [P, TT])
        rowbase = sb("rowbase", [P, 1], I32)
        rowbase_f = sb("rowbase_f", [P, 1])
        zeros = sb("zeros", [P, TOK // 4 * H // P])
        wg0 = sb("wg0", [P, CT, E0])
        gam0 = sb("gam0", [P, B, CT])
        bet0 = sb("bet0", [P, B, CT])
        b1_0 = sb("b1_0", [P, E0, FT0])
        wg1 = sb("wg1", [P, 2 * CT, H])
        wsoma = sb("wsoma", [P, CT, H])
        wtemp = sb("wtemp", [P, CT, H])
        wout = sb("wout", [P, CT, H])
        wn1 = sb("wn1", [P, CT, HN])
        wn2 = sb("wn2", [HN, D])
        wn2_3 = sb("wn2_3", [HN, MR])
        spread = sb("spread", [MR, D, P], BF16)
        router = sb("router", [P, CT, E1])
        ws_gu = sb("ws_gu", [P, CT, 2 * FF1])
        ws_da = sb("ws_da", [P, H])
        ws_db = sb("ws_db", [FF1 - P, H])
        bg_h = sb("bg_h", [P, CT])
        btemp_h = sb("btemp_h", [P, CT])
        bsoma = sb("bsoma", [P, CT])
        bn1 = sb("bn1", [HN, 1])
        bn2_h = sb("bn2_h", [MR, 1])
        gam1 = sb("gam1", [P, CT])
        bet1 = sb("bet1", [P, CT])
        tau = sb("tau", [P, D + 1])
        alpha = sb("alpha", [P, D + 1])
        blend = sb("blend", [P, CT, D])
        blend_m = sb("blend_m", [P, CT])
        blend_s = sb("blend_s", [P, CT])
        mask_all = sb("mask_all", [P, E1, NT], BF16)
        Rx = sb("Rx", [NT, 4, P + 3], BF16)

        layer0 = ExitStack()
        outer, ctx_of = ctx, [layer0]

        def sb(name, shape, dt=F32):
            return ctx_of[0].enter_context(nc.sbuf_tensor(name, shape, dt))

        w1s = sb("w1s", [P, CT * FF0])
        w2s = sb("w2s", [P, FT0 * H])
        w1_hi = [sb(f"w1_hi{p}", [P, CT * FF0], F32R) for p in range(2)]
        w1_lo = [sb(f"w1_lo{p}", [P, CT * FF0], F32R) for p in range(2)]
        w2_hi = [sb(f"w2_hi{p}", [P, FT0 * H], F32R) for p in range(2)]
        w2_lo = [sb(f"w2_lo{p}", [P, FT0 * H], F32R) for p in range(2)]
        b2r = [sb(f"b2r{p}", [P, H]) for p in range(2)]
        idxT = sb("idxT", [P, B, E0], I32)
        gateT = sb("gateT", [P, B, E0])
        adapter = ExitStack()
        ctx_of[0] = adapter
        xt = [sb(f"xt{p}", [P, TT, H]) for p in range(2)]
        w1c = [sb(f"w1c{p}", [P, CT, AD]) for p in range(2)]
        w2c = [sb(f"w2c{p}", [AD + 1, H]) for p in range(2)]
        b1c = [sb(f"b1c{p}", [AD, 1]) for p in range(2)]
        xT = sb("xT", [P, CT, S])
        hT = sb("hT", [AD + 1, S])
        y = [sb(f"y{p}", [P, TT, H]) for p in range(2)]
        stat = sb("stat", [P, TT, 6])
        mv = [sb(f"mv{p}", [P, TT, 2]) for p in range(2)]
        veps = sb("veps", [P, TT])
        rstd = [sb(f"rstd{p}", [P, TT]) for p in range(2)]
        nrm = [sb(f"nrm{p}", [P, TT, H]) for p in range(2)]
        yT = sb("yT", [P, CT, S])
        lg0 = sb("lg0", [P, B, TT, E0])
        red0 = sb("red0", [P, B * TT])
        prob = sb("prob", [P, TT, B * E0])
        ranks = sb("ranks", [B * E0, S])
        gval = sb("gval", [B * E0, K0])
        gidx = sb("gidx", [B * E0, K0], U32)
        gidx_f = sb("gidx_f", [B * E0, K0])
        adapter.close()
        ctx_of[0] = layer0
        take = [sb(f"take{p}", [P, 4], I32) for p in range(2)]
        put = [sb(f"put{p}", [P, 4], I32) for p in range(2)]
        xg0 = [sb(f"xg0_{p}", [P, 4, H]) for p in range(2)]
        ex_raw = sb("ex_raw", [P, CT, S])
        ex_hi = [sb(f"ex_hi{p}", [P, CT, S], F32R) for p in range(2)]
        ex_lo = [sb(f"ex_lo{p}", [P, CT, S], F32R) for p in range(2)]
        h1_raw = [sb(f"h1_raw{p}", [P, S]) for p in range(4)]
        h1_hi = sb("h1_hi", [P, FT0, S], F32R)
        h1_lo = sb("h1_lo", [P, FT0, S], F32R)
        ob = [sb(f"ob{p}", [P, 4, H]) for p in range(2)]
        layer0.close()
        ctx_of[0] = outer
        x1t = [sb(f"x1t{p}", [P, TT, H]) for p in range(2)]
        x1T = sb("x1T", [P, CT, S])
        ctxT = sb("ctxT", [P, CT, S])
        wgt = sb("wgt", [P, CT, S])
        gated2 = [sb(f"gated2_{p}", [P, CT, S]) for p in range(2)]
        h1T = sb("h1T", [HN, S])
        t8 = sb("t8", [MR, S])
        m8 = sb("m8", [MR, S])
        rest = sb("rest", [MR, S])
        parts = [sb(f"parts{p}", [MR, S], BF16) for p in range(2)]
        soma = [sb(f"soma{p}", [P, CT, S]) for p in range(2)]
        md = [sb(f"md{p}", [P, S]) for p in range(2)]
        drive = [sb(f"drive{p}", [P, CT, S]) for p in range(4)]
        trace = [sb(f"trace{p}", [P, CT, S]) for p in range(2)]
        acc = [sb(f"acc{p}", [P, CT, S]) for p in range(2)]
        gt = sb("gt", [P, CT, S])
        prodT = sb("prodT", [P, CT, S])
        stat1 = sb("stat1", [P, TT, 6])
        mv1 = sb("mv_b", [P, TT, 2])
        veps1 = sb("veps1", [P, TT])
        rstd1 = sb("rstd_b", [P, TT])
        zrow = sb("zrow", [P, TT, ZW])
        zT = sb("zT", [P, CT, S])
        top8 = sb("top8", [P, TT, 8])
        rep = sb("rep", [P, TT, E1])
        neg = sb("neg", [P, TT, E1])
        mask = sb("mask", [P, TT, E1])
        ex = sb("ex", [P, TT, E1])
        wsum = sb("wsum", [P, TT])
        sgA = sb("sgA", [P, S])
        sgB = sb("sgB", [FF1 - P, S])
        hsA = sb("hsA", [P, S])
        hsB = sb("hsB", [FF1 - P, S])
        xr = sb("xr", [P, TT, H])
        ost = sb("ost", [P, TT, H])
        mstat = sb("mstat", [P, 4, NT], BF16)
        Bf = sb("Bf", [NT, 4])
        Bn = sb("Bn", [NT, 4])
        ge = sb("ge", [NT, 4, P], BF16)
        lt = sb("lt", [NT, 4, P], BF16)
        sel = sb("sel", [NT, 4, P], BF16)
        meta = sb("meta", [P, 4, 3])
        cb = sb("cb", [P, 4])
        cmp = sb("cmp", [P, 4, P])
        pos = sb("pos", [P, 4])
        slot_f = sb("slot_f", [P, 4])
        slot_g = sb("slot_g", [P, 4])
        slots = sb("slots", [P, E1], I32)
        gi = [sb(f"gi{i}", [P, 1], I32) for i in range(4)]
        xg1 = [sb(f"xg1_{i}", [P, ZW]) for i in range(4)]
        xgT = [sb(f"xgT{p}", [P, CT, P]) for p in range(2)]
        wgr = [sb(f"wgr{i}", [P, CT, FF1]) for i in range(4)]
        wur = [sb(f"wur{i}", [P, CT, FF1]) for i in range(4)]
        wda = [sb(f"wda{i}", [P, H]) for i in range(4)]
        wdb = [sb(f"wdb{i}", [FF1 - P, H]) for i in range(4)]
        sg1 = [sb(f"sg1_{p}", [P, 2, P]) for p in range(2)]
        he = [sb(f"he{p}", [P, 2, P]) for p in range(2)]
        ys = [sb(f"ys{i}", [P, H]) for i in range(4)]
        pi = [sb(f"pi{i}", [P, 1], I32) for i in range(4)]
        share = [sb(f"share{i}", [P, 1]) for i in range(4)]

        bank = ctx.enter_context(nc.psum_tensor("bank", [P, 8, 512], F32))

        def two(n):
            return bank[:, n:n + 2, :]

        def rows4(n):
            return bank[:, n:n + 2, :].rearrange("p k (j c) -> p (k j) c", c=H)

        FR = FF1 - P
        RB = FR

        loaded0 = sem("loaded0", 0)
        loaded1 = sem("loaded1", 0)
        x1_set = sem("x1_set", 0)
        z_dummy = sem("z_dummy", 0)
        zeros_set = sem("zeros_set", 0)
        consts = sem("consts", 0)
        tally = sem("tally", 0)
        prep1 = sem("prep1", 0)
        prep1a = sem("prep1a", 0)
        N_CONST0 = 2

        a_in = [sem(f"a_in{p}", 16 * 7) for p in range(2)]
        a_stored = [sem(f"a_stored{p}", 16) for p in range(2)]
        a_xTm, a_xT, a_hm, a_h, a_ad, a_y, a_mv, a_rstd, a_nrm, a_nT, a_yT, a_lgm, a_lg = (
            sem("a_" + n) for n in ("xTm", "xT", "hm", "h", "ad", "y", "mv", "rstd", "nrm", "nT", "yT", "lgm", "lg"))

        k_sub, k_exp, k_prob, k_pT, k_sel, k_idx, k_tab = (
            sem("k_" + n, 0) for n in ("sub", "exp", "prob", "pT", "sel", "idx", "tab"))

        b_w1, b_w2 = sem("b_w1", 16), sem("b_w2", 32)
        b_w1h, b_w1l, b_w2h, b_w2l = sem("b_w1h"), sem("b_w1l"), sem("b_w2h"), sem("b_w2l")
        b_hi, b_lo, b_xraw = sem("b_hi"), sem("b_lo"), sem("b_xraw")
        b_got = [sem(f"b_got{p}", 0) for p in range(2)]
        b_put = [sem(f"b_put{p}", 0) for p in range(2)]
        b_take, b_place, e_gi, e_pi = sem("b_take"), sem("b_place"), sem("e_gi"), sem("e_pi")
        b_T, b_exT, b_hm, b_h, b_o, b_oa, b_out = (
            sem("b_" + n) for n in ("T", "exT", "hm", "h", "o", "oa", "out"))

        c_r1, c_r2, c_sp2 = sem("c_r1"), sem("c_r2"), sem("c_sp2")
        c_m8, c_t8, c_sp, c_cut, c_scan = (sem("c_" + n) for n in ("m8", "t8", "sp", "cut", "scan"))
        c_in = [sem(f"c_in{p}", 16) for p in range(2)]
        c_xr, c_zst, c_ost = sem("c_xr", 16), sem("c_zst", 16), sem("c_ost", 16)
        (c_Tm, c_x1T, c_ctx, c_wgm, c_wgt, c_gat, c_h1m, c_h1, c_som, c_so, c_mm, c_md, c_u, c_acc,
         c_tem, c_gt, c_pr, c_om, c_mv, c_rs, c_no, c_zm, c_zT, c_lgm, c_neg, c_ex, c_top, c_zr,
         c_bm, c_bt, c_hsB, c_am, c_at, c_hsA, c_dm, c_fin) = (
            sem("c_" + n) for n in (
                "Tm", "x1T", "ctx", "wgm", "wgt", "gat", "h1m", "h1", "som", "so", "mm", "md", "u", "acc",
                "tem", "gt", "pr", "om", "mv", "rs", "no", "zm", "zT", "lgm", "neg", "ex", "top", "zr",
                "bm", "bt", "hsB", "am", "at", "hsA", "dm", "fin"))

        e_w = [sem(f"e_w{i}", 64) for i in range(4)]
        e_got = [sem(f"e_got{i}", 0) for i in range(4)]
        e_put = [sem(f"e_put{p}", 0) for p in range(2)]
        e_sum = sem("e_sum", 0)
        (e_ms, e_R, e_Rc, e_B, e_S, e_G, e_slot, e_T, e_xT, e_gu, e_sg, e_h, e_d, e_ys) = (
            sem("e_" + n) for n in ("ms", "R", "Rc", "B", "S", "G", "slot", "T", "xT", "gu", "sg", "h", "d", "ys"))

        block = ctx.enter_context(nc.Block())

        def prev(h, p):
            return (h, 0) if p else (h - 1, 1)

        def nxt(h, p):
            return (h + 1, 0) if p else (h, 1)

        def staggered(eng, front, both, back):
            front(0, 0)
            with eng.Fori(0, B // 2 - 1) as i:
                both(i, 1)
                both(i + 1, 0)
            both(B // 2 - 1, 1)
            back(B // 2 - 1, 1)

        def experts(eng, group):
            n = E1 // 4
            group(0, True, True, False)
            with eng.Fori(1, n - 2) as k:
                group(k, True, False, False)
            group(n - 2, False, False, False)
            group(n - 1, False, False, True)

        def ffn(eng, group):
            group(0, False)
            with eng.Fori(1, E0 // 2 - 1) as g:
                group(g, False)
            group(E0 // 2 - 1, True)

        def ahead(work, b, p, d, front, middle):
            if d < D - 2:
                if middle:
                    work(b, p, d + 2)
            elif front:
                work(b + 1, 1 - p, d + 2 - D)

        def conditioning(eng, first, step):
            first()
            step(0, 0, True, True, True, False, False)
            step(0, 1, True, True, True, True, False)
            with eng.Fori(1, B // 2 - 1) as i:
                step(i, 0, True, True, True, True, True)
                step(i, 1, True, True, True, True, True)
            step(B // 2 - 1, 0, False, True, True, True, True)
            step(B // 2 - 1, 1, False, False, True, True, True)
            step(B // 2, 0, False, False, False, True, True)
            step(B // 2, 1, False, False, False, False, True)

        @block.sync
        def _(sp):
            def a_load(h, p):
                b = 2 * h + p
                sp.wait_ge(a_y, level(b - 2))
                settle(sp, tally)
                lang = sp.value_load(t["ids"][0:1, bass.ds(b, 1)], min_val=0, max_val=LANGS - 1)
                sp.dma_start(xt[p][:, :, :], x_rows[bass.ds(b * S, S), :].rearrange("(t p) c -> p t c", p=P)).then_inc(a_in[p], 16)
                sp.dma_start(w1c[p][:, :, :], t["aW1"].rearrange("l (c p) a -> l p c a", p=P)[bass.ds(lang, 1), :, :, :].rearrange("l p c a -> (l p) c a")).then_inc(a_in[p], 16)
                sp.dma_start(w2c[p][0:AD, :], t["aW2"][bass.ds(lang, 1), :, :].rearrange("l a c -> (l a) c")).then_inc(a_in[p], 16)
                sp.dma_start(w2c[p][AD:AD + 1, :], t["ab2"][bass.ds(lang, 1), :]).then_inc(a_in[p], 16)
                sp.dma_start(b1c[p][:, :], t["ab1"][bass.ds(lang, 1), :].rearrange("l a -> a l")).then_inc(a_in[p], 16)
                sp.dma_start(gam0[:, bass.ds(b, 1), :].rearrange("p b c -> p (b c)"), t["agam"][bass.ds(lang, 1), :, :].rearrange("l p c -> (l p) c")).then_inc(a_in[p], 16)
                sp.dma_start(bet0[:, bass.ds(b, 1), :].rearrange("p b c -> p (b c)"), t["abet"][bass.ds(lang, 1), :, :].rearrange("l p c -> (l p) c")).then_inc(a_in[p], 16)

            def a_store(h, p):
                b = 2 * h + p
                sp.wait_ge(a_nrm, level(b))
                sp.dma_start(n0_rows[bass.ds(b * S, S), :].rearrange("(t p) c -> p t c", p=P), nrm[p][:, :, :]).then_inc(a_stored[p], 16)

            def a_both(h, p):
                a_load(h, p)
                a_store(*prev(h, p))

            staggered(sp, a_load, a_both, a_store)

            def b_load(g, last):
                for q in range(2):
                    e = 2 * g + q
                    sp.wait_ge(b_w1l, level(e - 1))
                    sp.dma_start(w1s[:, :].rearrange("p (c f) -> p c f", c=CT), t["fW1"].rearrange("e (c p) f -> e p c f", p=P)[bass.ds(e, 1), :, :, :].rearrange("e p c f -> (e p) c f")).then_inc(b_w1, 16)
                    sp.wait_ge(b_w2l, level(e - 1))
                    sp.wait_ge(b_oa, level(2 * (e - 2) + 1))
                    sp.dma_start(w2s[:, :].rearrange("p (f c) -> p f c", c=H), t["fW2"].rearrange("e (f p) c -> e p f c", p=P)[bass.ds(e, 1), :, :, :].rearrange("e p f c -> (e p) f c")).then_inc(b_w2, 16)
                    sp.dma_start(b2r[q][:, :], t["fb2"][bass.ds(e, 1), :].to_broadcast([P, H])).then_inc(b_w2, 16)

            ffn(sp, b_load)

            for p in range(2):
                wait_moved(sp, b_put[p], E0 - 1, 64)

            def c_load(h, p):
                b = 2 * h + p
                sp.wait_ge(c_Tm, level(b - 2))
                sp.dma_start(x1t[p][:, :, :], x1_rows[bass.ds(b * S, S), :].rearrange("(t p) c -> p t c", p=P)).then_inc(c_in[p], 16)

            def c_first():
                c_load(0, 0)
                c_load(0, 1)

            def c_step(h, p, load, front, middle, gate, share):
                b = 2 * h + p
                if load:
                    c_load(h + 1, p)
                if share:
                    q = b - 2
                    sp.wait_ge(c_fin, level(q - 1))
                    sp.dma_start(xr[:, :, :], x1_rows[bass.ds(q * S, S), :].rearrange("(t p) c -> p t c", p=P)).then_inc(c_xr, 16)
                    sp.wait_ge(c_zr, level(q))
                    sp.dma_start(z_rows[bass.ds(q * S, S), :].rearrange("(t p) c -> p t c", p=P), zrow[:, :, :]).then_inc(c_zst, 16)
                    sp.wait_ge(c_fin, level(q))
                    sp.dma_start(out[bass.ds(q * S, S), :].rearrange("(t p) c -> p t c", p=P), ost[:, :, :]).then_inc(c_ost, 16)

            conditioning(sp, c_first, c_step)

            def e_load(k):
                for i in range(4):
                    e = 4 * k + i
                    sp.wait_ge(e_d, level(e - 4))
                    sp.dma_start(wgr[i][:, :, :], t["mwg"].rearrange("e (c p) f -> e p c f", p=P)[bass.ds(e, 1), :, :, :].rearrange("e p c f -> (e p) c f")).then_inc(e_w[i], 16)
                    sp.dma_start(wur[i][:, :, :], t["mwu"].rearrange("e (c p) f -> e p c f", p=P)[bass.ds(e, 1), :, :, :].rearrange("e p c f -> (e p) c f")).then_inc(e_w[i], 16)
                    sp.dma_start(wda[i][:, :], t["mwd"][bass.ds(e, 1), 0:P, :].rearrange("e f c -> (e f) c")).then_inc(e_w[i], 16)
                    sp.dma_start(wdb[i][:, :], t["mwd"][bass.ds(e, 1), P:FF1, :].rearrange("e f c -> (e f) c")).then_inc(e_w[i], 16)

            with sp.Fori(0, E1 // 4) as k:
                e_load(k)
            sp.wait_ge(e_sum, 16)

        @block.gpsimd
        def _(pool):
            G = nc.gpsimd
            for s, per in credited:
                pool.sem_inc(s, CREDIT * per)
            G.memset(bn2_h[:, :], 0.0)
            G.memset(zeros[:, :], 0.0).then_inc(zeros_set, 1)
            pool.drain()
            G.memset(ident[:, :], 0.0)
            pool.drain()
            G.memset(tri[:, :], 1.0)
            pool.drain()
            G.memset(before[:, :], 1.0)
            pool.drain()
            G.memset(spread[:, :, :], 0.0)
            pool.drain()
            G.memset(mhalf[:, :], -0.5)
            pool.drain()
            G.memset(hT[AD:AD + 1, :], 1.0)
            pool.drain()
            G.iota(iota_f[:, :], [[1, P]], base=0, channel_multiplier=0, allow_small_or_imprecise_dtypes=True)
            pool.drain()
            G.iota(iota_p[:, :], [[0, 1]], base=0, channel_multiplier=1, allow_small_or_imprecise_dtypes=True)
            pool.drain()
            G.iota(dummy_row[:, :], [[0, 1]], base=TOK, channel_multiplier=1, allow_small_or_imprecise_dtypes=True)
            pool.drain()
            G.iota(rowbase[:, :], [[0, 1]], base=0, channel_multiplier=S // E0)
            pool.drain()
            G.memset(Rx[:, :, P + 2], 1.0)
            pool.drain()
            G.iota(Rx[:, :, P + 1], [[0, 4]], base=0, channel_multiplier=P, allow_small_or_imprecise_dtypes=True)
            pool.drain()
            G.affine_select(out=ident[:, :], in_=ident[:, :], compare_op=ALU.not_equal, fill=1.0, base=0,
                            pattern=[[-1, P]], channel_multiplier=1)
            pool.drain()
            G.affine_select(out=tri[:, :], in_=tri[:, :], compare_op=ALU.is_ge, fill=0.0, base=0,
                            pattern=[[1, P]], channel_multiplier=-1)
            pool.drain()
            G.affine_select(out=before[:, :], in_=before[:, :], compare_op=ALU.is_ge, fill=0.0, base=-1,
                            pattern=[[1, NT]], channel_multiplier=-1)
            for part in range(3):
                pool.drain()
                G.affine_select(out=spread[:, :, :], in_=spread[:, :, :], compare_op=ALU.not_equal, fill=1.0,
                                base=-32 * part, pattern=[[-1, D], [0, P]], channel_multiplier=1)
            pool.drain().then_inc(consts, 1)

            def a_pow(h, p):
                b = 2 * h + p
                pool.wait_ge(a_mv, level(b))
                pool.wait_ge(a_nrm, level(b - 2))
                settle(pool, tally)
                G.tensor_scalar(veps[:, :], mv[p][:, :, 1], EPS, None, ALU.add)
                pool.drain()
                G.tensor_tensor(rstd[p][:, :], veps[:, :], mhalf[:, :], ALU.pow).then_inc(a_rstd, 1)
                pool.drain()

            with pool.Fori(0, B // 2) as i:
                a_pow(i, 0)
                a_pow(i, 1)

            pool.wait_ge(k_tab, 1)
            pool.wait_ge(x1_set, 16)
            for p in range(2):
                pool.wait_ge(a_stored[p], level(B // 2 - 1, 16))

            def b_gather(g, r):
                p, e, s = r & 1, 2 * g + (r >> 1), 4 * g + r
                pool.wait_ge(b_T, level(s - 2))
                settle(pool, tally)
                G.tensor_copy(take[p][:, :], idxT[:, 4 * p:4 * p + 4, bass.ds(e, 1)].rearrange("p b e -> p (b e)")).then_inc(b_take, 1)
                pool.wait_ge(b_take, level(s))
                settle(pool, tally)
                for j in range(4):
                    G.indirect_dma_start(xg0[p][:, j, :], None, n0_rows[:, :],
                                         bass.IndirectOffsetOnAxis(ap=take[p][:, j:j + 1], axis=0)).then_inc(b_got[p], 16)

            def b_scatter(g, r):
                p, e, s = r & 1, 2 * g + (r >> 1), 4 * g + r
                pool.wait_ge(b_out, level(s))
                wait_moved(pool, b_put[p], e - 1, 64)
                settle(pool, tally)
                G.tensor_copy(put[p][:, :], idxT[:, 4 * p:4 * p + 4, bass.ds(e, 1)].rearrange("p b e -> p (b e)")).then_inc(b_place, 1)
                pool.wait_ge(b_place, level(s))
                settle(pool, tally)
                for j in range(4):
                    G.indirect_dma_start(x1_rows[:, :], bass.IndirectOffsetOnAxis(ap=put[p][:, j:j + 1], axis=0),
                                         ob[p][:, j, :], None, compute_op=ALU.add).then_inc(b_put[p], 16)

            def b_group(g, last):
                for r in range(4):
                    if r < 2:
                        b_gather(g, r + 2)
                    elif not last:
                        b_gather(g + 1, r - 2)
                    b_scatter(g, r)

            b_gather(0, 0)
            b_gather(0, 1)
            ffn(pool, b_group)

            def rstd_of(q):
                pool.wait_ge(c_mv, level(q))
                pool.wait_ge(c_no, level(q - 1))
                settle(pool, tally)
                G.tensor_scalar(veps1[:, :], mv1[:, :, 1], 4 * EPS, None, ALU.add)
                pool.drain()
                G.tensor_tensor(rstd1[:, :], veps1[:, :], mhalf[:, :], ALU.pow).then_inc(c_rs, 1)

            def first_rest(n, pn):
                pool.wait_ge(c_sp, level(n))
                G.tensor_tensor(rest[:, :], m8[:, :], parts[pn][:, :], ALU.subtract).then_inc(c_r1, 1)

            def second_rest(n, pn):
                pool.wait_ge(c_sp2, level(n))
                settle(pool, tally)
                pool.drain()
                G.tensor_tensor(rest[64:MR, :], rest[64:MR, :], parts[pn][64:MR, :], ALU.subtract).then_inc(c_r2, 1)
                pool.drain()

            def drive_of(b, p, d):
                pool.wait_ge(c_md, level(D * b + d))
                pool.wait_ge(c_gat, level(b))
                pool.wait_ge(c_scan, level(D * b + d - 4))
                G.tensor_tensor(drive[d % 4][:, :, :], gated2[p][:, :, :],
                                md[d % 2][:, :].unsqueeze(1).to_broadcast([P, CT, S]), ALU.mult).then_inc(c_u, 1)

            def step(h, p, load, front, middle, gate, share):
                b = 2 * h + p
                for d in range(D):
                    ahead(drive_of, b, p, d, front, middle)
                    if d == 2 and front:
                        first_rest(b + 1, 1 - p)
                    if d == 3 and front:
                        second_rest(b + 1, 1 - p)
                    if d == 4 and gate:
                        rstd_of(b - 1)

            def front_only():
                first_rest(0, 0)
                second_rest(0, 0)
                drive_of(0, 0, 0)
                drive_of(0, 0, 1)

            conditioning(pool, front_only, step)

            pool.wait_ge(z_dummy, 16 * 6)
            pool.wait_ge(c_zst, level(B - 1, 16))
            pool.wait_ge(c_ost, level(B - 1, 16))

            def e_gather(k, i):
                e = 4 * k + i
                pool.wait_ge(e_slot, level(k))
                pool.wait_ge(e_xT, level(e - 4))
                settle(pool, tally)
                G.tensor_copy(gi[i][:, :], slots[:, bass.ds(e, 1)]).then_inc(e_gi, 1)
                pool.wait_ge(e_gi, level(e))
                settle(pool, tally)
                G.indirect_dma_start(xg1[i][:, :], None, z_rows[:, :],
                                     bass.IndirectOffsetOnAxis(ap=gi[i][:, :], axis=0)).then_inc(e_got[i], 16)

            def e_scatter(k, i):
                e = 4 * k + i
                pool.wait_ge(e_ys, level(e))
                wait_moved(pool, e_put[i % 2], 2 * k + i // 2 - 1, 16)
                G.tensor_copy(pi[i][:, :], slots[:, bass.ds(e, 1)]).then_inc(e_pi, 1)
                pool.wait_ge(e_pi, level(e))
                settle(pool, tally)
                G.indirect_dma_start((out, odd_rows)[i % 2][:, :], bass.IndirectOffsetOnAxis(ap=pi[i][:, :], axis=0),
                                     ys[i][:, :], None, compute_op=ALU.add).then_inc(e_put[i % 2], 16)

            def e_group(k, prepare, first, last):
                for i in range(4):
                    if i < 1:
                        e_gather(k, i + 3)
                    elif not last:
                        e_gather(k + 1, i - 1)
                    if i > 1:
                        e_scatter(k, i - 2)
                    elif not first:
                        e_scatter(k - 1, i + 2)

            for i in range(3):
                e_gather(0, i)
            experts(pool, e_group)
            e_scatter(E1 // 4 - 1, 2)
            e_scatter(E1 // 4 - 1, 3)
            for p in range(2):
                wait_moved(pool, e_put[p], E1 // 2 - 1, 16)
            pool.dma_start(out[0:TOK, :].rearrange("(a r) c -> a (r c)", a=P),
                           odd_rows[0:TOK, :].rearrange("(a r) c -> a (r c)", a=P),
                           accum_op=ALU.add, max_dma_last_dim=8192).then_inc(e_sum, 16)

        @block.scalar
        def _(act):
            A = nc.scalar
            act.dma_start(wg0[:, :, :], t["fWgT"].rearrange("(c p) e -> p c e", p=P)).then_inc(loaded0, 16)
            act.dma_start(b1_0[:, :, :], t["fb1"]).then_inc(loaded0, 16)
            def a_front(h, p):
                b = 2 * h + p
                act.wait_ge(a_xTm, level(b))
                act.wait_ge(a_hm, level(b - 1))
                A.activation(xT[:, :, :], two(0), ACT.Copy).then_inc(a_xT, 1)
                act.wait_ge(a_hm, level(b))
                act.wait_ge(a_ad, level(b - 1))
                A.activation(hT[0:AD, :], bank[0:AD, 2, :], ACT.Relu, bias=b1c[p][:, :]).then_inc(a_h, 1)

            def a_back(h, p):
                b = 2 * h + p
                act.wait_ge(a_nT, level(b))
                act.wait_ge(a_lgm, level(b - 1))
                settle(act, tally)
                for c in range(CT):
                    o = A.activation(yT[:, c, :], bank[:, 5 + c, :], ACT.Identity,
                                     bias=bet0[:, bass.ds(b, 1), c], scale=gam0[:, bass.ds(b, 1), c])
                o.then_inc(a_yT, 1)

            def a_both(h, p):
                a_front(h, p)
                a_back(*prev(h, p))

            staggered(act, a_front, a_both, a_back)

            act.dma_start(x1_rows.rearrange("(a r) c -> a (r c)", a=P), x_rows.rearrange("(a r) c -> a (r c)", a=P)).then_inc(x1_set, 16)
            act.wait_ge(zeros_set, 1)
            act.dma_start(z_rows[TOK:TOK + P, :], zeros[:, 0:ZW]).then_inc(z_dummy, 16)
            for n in range(4):
                rows = odd_rows[n * TOK // 4:(n + 1) * TOK // 4, :]
                act.dma_start(rows.rearrange("(a r) c -> a (r c)", a=P), zeros[:, :]).then_inc(z_dummy, 16)
            act.dma_start(odd_rows[TOK:TOK + P, :], zeros[:, 0:H]).then_inc(z_dummy, 16)
            n = 0
            for dst, src in (
                    (wg1[:, :, :], t["cWgT"].rearrange("(c p) e -> p c e", p=P)),
                    (wsoma[:, :, :], t["cWsomaT"].rearrange("(c p) e -> p c e", p=P)),
                    (wtemp[:, :, :], t["cWtempT"].rearrange("(c p) e -> p c e", p=P)),
                    (wout[:, :, :], t["cWoutT"].rearrange("(c p) e -> p c e", p=P)),
                    (wn1[:, :, :], t["cWn1T"].rearrange("(c p) e -> p c e", p=P)),
                    (wn2[:, :], t["cWn2T"]),
                    (router[:, :, :], t["routerT"].rearrange("(c p) e -> p c e", p=P)),
                    (ws_gu[:, :, :], t["wsgu"].rearrange("(c p) e -> p c e", p=P)),
                    (ws_da[:, :], t["wsd"][0:P, :]),
                    (ws_db[:, :], t["wsd"][P:FF1, :]),
                    (bg_h[:, :], t["cbg"]),
                    (btemp_h[:, :], t["cbtemp"]),
                    (bsoma[:, :], t["cbsoma"]),
                    (bn1[:, :], t["cbn1"].rearrange("(a o) -> a o", o=1)),
                    (bn2_h[0:D, :], t["cbn2"].rearrange("(d o) -> d o", o=1)),
                    (bn2_h[32:32 + D, :], t["cbn2"].rearrange("(d o) -> d o", o=1)),
                    (bn2_h[64:64 + D, :], t["cbn2"].rearrange("(d o) -> d o", o=1)),
                    (gam1[:, :], t["cgam"]),
                    (bet1[:, :], t["cbet"]),
                    (tau[:, 0:D], t["tau"].rearrange("(o d) -> o d", o=1).to_broadcast([P, D])),
                    (tau[:, D:D + 1], t["tau_ctx"].rearrange("(o d) -> o d", o=1).to_broadcast([P, 1])),
                    (blend[:, :, :], t["blendT"].rearrange("(c p) d -> p c d", p=P))):
                act.dma_start(dst, src).then_inc(loaded1, 16)
                n += 1
            assert n == N_LOADED1

            for first in (True, False):
                src, dst, came, split = ((w1s, w1_hi, b_w1, b_w1h) if first else (w2s, w2_hi, b_w2, b_w2h))
                act.wait_ge(came, level(0, 16 if first else 32))
                for n in range(4):
                    A.activation(dst[0][:, n * 512:(n + 1) * 512], src[:, n * 512:(n + 1) * 512], ACT.Copy).then_inc(split, 1)

            act.wait_ge(k_sub, 1)
            A.activation(lg0[:, :, :, :], lg0[:, :, :, :], ACT.Exp).then_inc(k_exp, 1)

            WC = CT * FF0 // 4

            def w_hi(e, q, first, n):
                src, dst, came, split, used = ((w1s, w1_hi, b_w1, b_w1h, b_hm) if first else
                                               (w2s, w2_hi, b_w2, b_w2h, b_o))
                if n == 0:
                    act.wait_ge(came, level(e, 16 if first else 32))
                    act.wait_ge(used, level(8 * (2 * (e - 2) + 1) + 7) if first else level(2 * (e - 2) + 1))
                o = A.activation(dst[q][:, n * WC:(n + 1) * WC], src[:, n * WC:(n + 1) * WC], ACT.Copy)
                o.then_inc(split, 1)

            def b_group(g, last):
                for r in range(4):
                    s, e, p, q = 4 * g + r, 2 * g + (r >> 1), r & 1, r >> 1
                    act.wait_ge(b_o, level(s - 1))
                    for f in range(FT0 + 1):
                        if f < FT0:
                            act.wait_ge(b_hm, level(8 * s + f))
                            act.wait_ge(b_lo, level(8 * s + f - 4))
                            settle(act, tally)
                            A.activation(h1_raw[f % 4][:, :], bank[:, 2 + f % 4, :], ACT.Gelu_apprx_tanh,
                                         bias=b1_0[:, bass.ds(e, 1), f]).then_inc(b_h, 1)
                        if f:
                            act.wait_ge(b_h, level(8 * s + f - 1))
                            A.activation(h1_hi[:, f - 1, :], h1_raw[(f - 1) % 4][:, :], ACT.Copy).then_inc(b_hi, 1)
                    if not (last and q == 1):
                        for n in range(4):
                            w_hi(e + 1, 1 - q, p == 0, n)

            ffn(act, b_group)

            act.wait_ge(prep1a, 1)
            A.activation(alpha[:, :], tau[:, :], ACT.Exp)
            A.activation(blend[:, :, :], blend[:, :, :], ACT.Exp)
            act.drain().then_inc(prep1, 1)

            def mod(b, p, d):
                act.wait_ge(c_mm, level(D * b + d))
                act.wait_ge(c_u, level(D * b + d - 2))
                A.activation(md[d % 2][:, :], bank[:, 6 + d % 2, :], ACT.Copy).then_inc(c_md, 1)

            def x1T_out(n):
                act.wait_ge(c_Tm, level(n))
                act.wait_ge(c_som, level(n - 1))
                act.wait_ge(c_gat, level(n - 1))
                A.activation(x1T[:, :, :], two(4), ACT.Copy).then_inc(c_x1T, 1)

            def wg_out(n):
                act.wait_ge(c_wgm, level(n))
                act.wait_ge(c_gat, level(n - 1))
                for c in range(CT):
                    o = A.activation(wgt[:, c, :], bank[:, 2 + c, :], ACT.Tanh, bias=bg_h[:, c:c + 1], scale=0.5)
                o.then_inc(c_wgt, 1)

            def h1_out(n):
                act.wait_ge(c_h1m, level(n))
                act.wait_ge(c_m8, level(n - 1))
                A.activation(h1T[:, :], bank[0:HN, 4, :], ACT.Gelu, bias=bn1[:, :]).then_inc(c_h1, 1)

            def t8_out(n, pn):
                act.wait_ge(c_m8, level(n))
                act.wait_ge(c_cut, level(n - 1))
                A.activation(t8[:, :], bank[0:MR, 4, :], ACT.Tanh, bias=bn2_h[:, :], scale=0.5).then_inc(c_t8, 1)
                act.drain()
                A.activation(m8[:, :], t8[:, :], ACT.Copy, bias=2.0)
                act.drain()
                act.wait_ge(c_mm, level(D * (n - 2) + D - 1))
                A.activation(parts[pn][:, :], m8[:, :], ACT.Copy).then_inc(c_sp, 1)

            def second_part(n, pn):
                act.wait_ge(c_r1, level(n))
                A.activation(parts[pn][32:64, :], rest[32:64, :], ACT.Copy)
                A.activation(parts[pn][64:MR, :], rest[64:MR, :], ACT.Copy).then_inc(c_sp2, 1)

            def third_part(n, pn):
                act.wait_ge(c_r2, level(n))
                A.activation(parts[pn][64:MR, :], rest[64:MR, :], ACT.Copy).then_inc(c_cut, 1)

            def soma_out(n, pn):
                act.wait_ge(c_som, level(n))
                act.wait_ge(c_pr, level(n - 2))
                for c in range(CT):
                    o = A.activation(soma[pn][:, c, :], bank[:, 2 + c, :], ACT.Gelu, bias=bsoma[:, c:c + 1])
                o.then_inc(c_so, 1)

            def gate_out(q):
                act.wait_ge(c_tem, level(q))
                act.wait_ge(c_pr, level(q - 1))
                for c in range(CT):
                    o = A.activation(gt[:, c, :], bank[:, 4 + c, :], ACT.Tanh, bias=btemp_h[:, c:c + 1], scale=0.5)
                o.then_inc(c_gt, 1)

            def z_out(q):
                act.wait_ge(c_zm, level(q))
                act.wait_ge(c_am, level(q - 1))
                for c in range(CT):
                    o = A.activation(zT[:, c, :], bank[:, c, :], ACT.Identity, bias=bet1[:, c:c + 1],
                                     scale=gam1[:, c:c + 1])
                o.then_inc(c_zT, 1)

            def shared_b_out(q):
                act.wait_ge(c_bm, level(q))
                act.wait_ge(c_hsB, level(q - 1))
                A.activation(sgB[:, :], bank[0:FR, 2, :], ACT.Tanh, scale=0.5).then_inc(c_bt, 1)

            def exponentials(q):
                act.wait_ge(c_neg, level(q))
                act.wait_ge(c_zr, level(q - 1))
                A.activation(ex[:, :, :], neg[:, :, :], ACT.Exp).then_inc(c_ex, 1)

            def shared_out(q):
                act.wait_ge(c_am, level(q))
                A.activation(sgA[:, :], bank[:, 2, :], ACT.Tanh, scale=0.5).then_inc(c_at, 1)

            def step(h, p, load, front, middle, gate, share):
                b = 2 * h + p
                for d in range(D):
                    ahead(mod, b, p, d, front, middle)
                    if d == 0 and front:
                        h1_out(b + 1)
                    if d == 1 and share:
                        exponentials(b - 2)
                        shared_out(b - 2)
                    if d == 1 and gate:
                        gate_out(b - 1)
                    if d == 2 and front:
                        t8_out(b + 1, 1 - p)
                    if d == 3 and front:
                        second_part(b + 1, 1 - p)
                    if d == 4 and front:
                        wg_out(b + 1)
                        third_part(b + 1, 1 - p)
                    if d == 6 and front:
                        soma_out(b + 1, 1 - p)
                    if d == 6 and gate:
                        z_out(b - 1)
                    if d == 7 and load:
                        x1T_out(b + 2)
                    if d == 7 and gate:
                        shared_b_out(b - 1)

            def front_only():
                x1T_out(0)
                h1_out(0)
                t8_out(0, 0)
                second_part(0, 0)
                wg_out(0)
                third_part(0, 0)
                soma_out(0, 0)
                mod(0, 0, 0)
                mod(0, 0, 1)
                x1T_out(1)

            conditioning(act, front_only, step)

            def silu(k, i):
                e = 4 * k + i
                act.wait_ge(e_gu, level(e))
                act.wait_ge(e_h, level(e - 2))
                A.activation(sg1[i % 2][:, 0, :], bank[:, 4 + i % 2, 0:P], ACT.Silu)
                A.activation(sg1[i % 2][0:FR, 1, :], bank[0:FR, 4 + i % 2, P:2 * P], ACT.Silu).then_inc(e_sg, 1)

            def weigh(k, i):
                e = 4 * k + i
                act.wait_ge(e_d, level(e))
                wait_moved(act, e_put[i % 2], 2 * k + i // 2 - 2, 16)
                A.activation(ys[i][:, :], bank[:, 6 + i % 2, 0:H], ACT.Copy, scale=share[i][:, :]).then_inc(e_ys, 1)

            def e_group(k, prepare, first, last):
                for i in range(4):
                    silu(k, i)
                    if i:
                        weigh(k, i - 1)
                    elif not first:
                        weigh(k - 1, 3)

            experts(act, e_group)
            weigh(E1 // 4 - 1, 3)

        @block.vector
        def _(dve):
            V = nc.vector
            dve.wait_ge(consts, 1)
            V.tensor_scalar(rowbase[:, :], rowbase[:, :], -S, None, ALU.bitwise_and)
            dve.drain()
            V.tensor_copy(rowbase_f[:, :], rowbase[:, :])

            def a_front(h, p):
                b = 2 * h + p
                dve.wait_ge(a_ad, level(b))
                V.tensor_tensor(y[p][:, :, :], rows4(3), xt[p][:, :, :], ALU.add).then_inc(a_y, 1)
                dve.drain()
                for j in range(TT):
                    V.bn_stats(stat[:, j, :], y[p][:, j, :])
                dve.drain()
                for j in range(TT):
                    o = V.bn_aggr(mv[p][:, j, :], stat[:, j, :])
                dve.drain().then_inc(a_mv, 1)

            def a_norm(h, p):
                b = 2 * h + p
                dve.wait_ge(a_rstd, level(b))
                dve.wait_ge(a_stored[p], level(h - 1, 16))
                dve.wait_ge(a_nT, level(b - 2))
                for j in range(TT):
                    o = V.tensor_scalar(nrm[p][:, j, :], y[p][:, j, :], mv[p][:, j, 0:1], rstd[p][:, j:j + 1],
                                        ALU.subtract, ALU.mult)
                o.then_inc(a_nrm, 1)

            def a_logits(h, p):
                b = 2 * h + p
                dve.wait_ge(a_lgm, level(b))
                V.tensor_copy(lg0[:, bass.ds(b, 1), :, :].rearrange("p b t e -> p (b t e)"), bank[:, 7, 0:TT * E0]).then_inc(a_lg, 1)

            def a_both(h, p):
                a_norm(*prev(h, p))
                a_front(h, p)
                a_logits(*prev(h, p))

            def a_back(h, p):
                a_norm(h, p)
                a_logits(h, p)

            staggered(dve, a_front, a_both, a_back)

            for first in (True, False):
                src, hi, lo, up, split = ((w1s, w1_hi, w1_lo, b_w1h, b_w1l) if first else
                                          (w2s, w2_hi, w2_lo, b_w2h, b_w2l))
                dve.wait_ge(up, level(3))
                V.tensor_tensor(lo[0][:, :], src[:, :], hi[0][:, :].bitcast(F32), ALU.subtract).then_inc(split, 1)

            lgf = lg0[:, :, :, :].rearrange("p b t e -> p (b t) e")
            rd = red0[:, :].unsqueeze(2).to_broadcast([P, B * TT, E0])
            dve.drain()
            V.tensor_reduce(red0[:, :], lgf, AX.X, ALU.max)
            dve.drain()
            V.tensor_tensor(lgf, lgf, rd, ALU.subtract)
            dve.drain().then_inc(k_sub, 1)
            dve.wait_ge(k_exp, 1)
            V.tensor_reduce(red0[:, :], lgf, AX.X, ALU.add)
            dve.drain()
            V.reciprocal(red0[:, :], red0[:, :])
            dve.drain()
            for j in range(TT):
                V.tensor_tensor(prob[:, j, :].rearrange("p (b e) -> p b e", e=E0), lg0[:, :, j, :],
                                red0[:, :].rearrange("p (b t) -> p b t", t=TT)[:, :, j].unsqueeze(2).to_broadcast([P, B, E0]),
                                ALU.mult)
            dve.drain().then_inc(k_prob, 1)
            dve.wait_ge(k_pT, 1)
            V.tensor_copy(ranks[:, :], bank[0:B * E0, 0, :])
            dve.drain()
            with dve.Fori(0, 1) as _one:
                pass
            for r in range(K0 // 8):
                V.max(gval[:, 8 * r:8 * r + 8], ranks[:, :])
                dve.drain()
                V.max_index(gidx[:, 8 * r:8 * r + 8], gval[:, 8 * r:8 * r + 8], ranks[:, :])
                dve.drain()
                V.match_replace(ranks[:, :], gval[:, 8 * r:8 * r + 8], ranks[:, :], -1.0)
                dve.drain()
            V.tensor_copy(gidx_f[:, :], gidx[:, :])
            dve.drain()
            V.tensor_scalar(gidx_f[:, :], gidx_f[:, :], rowbase_f[0:B * E0, :], None, ALU.add)
            dve.drain().then_inc(k_sel, 1)
            dve.wait_ge(k_idx, 1)
            V.tensor_copy(idxT[:, :, :].rearrange("p b e -> p (b e)"), bank[:, 1, 0:B * E0])
            V.tensor_copy(gateT[:, :, :].rearrange("p b e -> p (b e)"), bank[:, 1, B * E0:2 * B * E0])
            dve.drain().then_inc(k_tab, 1)

            WC = CT * FF0 // 4

            def w_lo(e, q, first, n):
                src, hi, lo, up, split = ((w1s, w1_hi, w1_lo, b_w1h, b_w1l) if first else
                                          (w2s, w2_hi, w2_lo, b_w2h, b_w2l))
                dve.wait_ge(up, level(4 * e + n))
                at = slice(n * WC, (n + 1) * WC)
                o = V.tensor_tensor(lo[q][:, at], src[:, at], hi[q][:, at].bitcast(F32), ALU.subtract)
                if n == 3:
                    o.then_inc(split, 1)

            def b_exT_out(s, p):
                dve.wait_ge(b_T, level(s))
                for j in range(4):
                    for c in range(CT):
                        b = 4 * p + j
                        o = V.tensor_scalar(ex_raw[:, c, j * P:(j + 1) * P], bank[:, c, j * P:(j + 1) * P],
                                            gam0[:, b, c:c + 1], bet0[:, b, c:c + 1], ALU.mult, ALU.add)
                o.then_inc(b_xraw, 1)
                dve.drain()
                dve.wait_ge(b_hm, level(8 * (s - 2) + 7))
                V.tensor_copy(ex_hi[p][:, :, :], ex_raw[:, :, :])
                dve.drain()
                V.tensor_tensor(ex_lo[p][:, :, :], ex_raw[:, :, :], ex_hi[p][:, :, :].bitcast(F32),
                                ALU.subtract).then_inc(b_exT, 1)

            def b_o_out(g, r):
                p, q, e, s = r & 1, r >> 1, 2 * g + (r >> 1), 4 * g + r
                dve.wait_ge(b_o, level(s))
                wait_moved(dve, b_put[p], e - 1, 64)
                V.tensor_tensor(ob[p][:, :, :], rows4(6), b2r[q][:, :].unsqueeze(1).to_broadcast([P, 4, H]),
                                ALU.add).then_inc(b_oa, 1)
                dve.drain()
                V.tensor_tensor(ob[p][:, :, :], ob[p][:, :, :],
                                gateT[:, 4 * p:4 * p + 4, bass.ds(e, 1)].to_broadcast([P, 4, H]),
                                ALU.mult).then_inc(b_out, 1)

            def b_group(g, last):
                for r in range(4):
                    p, q, s = r & 1, r >> 1, 4 * g + r
                    if r or not isinstance(g, int) or g:
                        b_o_out(*((g, r - 1) if r else (g - 1, 3)))
                    for f in range(FT0):
                        dve.wait_ge(b_hi, level(8 * s + f))
                        V.tensor_tensor(h1_lo[:, f, :], h1_raw[f % 4][:, :], h1_hi[:, f, :].bitcast(F32),
                                        ALU.subtract).then_inc(b_lo, 1)
                    if not (last and r == 3):
                        b_exT_out(4 * g + r + 1, (r + 1) & 1)
                    if not (last and q == 1):
                        for n in range(4):
                            w_lo(2 * g + q + 1, 1 - q, p == 0, n)

            b_exT_out(0, 0)
            ffn(dve, b_group)
            b_o_out(E0 // 2 - 1, 3)

            dve.wait_ge(loaded1, 16 * N_LOADED1)
            V.tensor_scalar(bg_h[:, :], bg_h[:, :], 0.5, None, ALU.mult)
            V.tensor_scalar(btemp_h[:, :], btemp_h[:, :], 0.5, None, ALU.mult)
            V.tensor_scalar(bn2_h[:, :], bn2_h[:, :], 0.5, None, ALU.mult)
            V.memset(wn2_3[:, :], 0.0)
            V.tensor_reduce(blend_m[:, :], blend[:, :, :], AX.X, ALU.max)
            dve.drain()
            for part in range(3):
                V.tensor_copy(wn2_3[:, 32 * part:32 * part + D], wn2[:, :])
            V.tensor_tensor(blend[:, :, :], blend[:, :, :], blend_m[:, :].unsqueeze(2).to_broadcast([P, CT, D]), ALU.subtract)
            dve.drain().then_inc(prep1a, 1)
            dve.wait_ge(prep1, 1)
            V.tensor_scalar(alpha[:, :], alpha[:, :], 1.0, None, ALU.add)
            V.tensor_reduce(blend_s[:, :], blend[:, :, :], AX.X, ALU.add)
            dve.drain()
            V.reciprocal(alpha[:, :], alpha[:, :])
            V.reciprocal(blend_s[:, :], blend_s[:, :])
            dve.drain()
            V.tensor_scalar(blend_s[:, :], blend_s[:, :], 0.25, None, ALU.mult)
            dve.drain()
            V.tensor_tensor(blend[:, :, :], blend[:, :, :], blend_s[:, :].unsqueeze(2).to_broadcast([P, CT, D]), ALU.mult)
            dve.drain().then_inc(prep1a, 1)

            def scan_unit(b, p, d):
                dve.wait_ge(c_u, level(D * b + d))
                for c in range(CT):
                    o = V.tensor_tensor_scan(trace[d % 2][:, c, :], alpha[:, d:d + 1].to_broadcast([P, S]),
                                             drive[d % 4][:, c, :], 0.0, ALU.mult, ALU.add)
                o.then_inc(c_scan, 1)

            def sum_unit(b, p, d):
                if d == 0:
                    dve.wait_ge(c_tem, level(b - 2))
                for c in range(CT):
                    if d == 0:
                        o = V.tensor_scalar(acc[p][:, c, :], trace[0][:, c, :], blend[:, c, 0:1], None, ALU.mult)
                    else:
                        o = V.scalar_tensor_tensor(acc[p][:, c, :], trace[d % 2][:, c, :], blend[:, c, d:d + 1],
                                                   acc[p][:, c, :], ALU.mult, ALU.add)
                if d == D - 1:
                    o.then_inc(c_acc, 1)

            def ctx_scan(n):
                dve.wait_ge(c_x1T, level(n))
                dve.wait_ge(c_wgm, level(n - 1))
                for c in range(CT):
                    o = V.tensor_tensor_scan(ctxT[:, c, :], alpha[:, D:D + 1].to_broadcast([P, S]), x1T[:, c, :],
                                             0.0, ALU.mult, ALU.add)
                o.then_inc(c_ctx, 1)

            def gate_in(n, pn):
                dve.wait_ge(c_wgt, level(n))
                dve.wait_ge(c_u, level(D * (n - 2) + D - 1))
                V.scalar_tensor_tensor(gated2[pn][:, :, :], wgt[:, :, :], 1.0, x1T[:, :, :], ALU.add,
                                       ALU.mult).then_inc(c_gat, 1)

            def gate_soma(q, pq):
                dve.wait_ge(c_gt, level(q))
                dve.wait_ge(c_so, level(q))
                dve.wait_ge(c_om, level(q - 1))
                V.scalar_tensor_tensor(prodT[:, :, :], gt[:, :, :], 1.0, soma[pq][:, :, :], ALU.add,
                                       ALU.mult).then_inc(c_pr, 1)

            def stats(q):
                dve.wait_ge(c_om, level(q))
                for j in range(TT):
                    V.bn_stats(stat1[:, j, :], rows4(0)[:, j, :])
                dve.drain()
                for j in range(TT):
                    V.bn_aggr(mv1[:, j, :], stat1[:, j, :])
                dve.drain().then_inc(c_mv, 1)

            def normalise(q):
                dve.wait_ge(c_rs, level(q))
                dve.wait_ge(c_zst, level(q - 1, 16))
                dve.wait_ge(c_zm, level(q - 1))
                for j in range(TT):
                    o = V.tensor_scalar(zrow[:, j, 0:H], rows4(0)[:, j, :], mv1[:, j, 0:1], rstd1[:, j:j + 1],
                                        ALU.subtract, ALU.mult)
                o.then_inc(c_no, 1)

            lgp = bank[:, 0, 0:TT * E1].rearrange("p (t e) -> p t e", e=E1)

            def pick(q):
                dve.wait_ge(c_lgm, level(q))
                settle(dve, tally)
                for j in range(TT):
                    V.max(top8[:, j, :], lgp[:, j, :])
                dve.drain()
                dve.wait_ge(c_ex, level(q - 1))
                V.tensor_tensor(neg[:, :, :], lgp, top8[:, :, 0:1].to_broadcast([P, TT, E1]), ALU.subtract).then_inc(c_neg, 1)
                for j in range(TT):
                    V.match_replace(rep[:, j, :], top8[:, j, :], lgp[:, j, :], -3.0e38)
                dve.drain()
                V.tensor_tensor(mask[:, :, :], rep[:, :, :], lgp, ALU.not_equal).then_inc(c_top, 1)
                dve.drain()
                V.tensor_copy(mask_all[:, :, bass.ds(q * TT, TT)].rearrange("p e t -> p t e"), mask[:, :, :])

            def shared_b(q):
                dve.wait_ge(c_bt, level(q))
                dve.wait_ge(c_dm, level(q - 1))
                V.scalar_tensor_tensor(hsB[:, :], sgB[:, :], 1.0, bank[0:FR, 2, :], ALU.add, ALU.mult)
                dve.drain()
                V.tensor_tensor(hsB[:, :], hsB[:, :], bank[0:FR, 3, :], ALU.mult).then_inc(c_hsB, 1)

            def shared_a(q):
                dve.wait_ge(c_at, level(q))
                V.scalar_tensor_tensor(hsA[:, :], sgA[:, :], 1.0, bank[:, 2, :], ALU.add, ALU.mult)
                dve.drain()
                V.tensor_tensor(hsA[:, :], hsA[:, :], bank[:, 3, :], ALU.mult).then_inc(c_hsA, 1)

            def route_weights(q):
                dve.wait_ge(c_ex, level(q))
                V.tensor_tensor(mask[:, :, :], mask[:, :, :], ex[:, :, :], ALU.mult)
                dve.drain()
                V.tensor_reduce(wsum[:, :], mask[:, :, :], AX.X, ALU.add)
                dve.drain()
                V.reciprocal(wsum[:, :], wsum[:, :])
                dve.drain()
                V.tensor_tensor(zrow[:, :, H:ZW], mask[:, :, :], wsum[:, :].unsqueeze(2).to_broadcast([P, TT, E1]),
                                ALU.mult).then_inc(c_zr, 1)

            def finish(q):
                dve.wait_ge(c_dm, level(q))
                dve.wait_ge(c_xr, level(q, 16))
                dve.wait_ge(c_ost, level(q - 1, 16))
                V.scalar_tensor_tensor(ost[:, :, :], rows4(4), 0.5, xr[:, :, :], ALU.mult, ALU.add).then_inc(c_fin, 1)

            def step(h, p, load, front, middle, gate, share):
                b = 2 * h + p
                for d in range(D):
                    if middle:
                        scan_unit(b, p, d)
                    if d == 0 and gate:
                        sum_unit(b - 1, 1 - p, D - 1)
                    if d and middle:
                        sum_unit(b, p, d - 1)
                    dve.drain()
                    if d == 0 and front:
                        ctx_scan(b + 1)
                    if d == 0 and share:
                        pick(b - 2)
                        shared_b(b - 2)
                    if d == 1 and share:
                        route_weights(b - 2)
                    if d == 2 and gate:
                        gate_soma(b - 1, 1 - p)
                    if d == 2 and share:
                        shared_a(b - 2)
                    if d == 4 and gate:
                        stats(b - 1)
                    if d == 5 and gate:
                        normalise(b - 1)
                    if d == 5 and front:
                        gate_in(b + 1, 1 - p)
                    if d == 5 and share:
                        finish(b - 2)

            def front_only():
                ctx_scan(0)
                gate_in(0, 0)
                dve.drain()

            conditioning(dve, front_only, step)

            dve.drain()

            def prep(k, part):
                if part == 0:
                    dve.wait_ge(e_R, level(k - 1))
                    V.tensor_copy(mstat[:, :, :], mask_all[:, bass.ds(4 * k, 4), :]).then_inc(e_ms, 1)
                elif part == 1:
                    dve.wait_ge(e_R, level(k))
                    dve.wait_ge(e_G, level(k - 1))
                    V.tensor_copy(Rx[:, :, 0:P], bank[0:NT, 1, :].rearrange("p (i s) -> p i s", i=4)).then_inc(e_Rc, 1)
                elif part == 2:
                    dve.wait_ge(e_B, level(k))
                    V.tensor_copy(Bf[:, :], bank[0:NT, 2, 508:512])
                    dve.drain()
                    V.tensor_tensor(Bn[:, :], Bf[:, :], Rx[:, :, P - 1], ALU.add)
                    V.tensor_copy(Rx[:, :, P], Bf[:, :])
                    dve.drain()
                    slot_no = iota_f[0:NT, :].unsqueeze(1).to_broadcast([NT, 4, P])
                    V.tensor_tensor(ge[:, :, :], slot_no, Bf[:, :].unsqueeze(2).to_broadcast([NT, 4, P]), ALU.is_ge)
                    V.tensor_tensor(lt[:, :, :], slot_no, Bn[:, :].unsqueeze(2).to_broadcast([NT, 4, P]), ALU.is_lt)
                    dve.drain()
                    V.tensor_tensor(sel[:, :, :], ge[:, :, :], lt[:, :, :], ALU.mult).then_inc(e_S, 1)
                else:
                    grp = rows4(1)
                    dve.wait_ge(e_G, level(k))
                    V.tensor_copy(meta[:, :, :], grp[:, :, P:P + 3])
                    dve.drain()
                    V.tensor_scalar(cb[:, :], meta[:, :, 0], -1.0, iota_p[:, :], ALU.mult, ALU.add)
                    dve.drain()
                    V.tensor_tensor(cmp[:, :, 0:P - 1], grp[:, :, 0:P - 1], cb[:, :].unsqueeze(2).to_broadcast([P, 4, P - 1]), ALU.is_le)
                    dve.drain()
                    V.tensor_reduce(pos[:, :], cmp[:, :, 0:P - 1], AX.X, ALU.add)
                    dve.drain()
                    V.scalar_tensor_tensor(slot_f[:, :], pos[:, :], dummy_row[:, :], meta[:, :, 1], ALU.subtract, ALU.add)
                    dve.drain()
                    V.tensor_tensor(slot_g[:, :], slot_f[:, :], meta[:, :, 2], ALU.mult)
                    dve.drain()
                    V.tensor_scalar(slots[:, bass.ds(4 * k, 4)], slot_g[:, :], dummy_row[:, :], None, ALU.add).then_inc(e_slot, 1)

            def xgT_out(k, i):
                e = 4 * k + i
                dve.wait_ge(e_T, level(e))
                dve.wait_ge(e_gu, level(e - 2))
                dve.wait_ge(e_ys, level(e - 4))
                V.tensor_copy(share[i][:, :], xg1[i][:, bass.ds(H + e, 1)])
                for c in range(CT):
                    o = V.tensor_scalar(xgT[i % 2][:, c, :], bank[:, 3 * (i % 2), c * P:(c + 1) * P],
                                        gam1[:, c:c + 1], bet1[:, c:c + 1], ALU.mult, ALU.add)
                o.then_inc(e_xT, 1)

            def hidden(k, i):
                e = 4 * k + i
                dve.wait_ge(e_sg, level(e))
                dve.wait_ge(e_d, level(e - 2))
                V.tensor_tensor(he[i % 2][:, 0, :], sg1[i % 2][:, 0, :], bank[:, 4 + i % 2, 2 * P:3 * P], ALU.mult)
                V.tensor_tensor(he[i % 2][0:FR, 1, :], sg1[i % 2][0:FR, 1, :], bank[0:FR, 4 + i % 2, 3 * P:4 * P],
                                ALU.mult).then_inc(e_h, 1)

            def e_group(k, prepare, first, last):
                for i in range(4):
                    if prepare and i == 0:
                        prep(k + 2, 0)
                    if i < 3:
                        xgT_out(k, i + 1)
                    elif not last:
                        xgT_out(k + 1, 0)
                    hidden(k, i)
                    if prepare and i < 3:
                        prep(k + 2, i + 1)

            for k in range(2):
                for part in range(4):
                    prep(k, part)
            xgT_out(0, 0)
            experts(dve, e_group)

        @block.tensor
        def _(pe):
            T = nc.tensor
            pe.wait_ge(consts, 1)
            pe.wait_ge(loaded0, 16 * N_CONST0)

            def a_front(h, p, mid=None):
                b = 2 * h + p
                pe.wait_ge(a_in[p], level(h, 16 * 7))
                pe.wait_ge(a_xT, level(b - 1))
                for c in range(CT):
                    for j in range(TT):
                        o = T.transpose(bank[:, c, j * P:(j + 1) * P], xt[p][:, j, c * P:(c + 1) * P], ident[:, :])
                o.then_inc(a_xTm, 1)
                pe.wait_ge(a_xT, level(b))
                pe.wait_ge(a_h, level(b - 1))
                for c in range(CT):
                    o = T.matmul(bank[0:AD, 2, :], w1c[p][:, c, :], xT[:, c, :], start=(c == 0), stop=(c == CT - 1))
                o.then_inc(a_hm, 1)
                if mid:
                    mid()
                pe.wait_ge(a_h, level(b))
                pe.wait_ge(a_y, level(b - 1))
                for j in range(TT):
                    o = T.matmul(rows4(3)[:, j, :], hT[:, j * P:(j + 1) * P], w2c[p][:, :], start=True, stop=True)
                o.then_inc(a_ad, 1)

            def a_backT(h, p):
                b = 2 * h + p
                pe.wait_ge(a_nrm, level(b))
                pe.wait_ge(a_yT, level(b - 1))
                for c in range(CT):
                    for j in range(TT):
                        o = T.transpose(bank[:, 5 + c, j * P:(j + 1) * P], nrm[p][:, j, c * P:(c + 1) * P], ident[:, :])
                o.then_inc(a_nT, 1)

            def a_logits(h, p):
                b = 2 * h + p
                pe.wait_ge(a_yT, level(b))
                pe.wait_ge(a_lg, level(b - 1))
                for j in range(TT):
                    for c in range(CT):
                        o = T.matmul(bank[:, 7, j * E0:(j + 1) * E0], yT[:, c, j * P:(j + 1) * P], wg0[:, c, :],
                                     start=(c == 0), stop=(c == CT - 1))
                o.then_inc(a_lgm, 1)

            def a_both(h, p):
                a_front(h, p, lambda: a_backT(*prev(h, p)))
                a_logits(*prev(h, p))

            def a_back(h, p):
                a_backT(h, p)
                a_logits(h, p)

            staggered(pe, a_front, a_both, a_back)

            pe.wait_ge(k_prob, 1)
            for j in range(TT):
                o = T.transpose(bank[0:B * E0, 0, j * P:(j + 1) * P], prob[:, j, :], ident[:, :])
            o.then_inc(k_pT, 1)
            pe.wait_ge(k_sel, 1)
            T.transpose(bank[:, 1, 0:B * E0], gidx_f[:, :], ident[0:B * E0, 0:B * E0])
            T.transpose(bank[:, 1, B * E0:2 * B * E0], gval[:, :], ident[0:B * E0, 0:B * E0]).then_inc(k_idx, 1)
            pe.wait_ge(k_tab, 1)

            def b_T_in(s, p, m):
                wait_moved(pe, b_got[p], m, 64)
                pe.wait_ge(b_xraw, level(s - 1))
                for j in range(4):
                    for c in range(CT):
                        o = T.transpose(bank[:, c, j * P:(j + 1) * P], xg0[p][:, j, c * P:(c + 1) * P], ident[:, :])
                o.then_inc(b_T, 1)

            def b_group(g, last):
                for r in range(4):
                    p, q, s, e = r & 1, r >> 1, 4 * g + r, 2 * g + (r >> 1)
                    if p == 0:
                        pe.wait_ge(b_w1l, level(e))
                    pe.wait_ge(b_exT, level(s))
                    for f in range(FT0):
                        pe.wait_ge(b_h, level(8 * s + f - 4))
                        for c in range(CT):
                            at = slice(c * FF0 + f * P, c * FF0 + (f + 1) * P)
                            for n, (w, x) in enumerate(((w1_hi, ex_hi), (w1_hi, ex_lo), (w1_lo, ex_hi))):
                                o = T.matmul(bank[:, 2 + f % 4, :], w[q][:, at], x[p][:, c, :],
                                             start=(c == 0 and n == 0), stop=(c == CT - 1 and n == 2))
                        o.then_inc(b_hm, 1)
                    if not (last and r == 3):
                        b_T_in(s + 1, 1 - p, 2 * g + (r + 1) // 2)
                    pe.wait_ge(b_lo, level(8 * s + 7))
                    if p == 0:
                        pe.wait_ge(b_w2l, level(e))
                    pe.wait_ge(b_oa, level(s - 1))
                    for j in range(4):
                        rows = slice(j * P, (j + 1) * P)
                        for f in range(FT0):
                            for n, (x, w) in enumerate(((h1_hi, w2_hi), (h1_hi, w2_lo), (h1_lo, w2_hi))):
                                o = T.matmul(rows4(6)[:, j, :], x[:, f, rows], w[q][:, f * H:(f + 1) * H],
                                             start=(f == 0 and n == 0), stop=(f == FT0 - 1 and n == 2))
                    o.then_inc(b_o, 1)

            b_T_in(0, 0, 0)
            ffn(pe, b_group)

            pe.wait_ge(prep1a, 2)

            def mod(b, p, d):
                if d == 0:
                    pe.wait_ge(c_cut, level(b))
                pe.wait_ge(c_md, level(D * b + d - 2))
                T.matmul(bank[:, 6 + d % 2, :], spread[:, d, :], parts[p][:, :], start=True, stop=True).then_inc(c_mm, 1)

            def project(o_banks, w, src):
                for n in range(CT):
                    k = len(src)
                    for c in range(k):
                        o = T.matmul(bank[:, o_banks + n, :], w[:, c, n * P:(n + 1) * P], src[c], start=(c == 0),
                                     stop=(c == k - 1))
                return o

            def x1T_in(n, hn, pn):
                pe.wait_ge(c_in[pn], level(hn, 16))
                pe.wait_ge(c_fin, level(n - 4))
                pe.wait_ge(c_t8, level(n - 1))
                pe.wait_ge(c_gt, level(n - 3))
                for c in range(CT):
                    for j in range(TT):
                        o = T.transpose(bank[:, 4 + c, j * P:(j + 1) * P], x1t[pn][:, j, c * P:(c + 1) * P], ident[:, :])
                o.then_inc(c_Tm, 1)

            def h1_in(n):
                pe.wait_ge(c_x1T, level(n))
                for c in range(CT):
                    o = T.matmul(bank[0:HN, 4, :], wn1[:, c, :], x1T[:, c, :], start=(c == 0), stop=(c == CT - 1))
                o.then_inc(c_h1m, 1)

            def temp_in(q, pq, front):
                pe.wait_ge(c_acc, level(q))
                if front:
                    pe.wait_ge(c_h1, level(q + 2))
                pe.wait_ge(c_fin, level(q - 2))
                project(4, wtemp, [acc[pq][:, 0, :], acc[pq][:, 1, :]]).then_inc(c_tem, 1)

            def t8_in(n):
                pe.wait_ge(c_h1, level(n))
                pe.wait_ge(c_gt, level(n - 2))
                T.matmul(bank[0:MR, 4, :], wn2_3[:, :], h1T[:, :], start=True, stop=True).then_inc(c_m8, 1)

            def wg_in(n, half):
                if half == 0:
                    pe.wait_ge(c_ctx, level(n))
                    pe.wait_ge(c_hsA, level(n - 3))
                for c, src in enumerate((x1T[:, 0, :], x1T[:, 1, :], ctxT[:, 0, :], ctxT[:, 1, :])):
                    o = T.matmul(bank[:, 2 + half, :], wg1[:, c, half * P:(half + 1) * P], src, start=(c == 0),
                                 stop=(c == 2 * CT - 1))
                if half == 1:
                    o.then_inc(c_wgm, 1)

            def soma_in(n):
                pe.wait_ge(c_wgt, level(n))
                project(2, wsoma, [x1T[:, 0, :], x1T[:, 1, :]]).then_inc(c_som, 1)

            def out_in(q):
                pe.wait_ge(c_pr, level(q))
                pe.wait_ge(c_top, level(q - 1))
                for j in range(TT):
                    for c in range(CT):
                        o = T.matmul(rows4(0)[:, j, :], prodT[:, c, j * P:(j + 1) * P], wout[:, c, :],
                                     start=(c == 0), stop=(c == CT - 1))
                o.then_inc(c_om, 1)

            def z_in(q):
                pe.wait_ge(c_no, level(q))
                for c in range(CT):
                    for j in range(TT):
                        o = T.transpose(bank[:, c, j * P:(j + 1) * P], zrow[:, j, c * P:(c + 1) * P], ident[:, :])
                o.then_inc(c_zm, 1)

            def logits_in(q):
                pe.wait_ge(c_zT, level(q))
                for j in range(TT):
                    for c in range(CT):
                        o = T.matmul(bank[:, 0, j * E1:(j + 1) * E1], zT[:, c, j * P:(j + 1) * P], router[:, c, :],
                                     start=(c == 0), stop=(c == CT - 1))
                o.then_inc(c_lgm, 1)

            def shared_b_in(q, front):
                if front:
                    pe.wait_ge(c_so, level(q + 2))
                pe.wait_ge(c_hsA, level(q - 1))
                for n, lo in ((0, P), (1, FF1 + P)):
                    for c in range(CT):
                        o = T.matmul(bank[0:FR, 2 + n, :], ws_gu[:, c, lo:lo + FR], zT[:, c, :], start=(c == 0),
                                     stop=(c == CT - 1))
                o.then_inc(c_bm, 1)

            def shared_a_in(q):
                pe.wait_ge(c_hsB, level(q))
                for n, lo in ((0, 0), (1, FF1)):
                    for c in range(CT):
                        o = T.matmul(bank[:, 2 + n, :], ws_gu[:, c, lo:lo + P], zT[:, c, :], start=(c == 0),
                                     stop=(c == CT - 1))
                o.then_inc(c_am, 1)

            def down_in(q, gate, front):
                pe.wait_ge(c_hsA, level(q))
                if gate:
                    pe.wait_ge(c_gt, level(q + 1))
                if front:
                    pe.wait_ge(c_t8, level(q + 3))
                pe.wait_ge(c_fin, level(q - 1))
                for j in range(TT):
                    T.matmul(rows4(4)[:, j, :], hsA[:, j * P:(j + 1) * P], ws_da[:, :], start=True, stop=False)
                    o = T.matmul(rows4(4)[:, j, :], hsB[:, j * P:(j + 1) * P], ws_db[:, :], start=False, stop=True)
                o.then_inc(c_dm, 1)

            def step(h, p, load, front, middle, gate, share):
                b = 2 * h + p
                for d in range(D):
                    ahead(mod, b, p, d, front, middle)
                    if d == 0 and front:
                        h1_in(b + 1)
                    if d == 1 and share:
                        shared_a_in(b - 2)
                    if d == 1 and gate:
                        temp_in(b - 1, 1 - p, front)
                    if d == 2 and front:
                        t8_in(b + 1)
                    if d == 3 and gate:
                        out_in(b - 1)
                    if d == 3 and front:
                        wg_in(b + 1, 0)
                    if d == 4 and front:
                        wg_in(b + 1, 1)
                    if d == 4 and share:
                        down_in(b - 2, gate, front)
                    if d == 6 and front:
                        soma_in(b + 1)
                    if d == 6 and gate:
                        z_in(b - 1)
                    if d == 7 and gate:
                        logits_in(b - 1)
                    if d == 7 and load:
                        x1T_in(b + 2, h + 1, p)
                    if d == 7 and gate:
                        shared_b_in(b - 1, front)

            def front_only():
                x1T_in(0, 0, 0)
                h1_in(0)
                t8_in(0)
                wg_in(0, 0)
                wg_in(0, 1)
                soma_in(0)
                mod(0, 0, 0)
                mod(0, 0, 1)
                x1T_in(1, 0, 1)

            conditioning(pe, front_only, step)

            pe.wait_ge(c_fin, level(B - 1))

            def prep(k, part):
                if part == 0:
                    pe.wait_ge(e_ms, level(k))
                    pe.wait_ge(e_slot, level(k - 1))
                    for i in range(4):
                        o = T.matmul(bank[0:NT, 1, i * P:(i + 1) * P], mstat[:, i, :], tri[:, :], start=True, stop=True)
                    o.then_inc(e_R, 1)
                elif part == 1:
                    pe.wait_ge(e_Rc, level(k))
                    settle(pe, tally)
                    T.matmul(bank[0:NT, 2, 508:512], before[:, :], Rx[:, :, P - 1], start=True, stop=True).then_inc(e_B, 1)
                else:
                    pe.wait_ge(e_S, level(k))
                    for i in range(4):
                        o = T.matmul(rows4(1)[:, i, 0:P + 3], sel[:, i, :], Rx[:, i, :], start=True, stop=True)
                    o.then_inc(e_G, 1)

            def rows_in(k, i):
                e = 4 * k + i
                wait_moved(pe, e_got[i], k, 16)
                pe.wait_ge(e_xT, level(e - 2))
                for c in range(CT):
                    o = T.transpose(bank[:, 3 * (i % 2), c * P:(c + 1) * P], xg1[i][:, c * P:(c + 1) * P], ident[:, :])
                o.then_inc(e_T, 1)

            def gate_up(k, i):
                e = 4 * k + i
                pe.wait_ge(e_w[i], level(k, 64))
                pe.wait_ge(e_xT, level(e))
                pe.wait_ge(e_h, level(e - 2))
                dst = bank[:, 4 + i % 2, :]
                for n, (w, lo, m) in enumerate(((wgr, 0, P), (wgr, P, FR), (wur, 0, P), (wur, P, FR))):
                    for c in range(CT):
                        o = T.matmul(dst[0:m, n * P:(n + 1) * P], w[i][:, c, lo:lo + m], xgT[i % 2][:, c, :],
                                     start=(c == 0), stop=(c == CT - 1))
                o.then_inc(e_gu, 1)

            def down(k, i):
                e = 4 * k + i
                pe.wait_ge(e_h, level(e))
                pe.wait_ge(e_ys, level(e - 2))
                T.matmul(bank[:, 6 + i % 2, 0:H], he[i % 2][:, 0, :], wda[i][:, :], start=True, stop=False)
                T.matmul(bank[:, 6 + i % 2, 0:H], he[i % 2][0:FR, 1, :], wdb[i][:, :], start=False,
                         stop=True).then_inc(e_d, 1)

            def e_group(k, prepare, first, last):
                for i in range(4):
                    gate_up(k, i)
                    if i < 3:
                        rows_in(k, i + 1)
                    elif not last:
                        rows_in(k + 1, 0)
                    if prepare and i < 3:
                        prep(k + 2, i)
                    if i:
                        down(k, i - 1)
                    elif not first:
                        down(k - 1, 3)

            for k in range(2):
                for part in range(3):
                    prep(k, part)
            rows_in(0, 0)
            experts(pe, e_group)
            down(E1 // 4 - 1, 3)


N_LOADED1 = 22

LAYOUT = [
    ("x", "x", ""), ("ids", "itok_B_0_8", ""), ("tau", "condB_tauraws", ""),
    ("cWn2T", "cond_256", "transposed"), ("cbn2", "condB_bn2", ""), ("blendT", "cond_1024", "transposed"),
    ("aW1", "L0_cond_W1", ""), ("ab1", "L0_cond_b1", ""), ("aW2", "L0_cond_W2", ""),
    ("ab2", "L0_cond_b2", ""), ("agam", "L0_cond_gamma", "columns"), ("abet", "L0_cond_beta", "columns"),
    ("fWgT", "L0_ffn_Wg", "transposed"), ("fW1", "L0_ffn_W1", ""), ("fb1", "L0_ffn_b1", "partition first"),
    ("fW2", "L0_ffn_W2", ""), ("fb2", "L0_ffn_b2", ""), ("tau_ctx", "L1_cond_tau_ctx", ""),
    ("cWgT", "L1_cond_Wg", "transposed"), ("cbg", "L1_cond_bg", "columns"), ("cWn1T", "L1_cond_Wn1", "transposed"),
    ("cbn1", "L1_cond_bn1", ""), ("cWsomaT", "L1_cond_Wsoma", "transposed"), ("cbsoma", "L1_cond_bsoma", "columns"),
    ("cWtempT", "L1_cond_Wtemp", "transposed"), ("cbtemp", "L1_cond_btemp", "columns"), ("cWoutT", "L1_cond_Wout", "transposed"),
    ("cgam", "L1_cond_gamma", "columns"), ("cbet", "L1_cond_beta", "columns"), ("routerT", "L1_ffn_router_w", "transposed"),
    ("mwg", "L1_ffn_w_gate", ""), ("mwu", "L1_ffn_w_up", ""), ("mwd", "L1_ffn_w_down", ""),
    ("wsgu", "L1_ffn_ws_gate_up", ""), ("wsd", "L1_ffn_ws_down", ""),
]


def kernel(**inputs):
    import numpy as np
    import concourse.bacc as bacc
    from concourse.bass_utils import run_bass_kernel_spmd

    nc = bacc.Bacc("TRN2", target_bir_lowering=False, num_devices=1)
    arrays, t = {}, {}
    for short, name, layout in LAYOUT:
        a = np.asarray(inputs[name])
        if layout == "transposed":
            a = a.T
        elif layout == "columns":
            a = a.reshape(*a.shape[:-1], -1, P).swapaxes(-1, -2)
        elif layout == "partition first":
            a = a.reshape(a.shape[0], -1, P).transpose(2, 0, 1)
        a = np.ascontiguousarray(a)
        a = a.reshape((1,)) if a.ndim == 0 else a
        a = a.reshape((1, -1)) if short == "ids" else a
        arrays[f"in_{short}"] = a
        t[short] = nc.dram_tensor(f"in_{short}", a.shape, mybir.dt.from_np(a.dtype), kind="ExternalInput").ap()
    t["out"] = nc.dram_tensor("out_0", (TOK + P, H), F32, kind="ExternalOutput").ap()
    build(nc, t)
    r = run_bass_kernel_spmd(nc, [arrays], core_ids=[0])
    return np.asarray(r.results[0]["out_0"])[:TOK].reshape(B, S, H)
```

```python
from contextlib import ExitStack

import concourse.bass as bass
from concourse import mybir

F32 = mybir.dt.float32
F32R = mybir.dt.float32r
BF16 = mybir.dt.bfloat16
I32 = mybir.dt.int32
U32 = mybir.dt.uint32
ALU = mybir.AluOpType
ACT = mybir.ActivationFunctionType
AX = mybir.AxisListType

P = 128
B, S, H = 8, 512, 256
TOK = B * S
CT = H // P
TT = S // P
LANGS, AD = 10, 64
E0, K0, FF0 = 8, 128, 1024
FT0 = FF0 // P
D = 8
MR = 2 * 32 + D
HN = H // 4
E1, TOPK, CAP, FF1 = 64, 8, 128, 192
NT = TOK // P
ZW = H + E1
EPS = 1e-5
CREDIT = 12


def level(m, per=1):
    return (m + 1 + CREDIT) * per


def wait_moved(eng, sem, m, per):
    if not isinstance(m, int) or m >= 0:
        eng.wait_ge(sem, (m + 1) * per)


def settle(eng, tally):
    eng.sem_inc(tally, 1)


def build(nc, t):
    ctx = ExitStack()
    credited = []

    def sb(name, shape, dt=F32):
        return ctx.enter_context(nc.sbuf_tensor(name, shape, dt))

    def sem(name, per=1):
        s = ctx.enter_context(nc.semaphore(name))
        if per:
            credited.append((s, per))
        return s

    out = t["out"]
    x_rows = t["x"].rearrange("b s h -> (b s) h")
    n0_rows = nc.dram_tensor("n0_rows", (TOK, H), F32, kind="Internal").ap()
    x1_rows = nc.dram_tensor("x1_rows", (TOK, H), F32, kind="Internal").ap()
    odd_rows = nc.dram_tensor("odd_rows", (TOK + P, H), F32, kind="Internal").ap()
    z_rows = nc.dram_tensor("z_rows", (TOK + P, ZW), F32, kind="Internal").ap()

    with ctx:
        ident = sb("ident", [P, P])
        flip = sb("flip", [P, P])
        iota_f = sb("iota_f", [P, P])
        iota_p = sb("iota_p", [P, 1])
        dummy_row = sb("dummy_row", [P, 1])
        tri = sb("tri", [P, P], BF16)
        before = sb("before", [NT, NT], BF16)
        mhalf = sb("mhalf", [P, TT])
        rowbase = sb("rowbase", [P, 1], I32)
        rowbase_f = sb("rowbase_f", [P, 1])
        zeros = sb("zeros", [P, TOK // 4 * H // P])
        wg0 = sb("wg0", [P, CT, E0])
        gam0 = sb("gam0", [P, B, CT])
        bet0 = sb("bet0", [P, B, CT])
        b1_0 = sb("b1_0", [P, E0, FT0])
        wg1 = sb("wg1", [P, 2 * CT, H])
        wsoma = sb("wsoma", [P, CT, H])
        wtemp = sb("wtemp", [P, CT, H])
        wout = sb("wout", [P, CT, H])
        wn1 = sb("wn1", [P, CT, HN])
        wn2 = sb("wn2", [HN, D])
        wn2_3 = sb("wn2_3", [HN, MR])
        spread = sb("spread", [MR, D, P], BF16)
        router = sb("router", [P, CT, E1])
        ws_gu = sb("ws_gu", [P, CT, 2 * FF1])
        ws_da = sb("ws_da", [P, H])
        ws_db = sb("ws_db", [P, H])
        bg_h = sb("bg_h", [P, CT])
        btemp_h = sb("btemp_h", [P, CT])
        bsoma = sb("bsoma", [P, CT])
        bn1 = sb("bn1", [HN, 1])
        bn2_h = sb("bn2_h", [MR, 1])
        gam1 = sb("gam1", [P, CT])
        bet1 = sb("bet1", [P, CT])
        tau = sb("tau", [P, D + 1])
        alpha = sb("alpha", [P, D + 1])
        blend = sb("blend", [P, CT, D])
        blend_m = sb("blend_m", [P, CT])
        blend_s = sb("blend_s", [P, CT])
        mask_all = sb("mask_all", [P, E1, NT], BF16)
        Rx = sb("Rx", [NT, 4, P + 3], BF16)

        layer0 = ExitStack()
        outer, ctx_of = ctx, [layer0]

        def sb(name, shape, dt=F32):
            return ctx_of[0].enter_context(nc.sbuf_tensor(name, shape, dt))

        w1s = sb("w1s", [P, CT * FF0])
        w2s = sb("w2s", [P, FT0 * H])
        w1_hi, w1_lo, w2_hi, w2_lo = zip(*(
            [sb(f"{n}{p}", [P, CT * FF0], F32R) for n in ("w1_hi", "w1_lo", "w2_hi", "w2_lo")] for p in range(2)))
        b2r = [sb(f"b2r{p}", [P, H]) for p in range(2)]
        idxT = sb("idxT", [P, B, E0], I32)
        gateT = sb("gateT", [P, B, E0])
        adapter = ExitStack()
        ctx_of[0] = adapter
        xt = [sb(f"xt{p}", [P, TT, H]) for p in range(2)]
        w1c = [sb(f"w1c{p}", [P, CT, AD]) for p in range(2)]
        w2c = [sb(f"w2c{p}", [AD + 1, H]) for p in range(2)]
        b1c = [sb(f"b1c{p}", [AD, 1]) for p in range(2)]
        xT = sb("xT", [P, CT, S])
        hT = sb("hT", [AD + 1, S])
        y = [sb(f"y{p}", [P, TT, H]) for p in range(2)]
        stat = sb("stat", [P, TT, 6])
        mv = [sb(f"mv{p}", [P, TT, 2]) for p in range(2)]
        veps = sb("veps", [P, TT])
        rstd = [sb(f"rstd{p}", [P, TT]) for p in range(2)]
        nrm = [sb(f"nrm{p}", [P, TT, H]) for p in range(2)]
        yT = sb("yT", [P, CT, S])
        lg0 = sb("lg0", [P, B, TT, E0])
        red0 = sb("red0", [P, B * TT])
        prob = sb("prob", [P, TT // 2, 2, B * E0])
        ranks = sb("ranks", [P, S // 2])
        gval = sb("gval", [P, K0])
        gidx = sb("gidx", [P, K0], U32)
        gidx_f = sb("gidx_f", [P, K0])
        lists = sb("lists", [P, 2, 2, B * E0])
        first_wins = sb("first_wins", [P, B * E0])
        idx_f = sb("idx_f", [P, B * E0])
        adapter.close()
        ctx_of[0] = layer0
        take = [sb(f"take{p}", [P, 4], I32) for p in range(2)]
        put = [sb(f"put{p}", [P, 4], I32) for p in range(2)]
        xg0 = [sb(f"xg0_{p}", [P, 4, H]) for p in range(2)]
        ex_raw = sb("ex_raw", [P, CT, S])
        ex_hi = [sb(f"ex_hi{p}", [P, CT, S], F32R) for p in range(2)]
        ex_lo = [sb(f"ex_lo{p}", [P, CT, S], F32R) for p in range(2)]
        h1_raw = [sb(f"h1_raw{p}", [P, S]) for p in range(4)]
        h1_hi = sb("h1_hi", [P, FT0, S], F32R)
        h1_lo = sb("h1_lo", [P, FT0, S], F32R)
        ob = [sb(f"ob{p}", [P, 4, H]) for p in range(2)]
        layer0.close()
        ctx_of[0] = outer
        x1t = [sb(f"x1t{p}", [P, TT, H]) for p in range(2)]
        x1T = sb("x1T", [P, CT, S])
        ctxT = sb("ctxT", [P, CT, S])
        wgt = sb("wgt", [P, CT, S])
        gated2 = [sb(f"gated2_{p}", [P, CT, S]) for p in range(2)]
        h1T = sb("h1T", [HN, S])
        t8 = sb("t8", [MR, S])
        m8 = sb("m8", [MR, S])
        rest = sb("rest", [MR, S])
        parts = [sb(f"parts{p}", [MR, S], BF16) for p in range(2)]
        soma = [sb(f"soma{p}", [P, CT, S]) for p in range(2)]
        md = [sb(f"md{p}", [P, S]) for p in range(2)]
        drive = [sb(f"drive{p}", [P, CT, S]) for p in range(4)]
        trace = [sb(f"trace{p}", [P, CT, S]) for p in range(2)]
        acc = [sb(f"acc{p}", [P, CT, S]) for p in range(2)]
        gt = sb("gt", [P, CT, S])
        prodT = sb("prodT", [P, CT, S])
        stat1 = sb("stat1", [P, TT, 6])
        mv1 = sb("mv_b", [P, TT, 2])
        veps1 = sb("veps1", [P, TT])
        rstd1 = sb("rstd_b", [P, TT])
        zrow = sb("zrow", [P, TT, ZW])
        zT = sb("zT", [P, CT, S])
        top8 = sb("top8", [P, TT, 8])
        rep = sb("rep", [P, TT, E1])
        neg = sb("neg", [P, TT, E1])
        mask = sb("mask", [P, TT, E1])
        ex = sb("ex", [P, TT, E1])
        wsum = sb("wsum", [P, TT])
        sgA = sb("sgA", [P, S])
        sgB = sb("sgB", [FF1 - P, S])
        hsA = sb("hsA", [P, S])
        hsB = sb("hsB", [P, S])
        xr = sb("xr", [P, TT, H])
        ost = sb("ost", [P, TT, H])
        mstat = sb("mstat", [P, 4, NT], BF16)
        Bf = sb("Bf", [NT, 4])
        Bn = sb("Bn", [NT, 4])
        ge = sb("ge", [NT, 4, P], BF16)
        lt = sb("lt", [NT, 4, P], BF16)
        sel = sb("sel", [NT, 4, P], BF16)
        meta = sb("meta", [P, 4, 3])
        cb = sb("cb", [P, 4])
        cmp = sb("cmp", [P, 4, P])
        pos = sb("pos", [P, 4])
        slot_f = sb("slot_f", [P, 4])
        slot_g = sb("slot_g", [P, 4])
        slots = sb("slots", [P, E1], I32)
        gi = [sb(f"gi{q}", [P, 2], I32) for q in range(2)]
        xg1 = [sb(f"xg1_{i}", [P, ZW]) for i in range(4)]
        xgT = [sb(f"xgT{i}", [P, CT, P]) for i in range(4)]
        wex = [sb(f"wex{i}", [P, CT * 2 * FF1 + H]) for i in range(4)]
        wdb = [sb(f"wdb{i}", [P, H]) for i in range(4)]
        sg1 = [sb(f"sg1_{p}", [P, 2, P]) for p in range(2)]
        he = [sb(f"he{p}", [P, 2, P]) for p in range(2)]
        ys = [sb(f"ys{i}", [P, H]) for i in range(4)]
        pi = [sb(f"pi{q}", [P, 2], I32) for q in range(2)]
        share = [sb(f"share{i}", [P, 1]) for i in range(4)]

        bank = ctx.enter_context(nc.psum_tensor("bank", [P, 8, 512], F32))

        def two(n):
            return bank[:, n:n + 2, :]

        def rows4(n):
            return bank[:, n:n + 2, :].rearrange("p k (j c) -> p (k j) c", c=H)

        def prep_bank(k):
            return 6 if isinstance(k, int) and k < 2 else 1

        FR = FF1 - P
        LAST = slice(P - FR, P)
        assert FR == P - FR

        loaded0 = sem("loaded0", 0)
        loaded1 = sem("loaded1", 0)
        x1_set = sem("x1_set", 0)
        z_dummy = sem("z_dummy", 0)
        zeros_set = sem("zeros_set", 0)
        ident_set = sem("ident_set", 0)
        consts = sem("consts", 0)
        tally = sem("tally", 0)
        prep1 = sem("prep1", 0)
        prep1a = sem("prep1a", 0)
        N_CONST0 = 2

        a_in = [sem(f"a_in{p}", 16 * 7) for p in range(2)]
        a_stored = [sem(f"a_stored{p}", 16) for p in range(2)]
        a_xTm, a_xT, a_hm, a_h, a_ad, a_y, a_mv, a_rstd, a_nrm, a_nT, a_yT, a_lgm, a_lg = (
            sem("a_" + n) for n in ("xTm", "xT", "hm", "h", "ad", "y", "mv", "rstd", "nrm", "nT", "yT", "lgm", "lg"))

        k_sub, k_exp, k_prob, k_pT, k_sel, k_idx, k_lists, k_rev, k_tab = (
            sem("k_" + n, 0) for n in ("sub", "exp", "prob", "pT", "sel", "idx", "lists", "rev", "tab"))

        b_w1, b_w2 = sem("b_w1", 16), sem("b_w2", 32)
        b_w1h, b_w1l, b_w2h, b_w2l = sem("b_w1h"), sem("b_w1l"), sem("b_w2h"), sem("b_w2l")
        b_hi, b_lo, b_xraw = sem("b_hi"), sem("b_lo"), sem("b_xraw")
        b_got = [sem(f"b_got{p}", 0) for p in range(2)]
        b_put = [sem(f"b_put{p}", 0) for p in range(2)]
        b_take, b_place, e_gi, e_pi = sem("b_take"), sem("b_place"), sem("e_gi"), sem("e_pi")
        b_T, b_exT, b_hm, b_h, b_o, b_oa, b_out = (
            sem("b_" + n) for n in ("T", "exT", "hm", "h", "o", "oa", "out"))

        c_r1, c_r2, c_sp2 = sem("c_r1"), sem("c_r2"), sem("c_sp2")
        c_m8, c_t8, c_sp, c_cut, c_scan = (sem("c_" + n) for n in ("m8", "t8", "sp", "cut", "scan"))
        c_in = [sem(f"c_in{p}", 16) for p in range(2)]
        c_xr, c_zst, c_ost = sem("c_xr", 16), sem("c_zst", 16), sem("c_ost", 16)
        (c_Tm, c_x1T, c_ctx, c_wgm, c_wgt, c_gat, c_h1m, c_h1, c_som, c_so, c_mm, c_md, c_u, c_acc,
         c_tem, c_gt, c_pr, c_om, c_mv, c_rs, c_no, c_zm, c_zT, c_lgm, c_neg, c_ex, c_top, c_zr,
         c_bm, c_bt, c_hsB, c_am, c_at, c_hsA, c_dm, c_fin) = (
            sem("c_" + n) for n in (
                "Tm", "x1T", "ctx", "wgm", "wgt", "gat", "h1m", "h1", "som", "so", "mm", "md", "u", "acc",
                "tem", "gt", "pr", "om", "mv", "rs", "no", "zm", "zT", "lgm", "neg", "ex", "top", "zr",
                "bm", "bt", "hsB", "am", "at", "hsA", "dm", "fin"))

        e_w = [sem(f"e_w{i}", 32) for i in range(4)]
        e_got = [sem(f"e_got{i}", 0) for i in range(4)]
        e_put = [sem(f"e_put{p}", 0) for p in range(2)]
        e_sum = sem("e_sum", 0)
        (e_ms, e_R, e_Rc, e_B, e_S, e_G, e_slot, e_T, e_xT, e_gu, e_sg, e_h, e_d, e_ys) = (
            sem("e_" + n) for n in ("ms", "R", "Rc", "B", "S", "G", "slot", "T", "xT", "gu", "sg", "h", "d", "ys"))

        block = ctx.enter_context(nc.Block())

        def prev(h, p):
            return (h, 0) if p else (h - 1, 1)

        def nxt(h, p):
            return (h + 1, 0) if p else (h, 1)

        def adapters(eng, first, both, finish):
            first()
            with eng.Fori(0, B // 2 - 1) as i:
                both(i, 1)
                both(i + 1, 0)
            both(B // 2 - 1, 1, True)
            finish()

        def experts(eng, group):
            n = E1 // 4
            group(0, True, True, False)
            with eng.Fori(1, n - 2) as k:
                group(k, True, False, False)
            group(n - 2, False, False, False)
            group(n - 1, False, False, True)

        def ffn(eng, group):
            group(0, False)
            with eng.Fori(1, E0 // 2 - 1) as g:
                group(g, False)
            group(E0 // 2 - 1, True)

        def ahead(work, b, p, d, front, middle):
            if d < D - 2:
                if middle:
                    work(b, p, d + 2)
            elif front:
                work(b + 1, 1 - p, d + 2 - D)

        def conditioning(eng, first, step):
            first()
            step(0, 0, True, True, True, False, False)
            step(0, 1, True, True, True, True, False)
            with eng.Fori(1, B // 2 - 1) as i:
                step(i, 0, True, True, True, True, True)
                step(i, 1, True, True, True, True, True)
            step(B // 2 - 1, 0, False, True, True, True, True)
            step(B // 2 - 1, 1, False, False, True, True, True)
            step(B // 2, 0, False, False, False, True, True)
            step(B // 2, 1, False, False, False, False, True)

        @block.sync
        def _(sp):
            def a_load(h, p):
                b = 2 * h + p
                sp.wait_ge(a_y, level(b - 2))
                settle(sp, tally)
                lang = sp.value_load(t["ids"][0:1, bass.ds(b, 1)], min_val=0, max_val=LANGS - 1)
                sp.dma_start(xt[p][:, :, :], x_rows[bass.ds(b * S, S), :].rearrange("(t p) c -> p t c", p=P)).then_inc(a_in[p], 16)
                sp.dma_start(w1c[p][:, :, :], t["aW1"].rearrange("l (c p) a -> l p c a", p=P)[bass.ds(lang, 1), :, :, :].rearrange("l p c a -> (l p) c a")).then_inc(a_in[p], 16)
                sp.dma_start(w2c[p][0:AD, :], t["aW2"][bass.ds(lang, 1), :, :].rearrange("l a c -> (l a) c")).then_inc(a_in[p], 16)
                sp.dma_start(w2c[p][AD:AD + 1, :], t["ab2"][bass.ds(lang, 1), :]).then_inc(a_in[p], 16)
                sp.dma_start(b1c[p][:, :], t["ab1"][bass.ds(lang, 1), :].rearrange("l a -> a l")).then_inc(a_in[p], 16)
                sp.dma_start(gam0[:, bass.ds(b, 1), :].rearrange("p b c -> p (b c)"), t["agam"][bass.ds(lang, 1), :, :].rearrange("l p c -> (l p) c")).then_inc(a_in[p], 16)
                sp.dma_start(bet0[:, bass.ds(b, 1), :].rearrange("p b c -> p (b c)"), t["abet"][bass.ds(lang, 1), :, :].rearrange("l p c -> (l p) c")).then_inc(a_in[p], 16)

            with sp.Fori(0, B // 2) as i:
                a_load(i, 0)
                a_load(i, 1)

            def b_load(g, last):
                for q in range(2):
                    e = 2 * g + q
                    sp.wait_ge(b_w1l, level(e - 1))
                    sp.dma_start(w1s[:, :].rearrange("p (c f) -> p c f", c=CT), t["fW1"].rearrange("e (c p) f -> e p c f", p=P)[bass.ds(e, 1), :, :, :].rearrange("e p c f -> (e p) c f")).then_inc(b_w1, 16)
                    sp.wait_ge(b_w2l, level(e - 1))
                    sp.wait_ge(b_oa, level(2 * (e - 2) + 1))
                    sp.dma_start(w2s[:, :].rearrange("p (f c) -> p f c", c=H), t["fW2"].rearrange("e (f p) c -> e p f c", p=P)[bass.ds(e, 1), :, :, :].rearrange("e p f c -> (e p) f c")).then_inc(b_w2, 16)
                    sp.dma_start(b2r[q][:, :], t["fb2"][bass.ds(e, 1), :].to_broadcast([P, H])).then_inc(b_w2, 16)

            ffn(sp, b_load)

            wait_moved(sp, b_put[0], E0 - 1, 64)

            def c_load(h, p):
                b = 2 * h + p
                sp.wait_ge(c_Tm, level(b - 2))
                sp.dma_start(x1t[p][:, :, :], x1_rows[bass.ds(b * S, S), :].rearrange("(t p) c -> p t c", p=P)).then_inc(c_in[p], 16)

            def e_load(k):
                for i in range(4):
                    e = 4 * k + i
                    sp.wait_ge(e_d, level(e - 4))
                    sp.dma_start(wex[i][:, :], t["mwp"][bass.ds(e, 1), :, :].rearrange("e p w -> (e p) w")).then_inc(e_w[i], 16)
                    sp.dma_start(wdb[i][LAST, :], t["mwd"][bass.ds(e, 1), :, :].rearrange("e f c -> (e f) c")).then_inc(e_w[i], 16)

            def c_first():
                c_load(0, 0)
                c_load(0, 1)

            def c_step(h, p, load, front, middle, gate, share):
                b = 2 * h + p
                if load:
                    c_load(h + 1, p)
                if isinstance(b, int) and b == 1:
                    wait_moved(sp, b_put[1], E0 - 1, 64)
                if isinstance(b, int) and b == B:
                    e_load(0)
                if share:
                    q = b - 2
                    sp.wait_ge(c_fin, level(q - 1))
                    sp.dma_start(xr[:, :, :], x1_rows[bass.ds(q * S, S), :].rearrange("(t p) c -> p t c", p=P)).then_inc(c_xr, 16)
                    sp.wait_ge(c_zr, level(q))
                    sp.dma_start(z_rows[bass.ds(q * S, S), :].rearrange("(t p) c -> p t c", p=P), zrow[:, :, :]).then_inc(c_zst, 16)
                    sp.wait_ge(c_fin, level(q))
                    sp.dma_start(out[bass.ds(q * S, S), :].rearrange("(t p) c -> p t c", p=P), ost[:, :, :]).then_inc(c_ost, 16)

            conditioning(sp, c_first, c_step)

            with sp.Fori(1, E1 // 4) as k:
                e_load(k)
            sp.wait_ge(e_sum, 16)

        @block.gpsimd
        def _(pool):
            G = nc.gpsimd
            for s, per in credited:
                pool.sem_inc(s, CREDIT * per)
            G.memset(ident[:, :], 0.0)
            pool.drain()
            G.memset(hT[AD:AD + 1, :], 1.0)
            pool.drain()
            G.affine_select(out=ident[:, :], in_=ident[:, :], compare_op=ALU.not_equal, fill=1.0, base=0,
                            pattern=[[-1, P]], channel_multiplier=1)
            pool.drain().then_inc(ident_set, 1)
            G.memset(bn2_h[:, :], 0.0)
            pool.drain()
            G.memset(tri[:, :], 1.0)
            pool.drain()
            G.memset(before[:, :], 1.0)
            pool.drain()
            G.memset(spread[:, :, :], 0.0)
            pool.drain()
            G.memset(mhalf[:, :], -0.5)
            pool.drain()
            G.iota(iota_f[:, :], [[1, P]], base=0, channel_multiplier=0, allow_small_or_imprecise_dtypes=True)
            pool.drain()
            G.iota(iota_p[:, :], [[0, 1]], base=0, channel_multiplier=1, allow_small_or_imprecise_dtypes=True)
            pool.drain()
            G.iota(dummy_row[:, :], [[0, 1]], base=TOK, channel_multiplier=1, allow_small_or_imprecise_dtypes=True)
            pool.drain()
            G.iota(rowbase[:, :], [[0, 1]], base=0, channel_multiplier=S // E0)
            pool.drain()
            G.memset(Rx[:, :, P + 2], 1.0)
            pool.drain()
            G.iota(Rx[:, :, P + 1], [[0, 4]], base=0, channel_multiplier=P, allow_small_or_imprecise_dtypes=True)
            pool.drain()
            G.memset(flip[:, :], 0.0)
            pool.drain()
            G.affine_select(out=flip[:, :], in_=flip[:, :], compare_op=ALU.not_equal, fill=1.0, base=1 - P,
                            pattern=[[1, P]], channel_multiplier=1)
            pool.drain()
            pool.drain()
            G.affine_select(out=tri[:, :], in_=tri[:, :], compare_op=ALU.is_ge, fill=0.0, base=0,
                            pattern=[[1, P]], channel_multiplier=-1)
            pool.drain()
            G.affine_select(out=before[:, :], in_=before[:, :], compare_op=ALU.is_ge, fill=0.0, base=-1,
                            pattern=[[1, NT]], channel_multiplier=-1)
            for part in range(3):
                pool.drain()
                G.affine_select(out=spread[:, :, :], in_=spread[:, :, :], compare_op=ALU.not_equal, fill=1.0,
                                base=-32 * part, pattern=[[-1, D], [0, P]], channel_multiplier=1)
            pool.drain().then_inc(consts, 1)

            def a_pow(h, p):
                b = 2 * h + p
                pool.wait_ge(a_mv, level(b))
                pool.wait_ge(a_nrm, level(b - 2))
                settle(pool, tally)
                G.tensor_scalar(veps[:, :], mv[p][:, :, 1], EPS, None, ALU.add)
                pool.drain()
                G.tensor_tensor(rstd[p][:, :], veps[:, :], mhalf[:, :], ALU.pow).then_inc(a_rstd, 1)
                pool.drain()

            with pool.Fori(0, B // 2) as i:
                a_pow(i, 0)
                a_pow(i, 1)

            pool.wait_ge(k_tab, 1)
            pool.wait_ge(x1_set, 16)
            for p in range(2):
                pool.wait_ge(a_stored[p], level(B // 2 - 1, 16))

            def b_gather(g, r):
                p, e, s = r & 1, 2 * g + (r >> 1), 4 * g + r
                pool.wait_ge(b_T, level(s - 2))
                settle(pool, tally)
                G.tensor_copy(take[p][:, :], idxT[:, 4 * p:4 * p + 4, bass.ds(e, 1)].rearrange("p b e -> p (b e)")).then_inc(b_take, 1)
                pool.wait_ge(b_take, level(s))
                settle(pool, tally)
                for j in range(4):
                    G.indirect_dma_start(xg0[p][:, j, :], None, n0_rows[:, :],
                                         bass.IndirectOffsetOnAxis(ap=take[p][:, j:j + 1], axis=0)).then_inc(b_got[p], 16)

            def b_scatter(g, r):
                p, e, s = r & 1, 2 * g + (r >> 1), 4 * g + r
                pool.wait_ge(b_out, level(s))
                wait_moved(pool, b_put[p], e - 1, 64)
                settle(pool, tally)
                G.tensor_copy(put[p][:, :], idxT[:, 4 * p:4 * p + 4, bass.ds(e, 1)].rearrange("p b e -> p (b e)")).then_inc(b_place, 1)
                pool.wait_ge(b_place, level(s))
                settle(pool, tally)
                for j in range(4):
                    G.indirect_dma_start(x1_rows[:, :], bass.IndirectOffsetOnAxis(ap=put[p][:, j:j + 1], axis=0),
                                         ob[p][:, j, :], None, compute_op=ALU.add).then_inc(b_put[p], 16)

            def rstd_of(q):
                pool.wait_ge(c_mv, level(q))
                pool.wait_ge(c_no, level(q - 1))
                settle(pool, tally)
                G.tensor_scalar(veps1[:, :], mv1[:, :, 1], 4 * EPS, None, ALU.add)
                pool.drain()
                G.tensor_tensor(rstd1[:, :], veps1[:, :], mhalf[:, :], ALU.pow).then_inc(c_rs, 1)

            def first_rest(n, pn):
                pool.wait_ge(c_sp, level(n))
                G.tensor_tensor(rest[:, :], m8[:, :], parts[pn][:, :], ALU.subtract).then_inc(c_r1, 1)

            def second_rest(n, pn):
                pool.wait_ge(c_sp2, level(n))
                settle(pool, tally)
                pool.drain()
                G.tensor_tensor(rest[64:MR, :], rest[64:MR, :], parts[pn][64:MR, :], ALU.subtract).then_inc(c_r2, 1)
                pool.drain()

            def drive_of(b, p, d):
                pool.wait_ge(c_md, level(D * b + d))
                pool.wait_ge(c_gat, level(b))
                pool.wait_ge(c_scan, level(D * b + d - 4))
                G.tensor_tensor(drive[d % 4][:, :, :], gated2[p][:, :, :],
                                md[d % 2][:, :].unsqueeze(1).to_broadcast([P, CT, S]), ALU.mult).then_inc(c_u, 1)

            def b_group(g, last):
                for r in range(4):
                    if r < 2:
                        b_gather(g, r + 2)
                    elif not last:
                        b_gather(g + 1, r - 2)
                    if last and r == 3:
                        first_rest(0, 0)
                        second_rest(0, 0)
                    b_scatter(g, r)

            b_gather(0, 0)
            b_gather(0, 1)
            ffn(pool, b_group)

            def step(h, p, load, front, middle, gate, share):
                b = 2 * h + p
                for d in range(D):
                    ahead(drive_of, b, p, d, front, middle)
                    if d == 2 and front:
                        first_rest(b + 1, 1 - p)
                    if d == 3 and front:
                        second_rest(b + 1, 1 - p)
                    if d == 4 and gate:
                        rstd_of(b - 1)

            def front_only():
                drive_of(0, 0, 0)
                drive_of(0, 0, 1)

            conditioning(pool, front_only, step)

            pool.wait_ge(z_dummy, 16 * 6)
            pool.wait_ge(c_zst, level(B - 1, 16))

            def e_gather(k, i):
                q = i // 2
                pool.wait_ge(e_xT, level(4 * (k - 1) + i + 1 - i % 2))
                if i % 2 == 0:
                    pool.wait_ge(e_slot, level(k))
                    settle(pool, tally)
                    G.tensor_copy(gi[q][:, :], slots[:, bass.ds(4 * k + i, 2)]).then_inc(e_gi, 1)
                    pool.wait_ge(e_gi, level(2 * k + q))
                settle(pool, tally)
                G.indirect_dma_start(xg1[i][:, :], None, z_rows[:, :],
                                     bass.IndirectOffsetOnAxis(ap=gi[q][:, i % 2:i % 2 + 1], axis=0)).then_inc(e_got[i], 16)

            def e_scatter(k, i):
                q = i // 2
                if i % 2 == 0:
                    for p in range(2):
                        wait_moved(pool, e_put[p], 2 * (k - 1) + q, 16)
                    settle(pool, tally)
                    G.tensor_copy(pi[q][:, :], slots[:, bass.ds(4 * k + i, 2)]).then_inc(e_pi, 1)
                    pool.wait_ge(e_pi, level(2 * k + q))
                pool.wait_ge(e_ys, level(4 * k + i))
                wait_moved(pool, e_put[i % 2], 2 * k + q - 1, 16)
                settle(pool, tally)
                G.indirect_dma_start((out, odd_rows)[i % 2][:, :], bass.IndirectOffsetOnAxis(ap=pi[q][:, i % 2:i % 2 + 1], axis=0),
                                     ys[i][:, :], None, compute_op=ALU.add).then_inc(e_put[i % 2], 16)

            def e_group(k, prepare, first, last):
                for i in range(4):
                    if not last:
                        e_gather(k + 1, i)
                    if i > 1:
                        e_scatter(k, i - 2)
                    elif not first:
                        e_scatter(k - 1, i + 2)

            for i in range(4):
                e_gather(0, i)
            pool.wait_ge(c_ost, level(B - 1, 16))
            experts(pool, e_group)
            e_scatter(E1 // 4 - 1, 2)
            e_scatter(E1 // 4 - 1, 3)
            for p in range(2):
                wait_moved(pool, e_put[p], E1 // 2 - 1, 16)
            pool.dma_start(out[0:TOK, :].rearrange("(a r) c -> a (r c)", a=P),
                           odd_rows[0:TOK, :].rearrange("(a r) c -> a (r c)", a=P),
                           accum_op=ALU.add, max_dma_last_dim=8192).then_inc(e_sum, 16)

        @block.scalar
        def _(act):
            A = nc.scalar
            act.dma_start(wg0[:, :, :], t["fWgT"].rearrange("(c p) e -> p c e", p=P)).then_inc(loaded0, 16)
            act.dma_start(b1_0[:, :, :], t["fb1"]).then_inc(loaded0, 16)
            def a_xT_out(h, p):
                b = 2 * h + p
                act.wait_ge(a_xTm, level(b))
                act.wait_ge(a_hm, level(b - 1))
                A.activation(xT[:, :, :], two(0), ACT.Copy).then_inc(a_xT, 1)

            def a_front(h, p):
                b = 2 * h + p
                act.wait_ge(a_hm, level(b))
                act.wait_ge(a_ad, level(b - 1))
                A.activation(hT[0:AD, :], bank[0:AD, 2, :], ACT.Relu, bias=b1c[p][:, :]).then_inc(a_h, 1)

            def a_back(h, p):
                b = 2 * h + p
                act.wait_ge(a_nT, level(b))
                act.wait_ge(a_lgm, level(b - 1))
                settle(act, tally)
                for c in range(CT):
                    o = A.activation(yT[:, c, :], bank[:, 5 + c, :], ACT.Identity,
                                     bias=bet0[:, bass.ds(b, 1), c], scale=gam0[:, bass.ds(b, 1), c])
                o.then_inc(a_yT, 1)

            def a_store(h, p):
                b = 2 * h + p
                act.wait_ge(a_nrm, level(b))
                act.dma_start(n0_rows[bass.ds(b * S, S), :].rearrange("(t p) c -> p t c", p=P), nrm[p][:, :, :]).then_inc(a_stored[p], 16)

            def a_both(h, p, last=False):
                a_front(h, p)
                a_back(*prev(h, p))
                if not last:
                    a_xT_out(*nxt(h, p))
                a_store(*prev(h, p))

            def a_first():
                a_xT_out(0, 0)
                a_front(0, 0)
                a_xT_out(0, 1)

            def a_last():
                a_back(B // 2 - 1, 1)
                a_store(B // 2 - 1, 1)

            adapters(act, a_first, a_both, a_last)

            act.dma_start(x1_rows.rearrange("(a r) c -> a (r c)", a=P), x_rows.rearrange("(a r) c -> a (r c)", a=P)).then_inc(x1_set, 16)
            act.wait_ge(zeros_set, 1)
            act.dma_start(z_rows[TOK:TOK + P, :], zeros[:, 0:ZW]).then_inc(z_dummy, 16)
            for n in range(4):
                rows = odd_rows[n * TOK // 4:(n + 1) * TOK // 4, :]
                act.dma_start(rows.rearrange("(a r) c -> a (r c)", a=P), zeros[:, :]).then_inc(z_dummy, 16)
            act.dma_start(odd_rows[TOK:TOK + P, :], zeros[:, 0:H]).then_inc(z_dummy, 16)
            act.wait_ge(k_sub, 1)
            A.activation(lg0[:, :, :, :], lg0[:, :, :, :], ACT.Exp).then_inc(k_exp, 1)

            n = 0
            for dst, src in (
                    (wg1[:, :, :], t["cWgT"].rearrange("(c p) e -> p c e", p=P)),
                    (wsoma[:, :, :], t["cWsomaT"].rearrange("(c p) e -> p c e", p=P)),
                    (wtemp[:, :, :], t["cWtempT"].rearrange("(c p) e -> p c e", p=P)),
                    (wout[:, :, :], t["cWoutT"].rearrange("(c p) e -> p c e", p=P)),
                    (wn1[:, :, :], t["cWn1T"].rearrange("(c p) e -> p c e", p=P)),
                    (wn2[:, :], t["cWn2T"]),
                    (router[:, :, :], t["routerT"].rearrange("(c p) e -> p c e", p=P)),
                    (ws_gu[:, :, 0:FF1], t["wsgu"][:, 0:FF1].rearrange("(c p) e -> p c e", p=P)),
                    (ws_gu[:, :, FF1:2 * P], t["wsgu"][:, FF1 + P:].rearrange("(c p) e -> p c e", p=P)),
                    (ws_gu[:, :, 2 * P:], t["wsgu"][:, FF1:FF1 + P].rearrange("(c p) e -> p c e", p=P)),
                    (ws_da[:, :], t["wsd"][0:P, :]),
                    (ws_db[LAST, :], t["wsd"][P:FF1, :]),
                    (bg_h[:, :], t["cbg"]),
                    (btemp_h[:, :], t["cbtemp"]),
                    (bsoma[:, :], t["cbsoma"]),
                    (bn1[:, :], t["cbn1"].rearrange("(a o) -> a o", o=1)),
                    (bn2_h[0:D, :], t["cbn2"].rearrange("(d o) -> d o", o=1)),
                    (bn2_h[32:32 + D, :], t["cbn2"].rearrange("(d o) -> d o", o=1)),
                    (bn2_h[64:64 + D, :], t["cbn2"].rearrange("(d o) -> d o", o=1)),
                    (gam1[:, :], t["cgam"]),
                    (bet1[:, :], t["cbet"]),
                    (tau[:, 0:D], t["tau"].rearrange("(o d) -> o d", o=1).to_broadcast([P, D])),
                    (tau[:, D:D + 1], t["tau_ctx"].rearrange("(o d) -> o d", o=1).to_broadcast([P, 1])),
                    (blend[:, :, :], t["blendT"].rearrange("(c p) d -> p c d", p=P))):
                act.dma_start(dst, src).then_inc(loaded1, 16)
                n += 1
            assert n == N_LOADED1

            for first in (True, False):
                src, dst, came, split = ((w1s, w1_hi, b_w1, b_w1h) if first else (w2s, w2_hi, b_w2, b_w2h))
                act.wait_ge(came, level(0, 16 if first else 32))
                for n in range(4):
                    A.activation(dst[0][:, n * 512:(n + 1) * 512], src[:, n * 512:(n + 1) * 512], ACT.Copy).then_inc(split, 1)

            WC = CT * FF0 // 4

            def w_hi(e, q, first, n):
                src, dst, came, split, used = ((w1s, w1_hi, b_w1, b_w1h, b_hm) if first else
                                               (w2s, w2_hi, b_w2, b_w2h, b_o))
                if n == 0:
                    act.wait_ge(came, level(e, 16 if first else 32))
                    act.wait_ge(used, level(8 * (2 * (e - 2) + 1) + 7) if first else level(2 * (e - 2) + 1))
                o = A.activation(dst[q][:, n * WC:(n + 1) * WC], src[:, n * WC:(n + 1) * WC], ACT.Copy)
                o.then_inc(split, 1)

            def b_group(g, last):
                for r in range(4):
                    s, e, p, q = 4 * g + r, 2 * g + (r >> 1), r & 1, r >> 1
                    act.wait_ge(b_o, level(s - 1))
                    for f in range(FT0 + 1):
                        if f < FT0:
                            act.wait_ge(b_hm, level(8 * s + f))
                            act.wait_ge(b_lo, level(8 * s + f - 4))
                            settle(act, tally)
                            A.activation(h1_raw[f % 4][:, :], bank[:, 2 + f % 4, :], ACT.Gelu_apprx_tanh,
                                         bias=b1_0[:, bass.ds(e, 1), f]).then_inc(b_h, 1)
                        if f:
                            act.wait_ge(b_h, level(8 * s + f - 1))
                            A.activation(h1_hi[:, f - 1, :], h1_raw[(f - 1) % 4][:, :], ACT.Copy).then_inc(b_hi, 1)
                    if not (last and q == 1):
                        for n in range(4):
                            w_hi(e + 1, 1 - q, p == 0, n)

            ffn(act, b_group)

            act.wait_ge(prep1a, 1)
            A.activation(alpha[:, :], tau[:, :], ACT.Exp)
            A.activation(blend[:, :, :], blend[:, :, :], ACT.Exp)
            act.drain().then_inc(prep1, 1)

            def mod(b, p, d):
                act.wait_ge(c_mm, level(D * b + d))
                act.wait_ge(c_u, level(D * b + d - 2))
                A.activation(md[d % 2][:, :], bank[:, 6 + d % 2, :], ACT.Copy).then_inc(c_md, 1)

            def x1T_out(n):
                act.wait_ge(c_Tm, level(n))
                act.wait_ge(c_som, level(n - 1))
                act.wait_ge(c_gat, level(n - 1))
                A.activation(x1T[:, :, :], two(4), ACT.Copy).then_inc(c_x1T, 1)

            def wg_out(n):
                act.wait_ge(c_wgm, level(n))
                act.wait_ge(c_gat, level(n - 1))
                for c in range(CT):
                    o = A.activation(wgt[:, c, :], bank[:, 2 + c, :], ACT.Tanh, bias=bg_h[:, c:c + 1], scale=0.5)
                o.then_inc(c_wgt, 1)

            def h1_out(n):
                act.wait_ge(c_h1m, level(n))
                act.wait_ge(c_m8, level(n - 1))
                A.activation(h1T[:, :], bank[0:HN, 4, :], ACT.Gelu, bias=bn1[:, :]).then_inc(c_h1, 1)

            def t8_out(n, pn):
                act.wait_ge(c_m8, level(n))
                act.wait_ge(c_cut, level(n - 1))
                A.activation(t8[:, :], bank[0:MR, 4, :], ACT.Tanh, bias=bn2_h[:, :], scale=0.5).then_inc(c_t8, 1)
                act.drain()
                A.activation(m8[:, :], t8[:, :], ACT.Copy, bias=2.0)
                act.drain()
                act.wait_ge(c_mm, level(D * (n - 2) + D - 1))
                A.activation(parts[pn][:, :], m8[:, :], ACT.Copy).then_inc(c_sp, 1)

            def second_part(n, pn):
                act.wait_ge(c_r1, level(n))
                A.activation(parts[pn][32:64, :], rest[32:64, :], ACT.Copy)
                A.activation(parts[pn][64:MR, :], rest[64:MR, :], ACT.Copy).then_inc(c_sp2, 1)

            def third_part(n, pn):
                act.wait_ge(c_r2, level(n))
                A.activation(parts[pn][64:MR, :], rest[64:MR, :], ACT.Copy).then_inc(c_cut, 1)

            def soma_out(n, pn):
                act.wait_ge(c_som, level(n))
                act.wait_ge(c_pr, level(n - 2))
                for c in range(CT):
                    o = A.activation(soma[pn][:, c, :], bank[:, 2 + c, :], ACT.Gelu, bias=bsoma[:, c:c + 1])
                o.then_inc(c_so, 1)

            def gate_out(q):
                act.wait_ge(c_tem, level(q))
                act.wait_ge(c_pr, level(q - 1))
                for c in range(CT):
                    o = A.activation(gt[:, c, :], bank[:, 4 + c, :], ACT.Tanh, bias=btemp_h[:, c:c + 1], scale=0.5)
                o.then_inc(c_gt, 1)

            def z_out(q):
                act.wait_ge(c_zm, level(q))
                act.wait_ge(c_am, level(q - 1))
                for c in range(CT):
                    o = A.activation(zT[:, c, :], bank[:, c, :], ACT.Identity, bias=bet1[:, c:c + 1],
                                     scale=gam1[:, c:c + 1])
                o.then_inc(c_zT, 1)

            def shared_b_out(q):
                act.wait_ge(c_bm, level(q))
                act.wait_ge(c_hsB, level(q - 1))
                A.activation(sgB[:, :], bank[0:FR, 2, :], ACT.Tanh, scale=0.5).then_inc(c_bt, 1)

            def exponentials(q):
                act.wait_ge(c_neg, level(q))
                act.wait_ge(c_zr, level(q - 1))
                A.activation(ex[:, :, :], neg[:, :, :], ACT.Exp).then_inc(c_ex, 1)

            def shared_out(q):
                act.wait_ge(c_am, level(q))
                A.activation(sgA[:, :], bank[:, 2, :], ACT.Tanh, scale=0.5).then_inc(c_at, 1)

            def step(h, p, load, front, middle, gate, share):
                b = 2 * h + p
                for d in range(D):
                    ahead(mod, b, p, d, front, middle)
                    if d == 0 and front:
                        h1_out(b + 1)
                    if d == 1 and share:
                        exponentials(b - 2)
                        shared_out(b - 2)
                    if d == 1 and gate:
                        gate_out(b - 1)
                    if d == 2 and front:
                        t8_out(b + 1, 1 - p)
                    if d == 3 and front:
                        second_part(b + 1, 1 - p)
                    if d == 4 and front:
                        wg_out(b + 1)
                        third_part(b + 1, 1 - p)
                    if d == 6 and front:
                        soma_out(b + 1, 1 - p)
                    if d == 6 and gate:
                        z_out(b - 1)
                    if d == 7 and load:
                        x1T_out(b + 2)
                    if d == 7 and gate:
                        shared_b_out(b - 1)

            def front_only():
                x1T_out(0)
                h1_out(0)
                t8_out(0, 0)
                second_part(0, 0)
                wg_out(0)
                third_part(0, 0)
                soma_out(0, 0)
                mod(0, 0, 0)
                mod(0, 0, 1)
                x1T_out(1)

            conditioning(act, front_only, step)

            def silu(k, i):
                e = 4 * k + i
                act.wait_ge(e_gu, level(e))
                act.wait_ge(e_h, level(e - 2))
                A.activation(sg1[i % 2][:, 0, :], bank[:, 4 + i % 2, 0:P], ACT.Silu)
                A.activation(sg1[i % 2][LAST, 1, :], bank[0:FR, 4 + i % 2, P:2 * P], ACT.Silu).then_inc(e_sg, 1)

            def weigh(k, i):
                e = 4 * k + i
                act.wait_ge(e_d, level(e))
                wait_moved(act, e_put[i % 2], 2 * k + i // 2 - 2, 16)
                A.activation(ys[i][:, :], bank[:, 6 + i % 2, 0:H], ACT.Copy, scale=share[i][:, :]).then_inc(e_ys, 1)

            def e_group(k, prepare, first, last):
                for i in range(4):
                    silu(k, i)
                    if i:
                        weigh(k, i - 1)
                    elif not first:
                        weigh(k - 1, 3)

            experts(act, e_group)
            weigh(E1 // 4 - 1, 3)

        @block.vector
        def _(dve):
            V = nc.vector
            V.memset(zeros[:, :], 0.0).then_inc(zeros_set, 1)

            def a_front(h, p):
                b = 2 * h + p
                dve.wait_ge(a_ad, level(b))
                V.tensor_tensor(y[p][:, :, :], rows4(3), xt[p][:, :, :], ALU.add).then_inc(a_y, 1)
                dve.drain()
                for j in range(TT):
                    V.bn_stats(stat[:, j, :], y[p][:, j, :])
                dve.drain()
                for j in range(TT):
                    o = V.bn_aggr(mv[p][:, j, :], stat[:, j, :])
                dve.drain().then_inc(a_mv, 1)

            def a_norm(h, p):
                b = 2 * h + p
                dve.wait_ge(a_rstd, level(b))
                dve.wait_ge(a_stored[p], level(h - 1, 16))
                dve.wait_ge(a_nT, level(b - 2))
                for j in range(TT):
                    o = V.tensor_scalar(nrm[p][:, j, :], y[p][:, j, :], mv[p][:, j, 0:1], rstd[p][:, j:j + 1],
                                        ALU.subtract, ALU.mult)
                o.then_inc(a_nrm, 1)

            def a_logits(h, p):
                b = 2 * h + p
                dve.wait_ge(a_lgm, level(b))
                V.tensor_copy(lg0[:, bass.ds(b, 1), :, :].rearrange("p b t e -> p (b t e)"), bank[:, 7, 0:TT * E0]).then_inc(a_lg, 1)

            def a_both(h, p, last=False):
                a_norm(*prev(h, p))
                a_front(h, p)
                a_logits(*prev(h, p))

            def a_last():
                a_norm(B // 2 - 1, 1)
                a_logits(B // 2 - 1, 1)

            adapters(dve, lambda: a_front(0, 0), a_both, a_last)

            dve.wait_ge(consts, 1)
            V.tensor_scalar(rowbase[:, :], rowbase[:, :], -S, None, ALU.bitwise_and)
            dve.drain()
            V.tensor_copy(rowbase_f[:, :], rowbase[:, :])
            dve.drain()
            V.tensor_scalar(rowbase_f[B * E0:P, :], rowbase_f[B * E0:P, :], float(S // 2 - B * S), None, ALU.add)
            lgf = lg0[:, :, :, :].rearrange("p b t e -> p (b t) e")
            rd = red0[:, :].unsqueeze(2).to_broadcast([P, B * TT, E0])
            dve.drain()
            V.tensor_reduce(red0[:, :], lgf, AX.X, ALU.max)
            dve.drain()
            V.tensor_tensor(lgf, lgf, rd, ALU.subtract)
            dve.drain().then_inc(k_sub, 1)
            dve.wait_ge(k_exp, 1)
            V.tensor_reduce(red0[:, :], lgf, AX.X, ALU.add)
            dve.drain()
            V.reciprocal(red0[:, :], red0[:, :])
            dve.drain()
            for j in range(TT):
                V.tensor_tensor(prob[:, j % 2, j // 2, :].rearrange("p (b e) -> p b e", e=E0), lg0[:, :, j, :],
                                red0[:, :].rearrange("p (b t) -> p b t", t=TT)[:, :, j].unsqueeze(2).to_broadcast([P, B, E0]),
                                ALU.mult)
            dve.drain().then_inc(k_prob, 1)
            dve.wait_ge(k_pT, 1)
            V.tensor_copy(ranks[:, :], bank[:, 0, 0:S // 2])
            dve.drain()
            for r in range(K0 // 8):
                V.max(gval[:, 8 * r:8 * r + 8], ranks[:, :])
                dve.drain()
                V.max_index(gidx[:, 8 * r:8 * r + 8], gval[:, 8 * r:8 * r + 8], ranks[:, :])
                V.match_replace(ranks[:, :], gval[:, 8 * r:8 * r + 8], ranks[:, :], -1.0)
                dve.drain()
            V.tensor_copy(gidx_f[:, :], gidx[:, :])
            dve.drain()
            V.tensor_scalar(gidx_f[:, :], gidx_f[:, :], rowbase_f[:, :], None, ALU.add)
            dve.drain().then_inc(k_sel, 1)
            dve.wait_ge(k_idx, 1)
            V.tensor_copy(lists[:, :, :, :].rearrange("p v h n -> p (v h n)"), bank[:, 1, 0:4 * B * E0])
            dve.drain().then_inc(k_lists, 1)
            dve.wait_ge(k_rev, 1)
            val, idx = lists[:, 0, 0, :], lists[:, 1, 0, :]
            val2, idx2 = bank[:, 2, 0:B * E0], bank[:, 2, B * E0:2 * B * E0]
            V.tensor_tensor(first_wins[:, :], val, val2, ALU.is_ge)
            V.tensor_tensor(idx_f[:, :], idx, idx2, ALU.subtract)
            V.tensor_tensor(gateT[:, :, :].rearrange("p b e -> p (b e)"), val, val2, ALU.max)
            dve.drain()
            V.tensor_tensor(idx_f[:, :], idx_f[:, :], first_wins[:, :], ALU.mult)
            dve.drain()
            V.tensor_tensor(idxT[:, :, :].rearrange("p b e -> p (b e)"), idx_f[:, :], idx2, ALU.add)
            dve.drain().then_inc(k_tab, 1)

            for first in (True, False):
                src, hi, lo, up, split = ((w1s, w1_hi, w1_lo, b_w1h, b_w1l) if first else
                                          (w2s, w2_hi, w2_lo, b_w2h, b_w2l))
                dve.wait_ge(up, level(3))
                V.tensor_tensor(lo[0][:, :], src[:, :], hi[0][:, :].bitcast(F32), ALU.subtract).then_inc(split, 1)

            WC = CT * FF0 // 4

            def w_lo(e, q, first, n):
                src, hi, lo, up, split = ((w1s, w1_hi, w1_lo, b_w1h, b_w1l) if first else
                                          (w2s, w2_hi, w2_lo, b_w2h, b_w2l))
                dve.wait_ge(up, level(4 * e + n))
                at = slice(n * WC, (n + 1) * WC)
                o = V.tensor_tensor(lo[q][:, at], src[:, at], hi[q][:, at].bitcast(F32), ALU.subtract)
                if n == 3:
                    o.then_inc(split, 1)

            def b_exT_out(s, p):
                dve.wait_ge(b_T, level(s))
                for j in range(4):
                    for c in range(CT):
                        b = 4 * p + j
                        o = V.tensor_scalar(ex_raw[:, c, j * P:(j + 1) * P], bank[:, c, j * P:(j + 1) * P],
                                            gam0[:, b, c:c + 1], bet0[:, b, c:c + 1], ALU.mult, ALU.add)
                o.then_inc(b_xraw, 1)
                dve.drain()
                dve.wait_ge(b_hm, level(8 * (s - 2) + 7))
                V.tensor_copy(ex_hi[p][:, :, :], ex_raw[:, :, :])
                dve.drain()
                V.tensor_tensor(ex_lo[p][:, :, :], ex_raw[:, :, :], ex_hi[p][:, :, :].bitcast(F32),
                                ALU.subtract).then_inc(b_exT, 1)

            def b_o_out(g, r):
                p, q, e, s = r & 1, r >> 1, 2 * g + (r >> 1), 4 * g + r
                dve.wait_ge(b_o, level(s))
                wait_moved(dve, b_put[p], e - 1, 64)
                V.tensor_tensor(ob[p][:, :, :], rows4(6), b2r[q][:, :].unsqueeze(1).to_broadcast([P, 4, H]),
                                ALU.add).then_inc(b_oa, 1)
                dve.drain()
                V.tensor_tensor(ob[p][:, :, :], ob[p][:, :, :],
                                gateT[:, 4 * p:4 * p + 4, bass.ds(e, 1)].to_broadcast([P, 4, H]),
                                ALU.mult).then_inc(b_out, 1)

            def b_group(g, last):
                for r in range(4):
                    p, q, s = r & 1, r >> 1, 4 * g + r
                    if r or not isinstance(g, int) or g:
                        b_o_out(*((g, r - 1) if r else (g - 1, 3)))
                    for f in range(FT0):
                        dve.wait_ge(b_hi, level(8 * s + f))
                        V.tensor_tensor(h1_lo[:, f, :], h1_raw[f % 4][:, :], h1_hi[:, f, :].bitcast(F32),
                                        ALU.subtract).then_inc(b_lo, 1)
                    if not (last and r == 3):
                        b_exT_out(4 * g + r + 1, (r + 1) & 1)
                    if not (last and q == 1):
                        for n in range(4):
                            w_lo(2 * g + q + 1, 1 - q, p == 0, n)

            b_exT_out(0, 0)
            ffn(dve, b_group)

            dve.wait_ge(loaded1, 16 * N_LOADED1)
            V.tensor_scalar(bg_h[:, :], bg_h[:, :], 0.5, None, ALU.mult)
            V.tensor_scalar(btemp_h[:, :], btemp_h[:, :], 0.5, None, ALU.mult)
            V.tensor_scalar(bn2_h[:, :], bn2_h[:, :], 0.5, None, ALU.mult)
            V.memset(wn2_3[:, :], 0.0)
            V.tensor_reduce(blend_m[:, :], blend[:, :, :], AX.X, ALU.max)
            dve.drain()
            for part in range(3):
                V.tensor_copy(wn2_3[:, 32 * part:32 * part + D], wn2[:, :])
            V.tensor_tensor(blend[:, :, :], blend[:, :, :], blend_m[:, :].unsqueeze(2).to_broadcast([P, CT, D]), ALU.subtract)
            dve.drain().then_inc(prep1a, 1)
            dve.wait_ge(prep1, 1)
            V.tensor_scalar(alpha[:, :], alpha[:, :], 1.0, None, ALU.add)
            V.tensor_reduce(blend_s[:, :], blend[:, :, :], AX.X, ALU.add)
            dve.drain()
            V.reciprocal(alpha[:, :], alpha[:, :])
            V.reciprocal(blend_s[:, :], blend_s[:, :])
            dve.drain()
            V.tensor_scalar(blend_s[:, :], blend_s[:, :], 0.25, None, ALU.mult)
            dve.drain()
            V.tensor_tensor(blend[:, :, :], blend[:, :, :], blend_s[:, :].unsqueeze(2).to_broadcast([P, CT, D]), ALU.mult)
            dve.drain().then_inc(prep1a, 1)

            def scan_unit(b, p, d):
                dve.wait_ge(c_u, level(D * b + d))
                for c in range(CT):
                    o = V.tensor_tensor_scan(trace[d % 2][:, c, :], alpha[:, d:d + 1].to_broadcast([P, S]),
                                             drive[d % 4][:, c, :], 0.0, ALU.mult, ALU.add)
                o.then_inc(c_scan, 1)

            def sum_unit(b, p, d):
                if d == 0:
                    dve.wait_ge(c_tem, level(b - 2))
                for c in range(CT):
                    if d == 0:
                        o = V.tensor_scalar(acc[p][:, c, :], trace[0][:, c, :], blend[:, c, 0:1], None, ALU.mult)
                    else:
                        o = V.scalar_tensor_tensor(acc[p][:, c, :], trace[d % 2][:, c, :], blend[:, c, d:d + 1],
                                                   acc[p][:, c, :], ALU.mult, ALU.add)
                if d == D - 1:
                    o.then_inc(c_acc, 1)

            def ctx_scan(n):
                dve.wait_ge(c_x1T, level(n))
                dve.wait_ge(c_wgm, level(n - 1))
                for c in range(CT):
                    o = V.tensor_tensor_scan(ctxT[:, c, :], alpha[:, D:D + 1].to_broadcast([P, S]), x1T[:, c, :],
                                             0.0, ALU.mult, ALU.add)
                o.then_inc(c_ctx, 1)

            def gate_in(n, pn):
                dve.wait_ge(c_wgt, level(n))
                dve.wait_ge(c_u, level(D * (n - 2) + D - 1))
                V.scalar_tensor_tensor(gated2[pn][:, :, :], wgt[:, :, :], 1.0, x1T[:, :, :], ALU.add,
                                       ALU.mult).then_inc(c_gat, 1)

            def gate_soma(q, pq):
                dve.wait_ge(c_gt, level(q))
                dve.wait_ge(c_so, level(q))
                dve.wait_ge(c_om, level(q - 1))
                V.scalar_tensor_tensor(prodT[:, :, :], gt[:, :, :], 1.0, soma[pq][:, :, :], ALU.add,
                                       ALU.mult).then_inc(c_pr, 1)

            def stats(q):
                dve.wait_ge(c_om, level(q))
                for j in range(TT):
                    V.bn_stats(stat1[:, j, :], rows4(0)[:, j, :])
                dve.drain()
                for j in range(TT):
                    V.bn_aggr(mv1[:, j, :], stat1[:, j, :])
                dve.drain().then_inc(c_mv, 1)

            def normalise(q):
                dve.wait_ge(c_rs, level(q))
                dve.wait_ge(c_zst, level(q - 1, 16))
                dve.wait_ge(c_zm, level(q - 1))
                for j in range(TT):
                    o = V.tensor_scalar(zrow[:, j, 0:H], rows4(0)[:, j, :], mv1[:, j, 0:1], rstd1[:, j:j + 1],
                                        ALU.subtract, ALU.mult)
                o.then_inc(c_no, 1)

            lgp = bank[:, 0, 0:TT * E1].rearrange("p (t e) -> p t e", e=E1)

            def pick(q):
                dve.wait_ge(c_lgm, level(q))
                settle(dve, tally)
                for j in range(TT):
                    V.max(top8[:, j, :], lgp[:, j, :])
                dve.drain()
                dve.wait_ge(c_ex, level(q - 1))
                V.tensor_tensor(neg[:, :, :], lgp, top8[:, :, 0:1].to_broadcast([P, TT, E1]), ALU.subtract).then_inc(c_neg, 1)
                for j in range(TT):
                    V.match_replace(rep[:, j, :], top8[:, j, :], lgp[:, j, :], -3.0e38)
                dve.drain()
                V.tensor_tensor(mask[:, :, :], rep[:, :, :], lgp, ALU.not_equal).then_inc(c_top, 1)
                dve.drain()
                V.tensor_copy(mask_all[:, :, bass.ds(q * TT, TT)].rearrange("p e t -> p t e"), mask[:, :, :])

            def shared_b(q):
                dve.wait_ge(c_bt, level(q))
                dve.wait_ge(c_dm, level(q - 1))
                V.scalar_tensor_tensor(hsB[LAST, :], sgB[:, :], 1.0, bank[0:FR, 2, :], ALU.add, ALU.mult)
                dve.drain()
                V.tensor_tensor(hsB[LAST, :], hsB[LAST, :], bank[LAST, 2, :], ALU.mult).then_inc(c_hsB, 1)

            def shared_a(q):
                dve.wait_ge(c_at, level(q))
                V.scalar_tensor_tensor(hsA[:, :], sgA[:, :], 1.0, bank[:, 2, :], ALU.add, ALU.mult)
                dve.drain()
                V.tensor_tensor(hsA[:, :], hsA[:, :], bank[:, 3, :], ALU.mult).then_inc(c_hsA, 1)

            def route_weights(q):
                dve.wait_ge(c_ex, level(q))
                V.tensor_tensor(mask[:, :, :], mask[:, :, :], ex[:, :, :], ALU.mult)
                dve.drain()
                V.tensor_reduce(wsum[:, :], mask[:, :, :], AX.X, ALU.add)
                dve.drain()
                V.reciprocal(wsum[:, :], wsum[:, :])
                dve.drain()
                V.tensor_tensor(zrow[:, :, H:ZW], mask[:, :, :], wsum[:, :].unsqueeze(2).to_broadcast([P, TT, E1]),
                                ALU.mult).then_inc(c_zr, 1)

            def finish(q):
                dve.wait_ge(c_dm, level(q))
                dve.wait_ge(c_xr, level(q, 16))
                dve.wait_ge(c_ost, level(q - 1, 16))
                V.scalar_tensor_tensor(ost[:, :, :], rows4(4), 0.5, xr[:, :, :], ALU.mult, ALU.add).then_inc(c_fin, 1)

            def prep(k, part):
                if part == 0:
                    dve.wait_ge(e_R, level(k - 1))
                    V.tensor_copy(mstat[:, :, :], mask_all[:, bass.ds(4 * k, 4), :]).then_inc(e_ms, 1)
                elif part == 1:
                    dve.wait_ge(e_R, level(k))
                    dve.wait_ge(e_G, level(k - 1))
                    V.tensor_copy(Rx[:, :, 0:P], bank[0:NT, prep_bank(k), :].rearrange("p (i s) -> p i s", i=4)).then_inc(e_Rc, 1)
                elif part == 2:
                    dve.wait_ge(e_B, level(k))
                    V.tensor_copy(Bf[:, :], bank[0:NT, prep_bank(k) + 1, 508:512])
                    dve.drain()
                    V.tensor_tensor(Bn[:, :], Bf[:, :], Rx[:, :, P - 1], ALU.add)
                    V.tensor_copy(Rx[:, :, P], Bf[:, :])
                    dve.drain()
                    slot_no = iota_f[0:NT, :].unsqueeze(1).to_broadcast([NT, 4, P])
                    V.tensor_tensor(ge[:, :, :], slot_no, Bf[:, :].unsqueeze(2).to_broadcast([NT, 4, P]), ALU.is_ge)
                    V.tensor_tensor(lt[:, :, :], slot_no, Bn[:, :].unsqueeze(2).to_broadcast([NT, 4, P]), ALU.is_lt)
                    dve.drain()
                    V.tensor_tensor(sel[:, :, :], ge[:, :, :], lt[:, :, :], ALU.mult).then_inc(e_S, 1)
                else:
                    grp = rows4(prep_bank(k))
                    dve.wait_ge(e_G, level(k))
                    V.tensor_copy(meta[:, :, :], grp[:, :, P:P + 3])
                    dve.drain()
                    V.tensor_scalar(cb[:, :], meta[:, :, 0], -1.0, iota_p[:, :], ALU.mult, ALU.add)
                    dve.drain()
                    V.tensor_tensor(cmp[:, :, 0:P - 1], grp[:, :, 0:P - 1], cb[:, :].unsqueeze(2).to_broadcast([P, 4, P - 1]), ALU.is_le)
                    dve.drain()
                    V.tensor_reduce(pos[:, :], cmp[:, :, 0:P - 1], AX.X, ALU.add)
                    dve.drain()
                    V.scalar_tensor_tensor(slot_f[:, :], pos[:, :], dummy_row[:, :], meta[:, :, 1], ALU.subtract, ALU.add)
                    dve.drain()
                    V.tensor_tensor(slot_g[:, :], slot_f[:, :], meta[:, :, 2], ALU.mult)
                    dve.drain()
                    V.tensor_scalar(slots[:, bass.ds(4 * k, 4)], slot_g[:, :], dummy_row[:, :], None, ALU.add).then_inc(e_slot, 1)

            def last_share():
                pick(B - 1)
                dve.drain()
                prep(0, 0)
                shared_b(B - 1)
                route_weights(B - 1)
                prep(0, 1)
                dve.drain()
                prep(0, 2)
                shared_a(B - 1)
                prep(0, 3)
                prep(1, 0)
                finish(B - 1)
                prep(1, 1)
                dve.drain()
                prep(1, 2)
                prep(1, 3)
                dve.drain()

            def step(h, p, load, front, middle, gate, share):
                b = 2 * h + p
                if isinstance(b, int) and b == B + 1:
                    dve.drain()
                    last_share()
                    return
                for d in range(D):
                    if middle:
                        scan_unit(b, p, d)
                    if d == 0 and gate:
                        sum_unit(b - 1, 1 - p, D - 1)
                    if d and middle:
                        sum_unit(b, p, d - 1)
                    dve.drain()
                    if d == 0 and front:
                        ctx_scan(b + 1)
                    if d == 0 and share:
                        pick(b - 2)
                        shared_b(b - 2)
                    if d == 1 and share:
                        route_weights(b - 2)
                    if d == 2 and gate:
                        gate_soma(b - 1, 1 - p)
                    if d == 2 and share:
                        shared_a(b - 2)
                    if d == 4 and gate:
                        stats(b - 1)
                    if d == 5 and gate:
                        normalise(b - 1)
                    if d == 5 and front:
                        gate_in(b + 1, 1 - p)
                    if d == 5 and share:
                        finish(b - 2)

            def front_only():
                ctx_scan(0)
                gate_in(0, 0)
                dve.drain()
                b_o_out(E0 // 2 - 1, 3)

            conditioning(dve, front_only, step)

            dve.drain()

            def xgT_out(k, i):
                e = 4 * k + i
                dve.wait_ge(e_T, level(e))
                dve.wait_ge(e_gu, level(e - 4))
                dve.wait_ge(e_ys, level(e - 4))
                V.tensor_copy(share[i][:, :], xg1[i][:, bass.ds(H + e, 1)])
                for c in range(CT):
                    o = V.tensor_scalar(xgT[i][:, c, :], bank[:, 3 * (i % 2), c * P:(c + 1) * P],
                                        gam1[:, c:c + 1], bet1[:, c:c + 1], ALU.mult, ALU.add)
                o.then_inc(e_xT, 1)

            def hidden(k, i):
                e = 4 * k + i
                dve.wait_ge(e_sg, level(e))
                dve.wait_ge(e_d, level(e - 2))
                V.tensor_tensor(he[i % 2][:, 0, :], sg1[i % 2][:, 0, :], bank[:, 4 + i % 2, 2 * P:3 * P], ALU.mult)
                V.tensor_tensor(he[i % 2][LAST, 1, :], sg1[i % 2][LAST, 1, :], bank[LAST, 4 + i % 2, P:2 * P],
                                ALU.mult).then_inc(e_h, 1)

            def e_group(k, prepare, first, last):
                for i in range(4):
                    if prepare and i == 0:
                        prep(k + 2, 0)
                    hidden(k, i)
                    if i < 2:
                        xgT_out(k, i + 2)
                    elif not last:
                        xgT_out(k + 1, i - 2)
                    if prepare and i < 3:
                        prep(k + 2, i + 1)

            xgT_out(0, 0)
            xgT_out(0, 1)
            experts(dve, e_group)

        @block.tensor
        def _(pe):
            T = nc.tensor
            pe.wait_ge(ident_set, 1)
            pe.wait_ge(loaded0, 16 * N_CONST0)

            def a_xT_in(h, p):
                b = 2 * h + p
                pe.wait_ge(a_in[p], level(h, 16 * 7))
                pe.wait_ge(a_xT, level(b - 1))
                for c in range(CT):
                    for j in range(TT):
                        o = T.transpose(bank[:, c, j * P:(j + 1) * P], xt[p][:, j, c * P:(c + 1) * P], ident[:, :])
                o.then_inc(a_xTm, 1)

            def a_hidden(h, p):
                b = 2 * h + p
                pe.wait_ge(a_xT, level(b))
                pe.wait_ge(a_h, level(b - 1))
                for c in range(CT):
                    o = T.matmul(bank[0:AD, 2, :], w1c[p][:, c, :], xT[:, c, :], start=(c == 0), stop=(c == CT - 1))
                o.then_inc(a_hm, 1)

            def a_adapted(h, p):
                b = 2 * h + p
                pe.wait_ge(a_h, level(b))
                pe.wait_ge(a_y, level(b - 1))
                for j in range(TT):
                    o = T.matmul(rows4(3)[:, j, :], hT[:, j * P:(j + 1) * P], w2c[p][:, :], start=True, stop=True)
                o.then_inc(a_ad, 1)

            def a_backT(h, p):
                b = 2 * h + p
                pe.wait_ge(a_nrm, level(b))
                pe.wait_ge(a_yT, level(b - 1))
                for c in range(CT):
                    for j in range(TT):
                        o = T.transpose(bank[:, 5 + c, j * P:(j + 1) * P], nrm[p][:, j, c * P:(c + 1) * P], ident[:, :])
                o.then_inc(a_nT, 1)

            def a_logits(h, p):
                b = 2 * h + p
                pe.wait_ge(a_yT, level(b))
                pe.wait_ge(a_lg, level(b - 1))
                for j in range(TT):
                    for c in range(CT):
                        o = T.matmul(bank[:, 7, j * E0:(j + 1) * E0], yT[:, c, j * P:(j + 1) * P], wg0[:, c, :],
                                     start=(c == 0), stop=(c == CT - 1))
                o.then_inc(a_lgm, 1)

            def a_both(h, p, last=False):
                a_hidden(h, p)
                a_backT(*prev(h, p))
                a_adapted(h, p)
                if not last:
                    a_xT_in(*nxt(h, p))
                a_logits(*prev(h, p))

            def a_first():
                a_xT_in(0, 0)
                a_hidden(0, 0)
                a_adapted(0, 0)
                a_xT_in(0, 1)

            def a_last():
                a_backT(B // 2 - 1, 1)
                a_logits(B // 2 - 1, 1)

            adapters(pe, a_first, a_both, a_last)

            pe.wait_ge(consts, 1)
            pe.wait_ge(k_prob, 1)
            for j in range(TT // 2):
                o = T.transpose(bank[:, 0, j * P:(j + 1) * P], prob[:, j, :, :].rearrange("p h n -> p (h n)"), ident[:, :])
            o.then_inc(k_pT, 1)
            pe.wait_ge(k_sel, 1)
            T.transpose(bank[:, 1, 0:P], gval[:, :], ident[:, :])
            T.transpose(bank[:, 1, P:2 * P], gidx_f[:, :], ident[:, :]).then_inc(k_idx, 1)
            pe.wait_ge(k_lists, 1)
            T.matmul(bank[:, 2, 0:B * E0], flip[:, :], lists[:, 0, 1, :], start=True, stop=True)
            T.matmul(bank[:, 2, B * E0:2 * B * E0], flip[:, :], lists[:, 1, 1, :], start=True, stop=True).then_inc(k_rev, 1)
            pe.wait_ge(k_tab, 1)

            def b_T_in(s, p, m):
                wait_moved(pe, b_got[p], m, 64)
                pe.wait_ge(b_xraw, level(s - 1))
                for j in range(4):
                    for c in range(CT):
                        o = T.transpose(bank[:, c, j * P:(j + 1) * P], xg0[p][:, j, c * P:(c + 1) * P], ident[:, :])
                o.then_inc(b_T, 1)

            def b_group(g, last):
                for r in range(4):
                    p, q, s, e = r & 1, r >> 1, 4 * g + r, 2 * g + (r >> 1)
                    if p == 0:
                        pe.wait_ge(b_w1l, level(e))
                    pe.wait_ge(b_exT, level(s))
                    for f in range(FT0):
                        pe.wait_ge(b_h, level(8 * s + f - 4))
                        for c in range(CT):
                            at = slice(c * FF0 + f * P, c * FF0 + (f + 1) * P)
                            for n, (w, x) in enumerate(((w1_hi, ex_hi), (w1_hi, ex_lo), (w1_lo, ex_hi))):
                                o = T.matmul(bank[:, 2 + f % 4, :], w[q][:, at], x[p][:, c, :],
                                             start=(c == 0 and n == 0), stop=(c == CT - 1 and n == 2))
                        o.then_inc(b_hm, 1)
                    if not (last and r == 3):
                        b_T_in(s + 1, 1 - p, 2 * g + (r + 1) // 2)
                    pe.wait_ge(b_lo, level(8 * s + 7))
                    if p == 0:
                        pe.wait_ge(b_w2l, level(e))
                    pe.wait_ge(b_oa, level(s - 1))
                    for j in range(4):
                        rows = slice(j * P, (j + 1) * P)
                        for f in range(FT0):
                            for n, (x, w) in enumerate(((h1_hi, w2_hi), (h1_hi, w2_lo), (h1_lo, w2_hi))):
                                o = T.matmul(rows4(6)[:, j, :], x[:, f, rows], w[q][:, f * H:(f + 1) * H],
                                             start=(f == 0 and n == 0), stop=(f == FT0 - 1 and n == 2))
                        if j == TT - 1:
                            o.then_inc(b_o, 1)
                        if last and r == 3:
                            row_0(j)

            def mod(b, p, d):
                if d == 0:
                    pe.wait_ge(c_cut, level(b))
                pe.wait_ge(c_md, level(D * b + d - 2))
                T.matmul(bank[:, 6 + d % 2, :], spread[:, d, :], parts[p][:, :], start=True, stop=True).then_inc(c_mm, 1)

            def project(o_banks, w, src):
                for n in range(CT):
                    k = len(src)
                    for c in range(k):
                        o = T.matmul(bank[:, o_banks + n, :], w[:, c, n * P:(n + 1) * P], src[c], start=(c == 0),
                                     stop=(c == k - 1))
                return o

            def x1T_in(n, hn, pn):
                pe.wait_ge(c_in[pn], level(hn, 16))
                pe.wait_ge(c_fin, level(n - 4))
                pe.wait_ge(c_t8, level(n - 1))
                pe.wait_ge(c_gt, level(n - 3))
                for c in range(CT):
                    for j in range(TT):
                        o = T.transpose(bank[:, 4 + c, j * P:(j + 1) * P], x1t[pn][:, j, c * P:(c + 1) * P], ident[:, :])
                o.then_inc(c_Tm, 1)

            def h1_in(n):
                pe.wait_ge(c_x1T, level(n))
                for c in range(CT):
                    o = T.matmul(bank[0:HN, 4, :], wn1[:, c, :], x1T[:, c, :], start=(c == 0), stop=(c == CT - 1))
                o.then_inc(c_h1m, 1)

            def temp_in(q, pq, front):
                pe.wait_ge(c_acc, level(q))
                if front:
                    pe.wait_ge(c_h1, level(q + 2))
                pe.wait_ge(c_fin, level(q - 2))
                project(4, wtemp, [acc[pq][:, 0, :], acc[pq][:, 1, :]]).then_inc(c_tem, 1)

            def t8_in(n):
                pe.wait_ge(c_h1, level(n))
                pe.wait_ge(c_gt, level(n - 2))
                T.matmul(bank[0:MR, 4, :], wn2_3[:, :], h1T[:, :], start=True, stop=True).then_inc(c_m8, 1)

            def wg_in(n, half):
                if half == 0:
                    pe.wait_ge(c_ctx, level(n))
                    pe.wait_ge(c_hsA, level(n - 3))
                for c, src in enumerate((x1T[:, 0, :], x1T[:, 1, :], ctxT[:, 0, :], ctxT[:, 1, :])):
                    o = T.matmul(bank[:, 2 + half, :], wg1[:, c, half * P:(half + 1) * P], src, start=(c == 0),
                                 stop=(c == 2 * CT - 1))
                if half == 1:
                    o.then_inc(c_wgm, 1)

            def soma_in(n):
                pe.wait_ge(c_wgt, level(n))
                project(2, wsoma, [x1T[:, 0, :], x1T[:, 1, :]]).then_inc(c_som, 1)

            def out_in(q):
                pe.wait_ge(c_pr, level(q))
                pe.wait_ge(c_top, level(q - 1))
                for j in range(TT):
                    for c in range(CT):
                        o = T.matmul(rows4(0)[:, j, :], prodT[:, c, j * P:(j + 1) * P], wout[:, c, :],
                                     start=(c == 0), stop=(c == CT - 1))
                o.then_inc(c_om, 1)

            def z_in(q):
                pe.wait_ge(c_no, level(q))
                for c in range(CT):
                    for j in range(TT):
                        o = T.transpose(bank[:, c, j * P:(j + 1) * P], zrow[:, j, c * P:(c + 1) * P], ident[:, :])
                o.then_inc(c_zm, 1)

            def logits_in(q):
                pe.wait_ge(c_zT, level(q))
                for j in range(TT):
                    for c in range(CT):
                        o = T.matmul(bank[:, 0, j * E1:(j + 1) * E1], zT[:, c, j * P:(j + 1) * P], router[:, c, :],
                                     start=(c == 0), stop=(c == CT - 1))
                o.then_inc(c_lgm, 1)

            def shared_b_in(q, front):
                if front:
                    pe.wait_ge(c_so, level(q + 2))
                pe.wait_ge(c_hsA, level(q - 1))
                for c in range(CT):
                    o = T.matmul(bank[:, 2, :], ws_gu[:, c, P:2 * P], zT[:, c, :], start=(c == 0),
                                 stop=(c == CT - 1))
                o.then_inc(c_bm, 1)

            def shared_a_in(q):
                pe.wait_ge(c_hsB, level(q))
                for n, lo in ((0, 0), (1, 2 * P)):
                    for c in range(CT):
                        o = T.matmul(bank[:, 2 + n, :], ws_gu[:, c, lo:lo + P], zT[:, c, :], start=(c == 0),
                                     stop=(c == CT - 1))
                o.then_inc(c_am, 1)

            def down_in(q, gate, front):
                pe.wait_ge(c_hsA, level(q))
                if gate:
                    pe.wait_ge(c_gt, level(q + 1))
                if front:
                    pe.wait_ge(c_t8, level(q + 3))
                pe.wait_ge(c_fin, level(q - 1))
                for j in range(TT):
                    T.matmul(rows4(4)[:, j, :], hsA[:, j * P:(j + 1) * P], ws_da[:, :], start=True, stop=False)
                    o = T.matmul(rows4(4)[:, j, :], hsB[LAST, j * P:(j + 1) * P], ws_db[LAST, :], start=False, stop=True)
                o.then_inc(c_dm, 1)

            def prep(k, part):
                if part == 0:
                    pe.wait_ge(e_ms, level(k))
                    pe.wait_ge(e_slot, level(k - 1))
                    for i in range(4):
                        o = T.matmul(bank[0:NT, prep_bank(k), i * P:(i + 1) * P], mstat[:, i, :], tri[:, :], start=True, stop=True)
                    o.then_inc(e_R, 1)
                elif part == 1:
                    pe.wait_ge(e_Rc, level(k))
                    settle(pe, tally)
                    T.matmul(bank[0:NT, prep_bank(k) + 1, 508:512], before[:, :], Rx[:, :, P - 1], start=True, stop=True).then_inc(e_B, 1)
                else:
                    pe.wait_ge(e_S, level(k))
                    for i in range(4):
                        o = T.matmul(rows4(prep_bank(k))[:, i, 0:P + 3], sel[:, i, :], Rx[:, i, :], start=True, stop=True)
                    o.then_inc(e_G, 1)

            def last_share():
                prep(0, 0)
                shared_a_in(B - 1)
                prep(0, 1)
                prep(0, 2)
                down_in(B - 1, False, False)
                for part in range(3):
                    prep(1, part)

            def step(h, p, load, front, middle, gate, share):
                b = 2 * h + p
                if isinstance(b, int) and b == B + 1:
                    last_share()
                    return
                for d in range(D):
                    ahead(mod, b, p, d, front, middle)
                    if d == 0 and front:
                        h1_in(b + 1)
                    if d == 1 and share:
                        shared_a_in(b - 2)
                    if d == 1 and gate:
                        temp_in(b - 1, 1 - p, front)
                    if d == 2 and front:
                        t8_in(b + 1)
                    if d == 3 and gate:
                        out_in(b - 1)
                    if d == 3 and front:
                        wg_in(b + 1, 0)
                    if d == 4 and front:
                        wg_in(b + 1, 1)
                    if d == 4 and share:
                        down_in(b - 2, gate, front)
                    if d == 6 and front:
                        soma_in(b + 1)
                    if d == 6 and gate:
                        z_in(b - 1)
                    if d == 7 and gate:
                        logits_in(b - 1)
                    if d == 7 and load:
                        x1T_in(b + 2, h + 1, p)
                    if d == 7 and gate:
                        shared_b_in(b - 1, front)

            def row_0(j):
                if j == 0:
                    x1T_in(0, 0, 0)
                elif j == 1:
                    h1_in(0)
                    pe.wait_ge(prep1a, 2)
                elif j == 2:
                    t8_in(0)
                    wg_in(0, 0)
                    wg_in(0, 1)
                else:
                    soma_in(0)

            b_T_in(0, 0, 0)
            ffn(pe, b_group)

            def front_only():
                pe.wait_ge(b_oa, level(2 * E0 - 1))
                mod(0, 0, 0)
                mod(0, 0, 1)
                x1T_in(1, 0, 1)

            conditioning(pe, front_only, step)

            pe.wait_ge(c_fin, level(B - 1))

            def rows_in(k, i):
                e = 4 * k + i
                wait_moved(pe, e_got[i], k, 16)
                pe.wait_ge(e_xT, level(e - 2))
                for c in range(CT):
                    o = T.transpose(bank[:, 3 * (i % 2), c * P:(c + 1) * P], xg1[i][:, c * P:(c + 1) * P], ident[:, :])
                o.then_inc(e_T, 1)

            def gate_up(k, i):
                e = 4 * k + i
                pe.wait_ge(e_w[i], level(k, 32))
                pe.wait_ge(e_xT, level(e))
                pe.wait_ge(e_h, level(e - 2))
                dst = bank[:, 4 + i % 2, :]
                for n in range(3):
                    for c in range(CT):
                        at = c * 2 * FF1 + n * P
                        o = T.matmul(dst[:, n * P:(n + 1) * P], wex[i][:, at:at + P], xgT[i][:, c, :],
                                     start=(c == 0), stop=(c == CT - 1))
                o.then_inc(e_gu, 1)

            def down(k, i):
                e = 4 * k + i
                pe.wait_ge(e_h, level(e))
                pe.wait_ge(e_ys, level(e - 2))
                T.matmul(bank[:, 6 + i % 2, 0:H], he[i % 2][:, 0, :], wex[i][:, CT * 2 * FF1:], start=True, stop=False)
                T.matmul(bank[:, 6 + i % 2, 0:H], he[i % 2][LAST, 1, :], wdb[i][LAST, :], start=False,
                         stop=True).then_inc(e_d, 1)

            def e_group(k, prepare, first, last):
                for i in range(4):
                    gate_up(k, i)
                    if i < 2:
                        rows_in(k, i + 2)
                    elif not last:
                        rows_in(k + 1, i - 2)
                    if i:
                        down(k, i - 1)
                    elif not first:
                        down(k - 1, 3)
                    if prepare and i < 3:
                        prep(k + 2, i)

            rows_in(0, 0)
            rows_in(0, 1)
            experts(pe, e_group)
            down(E1 // 4 - 1, 3)


N_LOADED1 = 24

LAYOUT = [
    ("x", "x", ""), ("ids", "itok_B_0_8", ""), ("tau", "condB_tauraws", ""),
    ("cWn2T", "cond_256", "transposed"), ("cbn2", "condB_bn2", ""), ("blendT", "cond_1024", "transposed"),
    ("aW1", "L0_cond_W1", ""), ("ab1", "L0_cond_b1", ""), ("aW2", "L0_cond_W2", ""),
    ("ab2", "L0_cond_b2", ""), ("agam", "L0_cond_gamma", "columns"), ("abet", "L0_cond_beta", "columns"),
    ("fWgT", "L0_ffn_Wg", "transposed"), ("fW1", "L0_ffn_W1", ""), ("fb1", "L0_ffn_b1", "partition first"),
    ("fW2", "L0_ffn_W2", ""), ("fb2", "L0_ffn_b2", ""), ("tau_ctx", "L1_cond_tau_ctx", ""),
    ("cWgT", "L1_cond_Wg", "transposed"), ("cbg", "L1_cond_bg", "columns"), ("cWn1T", "L1_cond_Wn1", "transposed"),
    ("cbn1", "L1_cond_bn1", ""), ("cWsomaT", "L1_cond_Wsoma", "transposed"), ("cbsoma", "L1_cond_bsoma", "columns"),
    ("cWtempT", "L1_cond_Wtemp", "transposed"), ("cbtemp", "L1_cond_btemp", "columns"), ("cWoutT", "L1_cond_Wout", "transposed"),
    ("cgam", "L1_cond_gamma", "columns"), ("cbet", "L1_cond_beta", "columns"), ("routerT", "L1_ffn_router_w", "transposed"),
    ("mwp", "L1_ffn_w_*", "packed"), ("mwd", "L1_ffn_w_down", "packed"),
    ("wsgu", "L1_ffn_ws_gate_up", ""), ("wsd", "L1_ffn_ws_down", ""),
]


def kernel(**inputs):
    import numpy as np
    import concourse.bacc as bacc
    from concourse.bass_utils import run_bass_kernel_spmd

    nc = bacc.Bacc("TRN2", target_bir_lowering=False, num_devices=1)
    arrays, t = {}, {}
    gate, up = (np.asarray(inputs[name]).reshape(E1, CT, P, FF1).swapaxes(1, 2) for name in ("L1_ffn_w_gate", "L1_ffn_w_up"))
    wdown = np.asarray(inputs["L1_ffn_w_down"])
    up = np.concatenate([up[..., P:], up[..., :P]], axis=-1)
    both = np.concatenate([gate, up], axis=-1).reshape(E1, P, CT * 2 * FF1)
    packed = {"mwp": np.concatenate([both, wdown[:, :P]], axis=-1), "mwd": wdown[:, P:]}

    for short, name, layout in LAYOUT:
        a = packed[short] if layout == "packed" else np.asarray(inputs[name])
        if layout == "transposed":
            a = a.T
        elif layout == "columns":
            a = a.reshape(*a.shape[:-1], -1, P).swapaxes(-1, -2)
        elif layout == "partition first":
            a = a.reshape(a.shape[0], -1, P).transpose(2, 0, 1)
        a = np.ascontiguousarray(a)
        a = a.reshape((1,)) if a.ndim == 0 else a
        a = a.reshape((1, -1)) if short == "ids" else a
        arrays[f"in_{short}"] = a
        t[short] = nc.dram_tensor(f"in_{short}", a.shape, mybir.dt.from_np(a.dtype), kind="ExternalInput").ap()
    t["out"] = nc.dram_tensor("out_0", (TOK + P, H), F32, kind="ExternalOutput").ap()
    build(nc, t)
    r = run_bass_kernel_spmd(nc, [arrays], core_ids=[0])
    return np.asarray(r.results[0]["out_0"])[:TOK].reshape(B, S, H)
```
